# Optimizing a Trainium2 kernel written in Bass

```python
import numpy as np
import jax
import jax.numpy as jnp

def _softmax(x, axis=-1):
    return jax.nn.softmax(x, axis=axis)

def _gelu(x):
    return jax.nn.gelu(x, approximate=True)

def _silu(x):
    return jax.nn.silu(x)

def _sigmoid(x):
    return jax.nn.sigmoid(x)

def _layernorm(x, axis=-1, eps=1e-05):
    m = jnp.mean(x, axis=axis, keepdims=True)
    v = jnp.var(x, axis=axis, keepdims=True)
    return (x - m) / jnp.sqrt(v + eps)

def _scatter_add(tgt, idx, src, axis=0):
    return tgt.at[idx].add(src)

def _segment_sum(src, seg, n):
    return jax.ops.segment_sum(src, seg, n)
kernel_name = 'mk_conv_seq_d4_conv_nchw512_r2_6983b7'

def setup_inputs(seed: int=0):
    np.random.seed(seed)
    _w = jnp.asarray

    def _rec_inputs():
        import jax
        import jax.numpy as jnp
        _gk = jax.random.key(seed)
        x = -0.0002928 + 1 * jax.random.normal(jax.random.fold_in(_gk, 1), (8, 256, 32, 32), jnp.float32)
        return x
    x = _rec_inputs()

    def _L0_conv_setup():
        import jax, jax.numpy as jnp
        import numpy as np
        NUM_HEADS = 8
        HEAD_DIM = 32
        SCALE = HEAD_DIM ** (-0.5)
        key = jax.random.key(seed)
        k_x, k_wp, k_bp, k_wo, k_bo = jax.random.split(key, 5)
        C = 256
        inner = NUM_HEADS * HEAD_DIM
        return {'x': jax.random.normal(k_x, (8, C, 32, 32), dtype=jnp.float32), 'w_proj': jax.random.normal(k_wp, (C, 3 * inner), dtype=jnp.float32) * C ** (-0.5), 'b_proj': jax.random.normal(k_bp, (3 * inner,), dtype=jnp.float32) * 0.02, 'w_out': jax.random.normal(k_wo, (inner, C), dtype=jnp.float32) * inner ** (-0.5), 'b_out': jax.random.normal(k_bo, (C,), dtype=jnp.float32) * 0.02}
    _L0_conv_all = _L0_conv_setup()
    _L0_conv_in = {k: v for k, v in _L0_conv_all.items() if k in ('w_proj', 'b_proj', 'w_out', 'b_out')}
    del _L0_conv_all

    def _L1_conv_setup():
        import jax, jax.numpy as jnp
        import numpy as np
        B, C, H, W = (2, 256, 32, 32)
        G = 32
        EPS = 1e-06
        key = jax.random.key(seed)
        ks = jax.random.split(key, 10)
        s = 1.0 / np.sqrt(C)
        return {'x': jax.random.normal(ks[0], (B, C, H, W), dtype=jnp.float32), 'gn_w': jnp.ones((C,), jnp.float32), 'gn_b': jnp.zeros((C,), jnp.float32), 'wq': jax.random.normal(ks[1], (C, C), jnp.float32) * s, 'bq': jnp.zeros((C,), jnp.float32), 'wk': jax.random.normal(ks[2], (C, C), jnp.float32) * s, 'bk': jnp.zeros((C,), jnp.float32), 'wv': jax.random.normal(ks[3], (C, C), jnp.float32) * s, 'bv': jnp.zeros((C,), jnp.float32), 'wo': jax.random.normal(ks[4], (C, C), jnp.float32) * s, 'bo': jnp.zeros((C,), jnp.float32)}
    _L1_conv_all = _L1_conv_setup()
    _L1_conv_in = {k: v for k, v in _L1_conv_all.items() if k in ('gn_w', 'gn_b', 'wq', 'bq', 'wk', 'bk', 'wv', 'bv', 'wo', 'bo')}
    del _L1_conv_all

    def _L2_conv_setup():
        import jax, jax.numpy as jnp
        import numpy as np
        EPS = 1e-05

        def mean_std_norm(x):
            mean = jnp.mean(x, axis=(2, 3), keepdims=True)
            var = jnp.var(x, axis=(2, 3), keepdims=True)
            return (x - mean) / jnp.sqrt(var + EPS)

        def conv1x1(x, w, b):
            return jnp.einsum('oc,bchw->bohw', w, x) + b[None, :, None, None]
        key = jax.random.key(seed)
        ks = jax.random.split(key, 9)
        C = 256
        s = 1.0 / np.sqrt(C)
        inp = {'content_feat': jax.random.normal(ks[0], (4, C, 32, 32), dtype=jnp.float32), 'f_w': jax.random.normal(ks[1], (C, C), dtype=jnp.float32) * s, 'f_b': jnp.zeros((C,), dtype=jnp.float32), 'g_w': jax.random.normal(ks[2], (C, C), dtype=jnp.float32) * s, 'g_b': jnp.zeros((C,), dtype=jnp.float32), 'h_w': jax.random.normal(ks[3], (C, C), dtype=jnp.float32) * s, 'h_b': jnp.zeros((C,), dtype=jnp.float32), 'o_w': jax.random.normal(ks[4], (C, C), dtype=jnp.float32) * s, 'o_b': jnp.zeros((C,), dtype=jnp.float32)}
        return inp
    _L2_conv_all = _L2_conv_setup()
    _L2_conv_in = {k: v for k, v in _L2_conv_all.items() if k in ('f_w', 'f_b', 'g_w', 'g_b', 'h_w', 'h_b', 'o_w', 'o_b')}
    del _L2_conv_all

    def _L3_conv_setup():
        import jax, jax.numpy as jnp
        import numpy as np
        N_HEAD, N_MIX, D_MODEL, D_K, D_V = (8, 2, 256, 32, 32)
        BN_EPS = 1e-05

        def avg_pool_3s2p1(x):
            dims, strides = ((1, 1, 3, 3), (1, 1, 2, 2))
            pad = [(0, 0), (0, 0), (1, 1), (1, 1)]
            s = jax.lax.reduce_window(x, 0.0, jax.lax.add, dims, strides, pad)
            cnt = jax.lax.reduce_window(jnp.ones_like(x), 0.0, jax.lax.add, dims, strides, pad)
            return s / cnt

        def conv1x1(x, w, b=None):
            y = jnp.einsum('bchw,oc->bohw', x, w)
            if b is not None:
                y = y + b.reshape(1, -1, 1, 1)
            return y
        key = jax.random.key(seed)
        ks = jax.random.split(key, 6)
        B, H, W = (4, 40, 40)
        x = jax.random.normal(ks[0], (B, D_MODEL, H, W), dtype=jnp.float32)
        sd_qk = np.sqrt(2.0 / (D_MODEL + D_K))
        w_qk = jax.random.normal(ks[1], (N_HEAD * D_K, D_MODEL), dtype=jnp.float32) * sd_qk
        b_qk = jnp.zeros((N_HEAD * D_K,), dtype=jnp.float32)
        sd_v = np.sqrt(2.0 / (D_MODEL + D_V))
        w_v = jax.random.normal(ks[2], (N_HEAD * D_V, D_MODEL), dtype=jnp.float32) * sd_v
        b_v = jnp.zeros((N_HEAD * D_V,), dtype=jnp.float32)
        std = np.power(N_MIX, -0.5)
        mix_weight = jax.random.uniform(ks[3], (N_MIX, D_K), dtype=jnp.float32, minval=-std, maxval=std)
        w_out = jax.random.normal(ks[4], (D_MODEL, N_HEAD * D_V), dtype=jnp.float32) * 0.02
        bn_weight = jnp.ones((D_MODEL,), dtype=jnp.float32)
        bn_bias = jnp.zeros((D_MODEL,), dtype=jnp.float32)
        return {'x': x, 'w_qk': w_qk, 'b_qk': b_qk, 'w_v': w_v, 'b_v': b_v, 'mix_weight': mix_weight, 'w_out': w_out, 'bn_weight': bn_weight, 'bn_bias': bn_bias}
    _L3_conv_all = _L3_conv_setup()
    _L3_conv_in = {k: v for k, v in _L3_conv_all.items() if k in ('w_qk', 'b_qk', 'w_v', 'b_v', 'mix_weight', 'w_out', 'bn_weight', 'bn_bias')}
    del _L3_conv_all
    return {'x': x, 'L0_conv_w_proj': _L0_conv_in['w_proj'], 'L0_conv_b_proj': _L0_conv_in['b_proj'], 'L0_conv_w_out': _L0_conv_in['w_out'], 'L0_conv_b_out': _L0_conv_in['b_out'], 'L1_conv_gn_w': _L1_conv_in['gn_w'], 'L1_conv_gn_b': _L1_conv_in['gn_b'], 'L1_conv_wq': _L1_conv_in['wq'], 'L1_conv_bq': _L1_conv_in['bq'], 'L1_conv_wk': _L1_conv_in['wk'], 'L1_conv_bk': _L1_conv_in['bk'], 'L1_conv_wv': _L1_conv_in['wv'], 'L1_conv_bv': _L1_conv_in['bv'], 'L1_conv_wo': _L1_conv_in['wo'], 'L1_conv_bo': _L1_conv_in['bo'], 'L2_conv_f_w': _L2_conv_in['f_w'], 'L2_conv_f_b': _L2_conv_in['f_b'], 'L2_conv_g_w': _L2_conv_in['g_w'], 'L2_conv_g_b': _L2_conv_in['g_b'], 'L2_conv_h_w': _L2_conv_in['h_w'], 'L2_conv_h_b': _L2_conv_in['h_b'], 'L2_conv_o_w': _L2_conv_in['o_w'], 'L2_conv_o_b': _L2_conv_in['o_b'], 'L3_conv_w_qk': _L3_conv_in['w_qk'], 'L3_conv_b_qk': _L3_conv_in['b_qk'], 'L3_conv_w_v': _L3_conv_in['w_v'], 'L3_conv_b_v': _L3_conv_in['b_v'], 'L3_conv_mix_weight': _L3_conv_in['mix_weight'], 'L3_conv_w_out': _L3_conv_in['w_out'], 'L3_conv_bn_weight': _L3_conv_in['bn_weight'], 'L3_conv_bn_bias': _L3_conv_in['bn_bias']}

def reference(x, L0_conv_w_proj, L0_conv_b_proj, L0_conv_w_out, L0_conv_b_out, L1_conv_gn_w, L1_conv_gn_b, L1_conv_wq, L1_conv_bq, L1_conv_wk, L1_conv_bk, L1_conv_wv, L1_conv_bv, L1_conv_wo, L1_conv_bo, L2_conv_f_w, L2_conv_f_b, L2_conv_g_w, L2_conv_g_b, L2_conv_h_w, L2_conv_h_b, L2_conv_o_w, L2_conv_o_b, L3_conv_w_qk, L3_conv_b_qk, L3_conv_w_v, L3_conv_b_v, L3_conv_mix_weight, L3_conv_w_out, L3_conv_bn_weight, L3_conv_bn_bias):
    import jax
    import jax.numpy as jnp

    def _L0_conv_ref(x, w_proj, b_proj, w_out, b_out):
        import jax, jax.numpy as jnp
        import numpy as np
        NUM_HEADS = 8
        HEAD_DIM = 32
        SCALE = HEAD_DIM ** (-0.5)
        B, C, H, W = x.shape
        N = H * W
        tokens = x.reshape(B, C, N).transpose(0, 2, 1)
        qkv = (tokens @ w_proj + b_proj).reshape(B, N, NUM_HEADS, 3 * HEAD_DIM)
        q, k, v = jnp.split(qkv, 3, axis=-1)
        attn = jnp.einsum('bihd,bjhd->bijh', q, k) * SCALE
        attn = jax.nn.softmax(attn, axis=2)
        res = jnp.einsum('bijh,bjhd->bihd', attn, v).reshape(B, N, NUM_HEADS * HEAD_DIM)
        out = res @ w_out + b_out + tokens
        return out.transpose(0, 2, 1).reshape(B, C, H, W)

    def _L1_conv_ref(x, gn_w, gn_b, wq, bq, wk, bk, wv, bv, wo, bo):
        import jax, jax.numpy as jnp
        import numpy as np
        B, C, H, W = (2, 256, 32, 32)
        G = 32
        EPS = 1e-06
        b, c, h, w = x.shape
        n = h * w
        xg = x.reshape(b, G, c // G, h, w)
        mu = xg.mean(axis=(2, 3, 4), keepdims=True)
        var = ((xg - mu) ** 2).mean(axis=(2, 3, 4), keepdims=True)
        hn = ((xg - mu) * jax.lax.rsqrt(var + EPS)).reshape(b, c, h, w)
        hn = hn * gn_w[None, :, None, None] + gn_b[None, :, None, None]
        hf = hn.reshape(b, c, n)
        q = jnp.einsum('oc,bcn->bno', wq, hf) + bq
        k = jnp.einsum('oc,bcn->bno', wk, hf) + bk
        v = jnp.einsum('oc,bcn->bno', wv, hf) + bv
        scale = jnp.asarray(c, x.dtype) ** (-0.5)
        att = jax.nn.softmax(jnp.einsum('bic,bjc->bij', q, k) * scale, axis=-1)
        o = jnp.einsum('bij,bjc->bic', att, v)
        out = jnp.einsum('oc,bnc->bno', wo, o) + bo
        return x + out.transpose(0, 2, 1).reshape(b, c, h, w)

    def _L2_conv_ref(content_feat, f_w, f_b, g_w, g_b, h_w, h_b, o_w, o_b):
        import jax, jax.numpy as jnp
        import numpy as np
        EPS = 1e-05

        def mean_std_norm(x):
            mean = jnp.mean(x, axis=(2, 3), keepdims=True)
            var = jnp.var(x, axis=(2, 3), keepdims=True)
            return (x - mean) / jnp.sqrt(var + EPS)

        def conv1x1(x, w, b):
            return jnp.einsum('oc,bchw->bohw', w, x) + b[None, :, None, None]
        B, C, H, W = content_feat.shape
        HW = H * W
        norm = mean_std_norm(content_feat)
        F_Fc = conv1x1(norm, f_w, f_b).reshape(B, C, HW).transpose(0, 2, 1)
        G_Fs = conv1x1(norm, g_w, g_b).reshape(B, C, HW)
        energy = jnp.einsum('bnc,bcm->bnm', F_Fc, G_Fs)
        attention = jax.nn.softmax(energy, axis=-1)
        H_Fs = conv1x1(content_feat, h_w, h_b).reshape(B, C, HW)
        out = jnp.einsum('bcn,bmn->bcm', H_Fs, attention).reshape(B, C, H, W)
        out = conv1x1(out, o_w, o_b)
        return out + content_feat

    def _L3_conv_ref(x, w_qk, b_qk, w_v, b_v, mix_weight, w_out, bn_weight, bn_bias):
        import jax, jax.numpy as jnp
        import numpy as np
        N_HEAD, N_MIX, D_MODEL, D_K, D_V = (8, 2, 256, 32, 32)
        BN_EPS = 1e-05

        def avg_pool_3s2p1(x):
            dims, strides = ((1, 1, 3, 3), (1, 1, 2, 2))
            pad = [(0, 0), (0, 0), (1, 1), (1, 1)]
            s = jax.lax.reduce_window(x, 0.0, jax.lax.add, dims, strides, pad)
            cnt = jax.lax.reduce_window(jnp.ones_like(x), 0.0, jax.lax.add, dims, strides, pad)
            return s / cnt

        def conv1x1(x, w, b=None):
            y = jnp.einsum('bchw,oc->bohw', x, w)
            if b is not None:
                y = y + b.reshape(1, -1, 1, 1)
            return y
        B, C, H, W = x.shape
        m = N_MIX
        d = D_K // m
        temperature = np.power(D_K, 0.5)
        xp = avg_pool_3s2p1(x)
        kt = conv1x1(x, w_qk, b_qk).reshape(B * N_HEAD, D_K, H * W)
        qt = conv1x1(xp, w_qk, b_qk).reshape(B * N_HEAD, D_K, -1)
        vt = conv1x1(xp, w_v, b_v).reshape(B * N_HEAD, D_V, -1)
        Bp = B * N_HEAD
        N = H * W
        N2 = vt.shape[2]
        bar_kt = jnp.mean(kt, axis=2, keepdims=True)
        pi = jax.nn.softmax(jnp.einsum('md,bdo->bmo', mix_weight, bar_kt), axis=1)
        pi = pi.reshape(Bp * m, 1, 1)
        kt2 = kt.reshape(Bp * m, d, N).transpose(0, 2, 1)
        vt2 = vt.reshape(Bp * m, d, N2)
        q = qt.transpose(0, 2, 1)
        attn = jax.nn.softmax(kt2, axis=2)
        attn = jnp.einsum('bnd,bdk->bnk', attn, vt2)
        attn = (attn * pi).reshape(Bp, m, N, N2).sum(axis=1)
        attn = attn / temperature
        out = jnp.einsum('bnk,bkd->bnd', attn, q)
        out = out.transpose(0, 2, 1).reshape(B, N_HEAD * D_V, H, W)
        out = conv1x1(out, w_out)
        mu = out.mean(axis=(0, 2, 3), keepdims=True)
        var = out.var(axis=(0, 2, 3), keepdims=True)
        out = (out - mu) * jax.lax.rsqrt(var + BN_EPS)
        out = out * bn_weight.reshape(1, -1, 1, 1) + bn_bias.reshape(1, -1, 1, 1)
        return out + x

    def _gn(v, G=32, eps=1e-05):
        B_, C_, H_, W_ = v.shape
        g = v.reshape(B_, G, C_ // G, H_, W_)
        m = jnp.mean(g, axis=(2, 3, 4), keepdims=True)
        s = jnp.var(g, axis=(2, 3, 4), keepdims=True)
        return ((g - m) / jnp.sqrt(s + eps)).reshape(v.shape)

    def _ln_c(v, eps=1e-06):
        m = jnp.mean(v, axis=1, keepdims=True)
        s = jnp.var(v, axis=1, keepdims=True)
        return (v - m) / jnp.sqrt(s + eps)

    def _ln_t(v, eps=1e-05):
        m = jnp.mean(v, axis=-1, keepdims=True)
        s = jnp.var(v, axis=-1, keepdims=True)
        return (v - m) / jnp.sqrt(s + eps)

    def _to_tokens(v):
        B_, C_, H_, W_ = v.shape
        return v.reshape(B_, C_, H_ * W_).transpose(0, 2, 1)

    def _from_tokens(t, like):
        B_, C_, H_, W_ = like.shape
        return t.transpose(0, 2, 1).reshape(B_, C_, H_, W_)
    x = _L0_conv_ref(x, L0_conv_w_proj, L0_conv_b_proj, L0_conv_w_out, L0_conv_b_out)
    x = _L1_conv_ref(x, L1_conv_gn_w, L1_conv_gn_b, L1_conv_wq, L1_conv_bq, L1_conv_wk, L1_conv_bk, L1_conv_wv, L1_conv_bv, L1_conv_wo, L1_conv_bo)
    x = _L2_conv_ref(x, L2_conv_f_w, L2_conv_f_b, L2_conv_g_w, L2_conv_g_b, L2_conv_h_w, L2_conv_h_b, L2_conv_o_w, L2_conv_o_b)
    x = _L3_conv_ref(x, L3_conv_w_qk, L3_conv_b_qk, L3_conv_w_v, L3_conv_b_v, L3_conv_mix_weight, L3_conv_w_out, L3_conv_bn_weight, L3_conv_bn_bias)
    return x

_drawn_inputs = setup_inputs


def setup_inputs(seed=0):
    import zlib

    import numpy as np

    out = dict(_drawn_inputs(seed))
    spreads = {'L1_conv_gn_w': (1.0, 0.2),
     'L1_conv_gn_b': (0.0, 0.1),
     'L1_conv_bq': (0.0, 0.1),
     'L1_conv_bk': (0.0, 0.1),
     'L1_conv_bv': (0.0, 0.1),
     'L1_conv_bo': (0.0, 0.1),
     'L2_conv_f_b': (0.0, 0.1),
     'L2_conv_g_b': (0.0, 0.1),
     'L2_conv_h_b': (0.0, 0.1),
     'L2_conv_o_b': (0.0, 0.1),
     'L3_conv_b_qk': (0.0, 0.1),
     'L3_conv_b_v': (0.0, 0.1),
     'L3_conv_bn_weight': (1.0, 0.2),
     'L3_conv_bn_bias': (0.0, 0.1)}
    factors = {}
    for name, (base, spread) in spreads.items():
        noise = np.random.default_rng([zlib.crc32(name.encode()), seed]).standard_normal(out[name].shape)
        drawn = base * np.exp(spread * noise) if base else spread * noise
        out[name] = jnp.asarray(drawn.astype(out[name].dtype))
    for name, factor in factors.items():
        out[name] = (out[name] * factor).astype(out[name].dtype)
    return out
```

```python
from contextlib import ExitStack

import concourse.bass as bass
from concourse import mybir

F32 = mybir.dt.float32
F32R = mybir.dt.float32r
ALU = mybir.AluOpType
ACT = mybir.ActivationFunctionType
X = mybir.AxisListType.X

P = 128
B = 8
C = 256
N = 1024
CT = C // P
NT = N // P
HALF = N // 2
HEADS = 8
D = C // HEADS
G = P // D
NG = HEADS // G
IMAX = 96
NMAX = 2 * NT
K0 = IMAX + NMAX
SLOTS = 3
WIN = 16
POOLED = 16
N2 = POOLED * POOLED


def tensor_steps():
    s = [("qk0", 0, 0), ("qk0", 1, 0), ("v0", 0), ("v0", 1)]
    for h in range(G):
        s += [("s0", 0, h, it) for it in range(NT)]
        s += [("qk0", h, 1)] if h < 2 else []
    s += [("m0", 0)]
    for jt in range(NT):
        s += [("st0", 0, jt, h) for h in range(G)]
        s += [("pv0", 0, jt - 1)] if jt else []
        s += [("s0", 1, *divmod(G * jt + k, NT)) for k in range(G)]
    s += [("pv0", 0, NT - 1), ("m0", 1)]
    for jt in range(NT):
        s += [("st0", 1, jt, h) for h in range(G)]
        s += [("pv0", 1, jt - 1)] if jt else []
        s += [("den0", 0)] if jt == 1 else []
    s += [("pv0", 1, NT - 1), ("den0", 1), ("out0", 0), ("out0", 1)]
    for layer in (1, 2):
        s += [("gn", 0), ("gn", 1)] if layer == 1 else []
        s += [("qk", layer, t, ct) for t in range(2) for ct in range(CT)]
        s += [("s", layer, it) for it in range(NT)]
        s += [("v", layer, 0), ("v", layer, 1), ("m", layer)]
        for n in range(NT):
            s += [("st", layer, n)]
            s += [("pv", layer, n - 1)] if n else []
            s += [("den", layer, 0)] if n == NT // 2 else []
        s += [("pv", layer, NT - 1), ("den", layer, 1)]
    s += [("kt", 0), ("kt", 1), ("qv",), ("mt",), ("g",), ("smt", 0), ("smt", 1), ("z", 0), ("z", 1)]
    return s


def scalar_steps():
    s = [("x_hi", 0), ("x_hi", 1), ("qk0_hi", 0, 0), ("qk0_hi", 1, 0), ("v0_kept", 0), ("v0_kept", 1),
         ("qk0_hi", 0, 1), ("qk0_hi", 1, 1)]
    s += [("exp0", 0, jt, h) for jt in range(NT) for h in range(G)] + [("pv0_out", 0)]
    for jt in range(NT):
        s += [("res_hi", 0)] if jt == 5 else []
        s += [("exp0", 1, jt, h) for h in range(G)]
    s += [("pv0_out", 1), ("res_hi", 1)]
    for layer in (1, 2):
        s += [("feat_hi", 0), ("feat_hi", 1)] if layer == 2 else []
        s += [("ln", layer), ("inv_std", layer), ("norm_hi", layer, 0), ("norm_hi", layer, 1)]
        s += [("qk_hi", layer, t, ct) for t in range(2) for ct in range(CT)]
        s += [("v_hi", layer, 0), ("v_hi", layer, 1)]
        for n in range(NT):
            s += [("exp_hi", layer, n), ("exp", layer, n)]
            s += [("pv_out", layer, 0)] if n == NT // 2 else []
        s += [("pv_out", layer, 1)]
    s += [("x3_hi", 0), ("x3_hi", 1), ("kt_exp", 0), ("kt_exp", 1), ("mix_exp",), ("g_hi", 0), ("g_hi", 1),
          ("smt_hi", 0), ("smt_hi", 1), ("z_kept", 0), ("z_kept", 1)]
    return s


def vector_steps():
    s = [("x_lo", 0), ("x_lo", 1), ("qk0_lo", 0, 0), ("qk0_lo", 1, 0)]
    for h in range(G):
        s += [("max0", 0, h, it) for it in range(NT)]
        s += [("qk0_lo", h, 1)] if h < 2 else []
    for g in range(NG):
        s += [("neg_hi", g), ("neg_copy", g), ("neg_lo", g)] + [("max_rows", g, h) for h in range(G)]
        for jt in range(NT):
            if g == 0:
                s += [("max0", 1, *divmod(G * jt + k, NT)) for k in range(G)]
            else:
                s += [("rec0", 0), ("res", 0)] if jt == 2 else [("res_lo", 0)] if jt == 6 else []
            s += [("add0", g, jt, 2), ("add0", g, jt, 3)] if jt else []
    s += [("rec0", 1), ("res", 1), ("res_lo", 1), ("x1", 0), ("x1", 1)]
    for layer in (1, 2):
        s += [("feat_lo", 0), ("feat_lo", 1)] if layer == 2 else []
        s += [("stat", layer, k) for k in range(4)] + [("mv", layer, 0), ("mv", layer, 1)]
        s += [("gn", k) for k in range(4)] if layer == 1 else []
        s += [("var", layer), ("newton", layer, 0), ("newton", layer, 1), ("newton", layer, 2)]
        s += [("scale", layer), ("offset", layer), ("shift", layer)] if layer == 1 else [("shift", layer)]
        for ct in range(CT):
            s += [("norm", layer, ct), ("norm_lo", layer, ct)]
        s += [("qk_lo", layer, t, ct) for t in range(2) for ct in range(CT)]
        s += [("max", layer, it) for it in range(NT)]
        s += [("neg_hi", layer, 0), ("neg_copy", layer, 0), ("neg_lo", layer, 0)]
        s += [("v_lo", layer, 0), ("v_lo", layer, 1), ("max_in", layer)]
        for n in range(NT):
            s += [("rec", layer, 0)] if n == 5 else []
            s += [("out", layer, 0), ("x", layer, 0, 0), ("x", layer, 0, 1)] if n == 6 else []
            s += [("exp_lo", layer, n)] + ([("add", layer, n)] if n % 4 else [])
        s += [("rec", layer, 1), ("out", layer, 1), ("x", layer, 1, 0), ("x", layer, 1, 1)]
    s += [("x3_lo", 0), ("x3_lo", 1)] + [("stat", 3, k) for k in range(4)] + [("mv", 3, 0), ("mv", 3, 1)]
    s += [("kt_in", 0), ("win_max", 0), ("kt_sub", 0), ("kt_in", 1), ("win_max", 1), ("kt_sub", 1), ("qv_in",)]
    s += [("win_sum", 0), ("win_rec", 0), ("sm", 0), ("mt_in",), ("kbar",)]
    s += [("win_sum", 1), ("win_rec", 1), ("sm", 1)]
    s += [("mix", k) for k in range(4)] + [("mix_sum",), ("mix_rec",), ("mix_pi",)]
    s += [("g_lo", 0), ("g_lo", 1), ("smt_lo", 0), ("smt_lo", 1)]
    s += [("z_stat", ct, k) for ct in range(CT) for k in range(2)]
    return s


def pool_steps():
    s = [("add0", g, jt, h) for g in range(NG) for jt in range(1, NT) for h in range(2)]
    s += [("pool", k, ct) for k in range(5) for ct in range(CT)]
    return s


class Steps:

    def __init__(self, names):
        assert len(set(names)) == len(names)
        self.names, self.count, self.place = names, len(names), {n: k + 1 for k, n in enumerate(names)}

    def at(self, b, *name):
        return (b + 1) * self.count + self.place[name]

    def before(self, b, *name):
        return b * self.count + self.place[name]

    def start(self):
        self.todo = list(self.names)

    def one(self, *name):
        assert self.todo.pop(0) == name, name
        return 1


def last_reader(name):
    kind, rest = name[0], name[1:]
    return {
        "qk0": ("vector", "qk0_lo", *rest), "v0": ("scalar", "v0_kept", *rest),
        "s0": ("vector", "max0", *rest), "m0": ("vector", "max_rows", *rest, G - 1),
        "st0": ("scalar", "exp0", *rest), "den0": ("vector", "res", *rest), "out0": ("vector", "x1", *rest),
        "gn": ("vector", "gn", 0) if rest == (0,) else ("vector", "var", 1),
        "qk": ("vector", "qk_lo", *rest), "s": ("vector", "max", *rest), "v": ("vector", "v_lo", *rest),
        "m": ("vector", "max_in", *rest), "st": ("scalar", "exp", *rest), "den": ("vector", "out", *rest),
        "kt": ("vector", "kt_in", *rest), "qv": ("vector", "qv_in"), "mt": ("vector", "kbar"),
        "g": ("vector", "g_lo", CT - 1), "smt": ("vector", "smt_lo", *rest), "z": ("scalar", "z_kept", *rest),
    }[kind]


def conv_seq_kernel(nc, x, L0_w_proj, L0_b_proj, L0_w_out, L0_b_out, L1_gn_w, L1_gn_b, L1_wq, L1_bq,
                    L1_wk, L1_bk, L1_wv, L1_bv, L1_wo, L1_bo, L2_f_w, L2_f_b, L2_g_w, L2_g_b, L2_h_w,
                    L2_h_b, L2_o_w, L2_o_b, L3_w_qk, L3_b_qk, L3_w_v, L3_b_v, L3_mix, L3_w_out,
                    L3_bn_w, L3_bn_b, out):
    tensor, scalar, vector, gps = (Steps(f()) for f in (tensor_steps, scalar_steps, vector_steps, pool_steps))
    tiles = [n for n in tensor.names if not n[0].startswith("pv")]
    place = {n: k for k, n in enumerate(tiles)}

    def slot(*name):
        return place[name] % SLOTS

    def leaver(b, *name):
        k = place[name]
        former = tiles[k - SLOTS] if k >= SLOTS else [n for n in tiles if slot(*n) == k][-1]
        engine, *step = last_reader(former)
        steps = {"scalar": scalar, "vector": vector}[engine]
        return engine, (steps.at if k >= SLOTS else steps.before)(b, *step)

    x_v = x.rearrange("b (t p) h w -> b p t (h w)", p=P)
    out_v = out.rearrange("b (t p) h w -> b p t (h w)", p=P)
    z_dram = nc.dram_tensor("z_scratch", (B, P, CT, N), F32, kind="Internal").ap()
    w3f_dram = nc.dram_tensor("w3f_scratch", (P, CT, 2 * C), F32, kind="Internal").ap()
    wo3_dram = nc.dram_tensor("wo3_scratch", (P, CT, C), F32, kind="Internal").ap()
    x3_dram = nc.dram_tensor("x3_scratch", (B, P, CT, N), F32, kind="Internal").ap()

    with ExitStack() as ctx:
        def sb(name, shape, dt=F32):
            return ctx.enter_context(nc.sbuf_tensor(name, shape, dt))

        def sem(name):
            return ctx.enter_context(nc.semaphore(name))

        def share(*uses):
            made = {}
            for use in uses[:-1]:
                with ExitStack() as short:
                    for name, shape, dt in use:
                        made[name] = short.enter_context(nc.sbuf_tensor(name, shape, dt))
            for name, shape, dt in uses[-1]:
                made[name] = sb(name, shape, dt)
            return made

        w0h = sb("w0h", [P, CT, 3, C], F32R)
        w0l = sb("w0l", [P, CT, 3, C], F32R)
        wo0h = sb("wo0h", [P, CT, C], F32R)
        wo0l = sb("wo0l", [P, CT, C], F32R)
        wqk = {(l, t, s): sb(f"w_{l}{t}{s}", [P, CT, C], F32R) for l in (1, 2) for t in "qkv" for s in "hl"}
        w3h = sb("w3h", [P, CT, C], F32R)
        w3l = sb("w3l", [P, CT, C], F32R)
        ident = sb("ident", [P, P])
        ones = sb("ones", [P, P])
        ones_r = sb("ones_r", [P, P], F32R)
        gn_avg = sb("gn_avg", [P, P])
        heads_mask = sb("heads_mask", [P, P])
        mix_own = sb("mix_own", [P, P])
        mix_other = sb("mix_other", [P, P])
        mixcol = sb("mixcol", [P, 2])
        mask8 = sb("mask8", [NMAX, NT])
        cols = sb("cols", [P, 48])
        b3row = sb("b3row", [P, 2 * C])
        pool_w = sb("pool_w", [P, POOLED, POOLED])
        small = sb("small", [P, 128])
        max_in = sb("max_in", [P, N], F32R)
        bn_rows = sb("bn_rows", [P, CT, 2 * B, 6])
        raw = sb("raw", [P, N])
        act = sb("act", [P, CT, N])

        shared = share([("x_in", [P, CT, N], F32)], [("v0", [P, NT, C], F32)])
        x_in, v0 = shared["x_in"], shared["v0"]
        shared = share([("xh", [P, CT, N], F32R), ("xl", [P, CT, N], F32R)], [("acc0", [P, G, N], F32)])
        xh, xl, acc0 = shared["xh"], shared["xl"], shared["acc0"]
        side = sb("side", [P, 2, CT, N], F32R)
        shared = share([("stage", [P, 32 * C], F32)],
                       [("p0", [P, 2, G, N], F32)],
                       [("qk_r", [P, 2, 2, CT, N], F32R)])
        stage, p0, qk_r = shared["stage"], shared["p0"], shared["qk_r"]
        shared = share([("vh", [P, NT, C], F32R), ("vl", [P, NT, C], F32R), ("ph", [P, 2, N], F32R),
                        ("pl", [P, 2, N], F32R), ("p12", [P, 2, N], F32), ("tmp", [P, N], F32),
                        ("acc", [P, N], F32)],
                       [("kt", [P, NT, C], F32), ("zbuf", [P, CT, N], F32), ("qv", [P, 2, 2 * C], F32),
                        ("xp", [P, CT, N2], F32), ("row_sum", [P, CT, 32, POOLED], F32),
                        ("mtm", [P, CT, P], F32), ("gh", [P, CT, C], F32R), ("gl", [P, CT, C], F32R),
                        ("gap", [P, 17 * C], F32), ("w3f", [P, CT, 2 * C], F32), ("wo3", [P, CT, C], F32)],
                       [("zin", [P, 2, CT, N], F32), ("xin3", [P, 2, CT, N], F32), ("fin", [P, 2, CT, N], F32)],
                       [("stack", [P, 2, NG, G, N], F32R)])
        vh, vl, ph, pl, p12, tmp, acc = (shared[n] for n in ("vh", "vl", "ph", "pl", "p12", "tmp", "acc"))
        kt, zbuf, qv, xp, row_sum, mtm, gh, gl, w3f, wo3 = (
            shared[n] for n in ("kt", "zbuf", "qv", "xp", "row_sum", "mtm", "gh", "gl", "w3f", "wo3"))
        zin, xin3, fin, stack = (shared[n] for n in ("zin", "xin3", "fin", "stack"))

        tile = [ctx.enter_context(nc.psum_tensor(f"tile{k}", [P, N], F32)) for k in range(SLOTS)]
        pv = ctx.enter_context(nc.psum_tensor("pv", [P, N], F32))

        names = ["bq0", "bk0", "bv0", "bo0", "gnw", "gnb", "bq1", "bk1", "bv1", "bo1", "bq2", "bk2",
                 "bv2", "bo2", "b3", "bnw", "bnb", "bvo1", "bvo2", "scale", "shift", "bnscale", "bnshift"]

        def col(name, ct=None):
            k = 2 * names.index(name)
            return cols[:, k:k + 2] if ct is None else cols[:, k + ct:k + ct + 1]

        maxima = small[:, 0:G * NT]
        negmax = small[:, 32:32 + G * NMAX].rearrange("p (h s t) -> p h s t", h=G, s=2)
        stats = small[:, 96:120].rearrange("p (t k s) -> p t k s", t=CT, k=2)
        mv = small[:, 120:124].rearrange("p (t s) -> p t s", t=CT)
        mh = sb("mh", [P, G, NT], F32R)
        pairs = sb("pairs", [P, 48])
        (gmean, gdev, gsq, gvar, veps, vln, y0, y1, y2, inv_std, mscale) = (
            pairs[:, 2 * k:2 * k + 2] for k in range(11))
        kbar, larger, mix_sum, mix_rec, mix_pi = (pairs[:, 22 + 2 * k:24 + 2 * k] for k in range(5))
        logits, mix_e, logits_in = pairs[:, 32:36], pairs[:, 36:40], pairs[:, 40:44]
        win = sb("win", [P, NT * C // WIN])
        win_r = sb("win_r", [P, NT * C // WIN])

        weights_in = sem("weights_in"); vectors_in = sem("vectors_in"); consts_made = sem("consts_made")
        setup_tensor = sem("setup_tensor"); setup_scalar = sem("setup_scalar"); setup_vector = sem("setup_vector")
        tensor_done = sem("tensor_done"); scalar_done = sem("scalar_done")
        vector_done = sem("vector_done"); pool_done = sem("pool_done")
        w3_kept = sem("w3_kept"); w3_back = sem("w3_back")
        x_loaded = sem("x_loaded"); act_loaded = sem("act_loaded")
        stacked = [sem(f"stacked{g}") for g in range(NG)]
        x3_stored = sem("x3_stored"); z_stored = sem("z_stored")
        bn_in = [sem("bn_in0"), sem("bn_in1")]; bn_steps = sem("bn_steps"); bn_scaled = sem("bn_scaled")
        bn_added = sem("bn_added"); stored = [sem("stored0"), sem("stored1")]
        STACK_DMAS = 2 * G * 3 + 1
        NVEC = 3 * G + 14 + G + 2
        U = CT * C

        ctx.enter_context(nc.allow_non_contiguous_dma(reason="vectors of a few hundred elements"))
        block = ctx.enter_context(nc.Block())

        @block.sync
        def _(sp):
            sp.dma_start(stage[:, 0:3 * U].rearrange("p (t n) -> p t n", t=CT),
                         L0_w_proj.rearrange("(t p) n -> p t n", p=P)).then_inc(weights_in, 16)
            for k, w in enumerate((L0_w_out, L1_wq, L1_wk, L1_wo, L2_f_w, L2_g_w, L2_o_w, L3_w_qk,
                                   L3_w_v, L3_w_out, L1_wv, L2_h_w)):
                sp.dma_start(stage[:, (3 + k) * U:(4 + k) * U].rearrange("p (t n) -> p t n", t=CT),
                             w.rearrange("(t p) n -> p t n", p=P)).then_inc(weights_in, 16)
            sp.dma_start(x_in[:], x_v[0]).then_inc(x_loaded, 16)
            hb = L0_b_proj.rearrange("(t h s d) -> s h d t", t=CT, h=G, s=3)
            for s, name in enumerate(("bq0", "bk0", "bv0")):
                for h in range(G):
                    sp.dma_start(col(name)[D * h:D * h + D, :], hb[s, h]).then_inc(vectors_in, 16)
            for name, v in (("bo0", L0_b_out), ("gnw", L1_gn_w), ("gnb", L1_gn_b), ("bq1", L1_bq),
                            ("bk1", L1_bk), ("bv1", L1_bv), ("bo1", L1_bo), ("bq2", L2_f_b), ("bk2", L2_g_b),
                            ("bv2", L2_h_b), ("bo2", L2_o_b), ("b3", L3_b_qk), ("bnw", L3_bn_w), ("bnb", L3_bn_b)):
                sp.dma_start(col(name), v.rearrange("(t p) -> p t", p=P)).then_inc(vectors_in, 16)
            for h in range(G):
                sp.dma_start(mixcol[D * h:D * h + D, :], L3_mix.rearrange("m d -> d m")).then_inc(vectors_in, 16)
            for k, v in enumerate((L3_b_qk, L3_b_v)):
                sp.dma_start(b3row[:, k * C:(k + 1) * C],
                             v.rearrange("(a n) -> a n", a=1).broadcast_to((P, C))).then_inc(vectors_in, 16)

            sp.wait_ge(setup_scalar, 19)
            sp.dma_start(w3f_dram, w3f[:]).then_inc(w3_kept, 16)
            sp.dma_start(wo3_dram, wo3[:]).then_inc(w3_kept, 16)
            sp.wait_ge(w3_kept, 32)

            def batch(b, last):
                for g in range(NG):
                    sp.wait_ge(vector_done, vector.at(b, "qk0_lo", 1, g))
                    for t, parts in enumerate(((0, 0, 1), (0, 1, 0))):
                        for h in range(G):
                            for k, part in enumerate(parts):
                                sp.dma_start(stack[D * k:D * k + D, t, g, h, :].bitcast(F32),
                                             qk_r[D * h:D * h + D, t, part, g, :].bitcast(F32)
                                             ).then_inc(stacked[g], 16)
                    sp.dma_start(stack[IMAX:K0, 1, g].rearrange("p h (a n) -> p (h a) n", n=P).bitcast(F32),
                                 ones[0:NMAX, :].rearrange("p (a n) -> p a n", a=1)
                                 .broadcast_to((NMAX, G * N // P, P))).then_inc(stacked[g], 16)
                sp.dma_start(act[:], x_v[b]).then_inc(act_loaded, 16)
                sp.wait_ge(tensor_done, tensor.at(b, "pv0", 1, NT - 1))
                sp.dma_start(w3f[:], w3f_dram).then_inc(w3_back, 16)
                sp.dma_start(wo3[:], wo3_dram).then_inc(w3_back, 16)
                if not last:
                    sp.dma_start(x_in[:], x_v[b + 1]).then_inc(x_loaded, 16)
                sp.wait_ge(vector_done, vector.at(b, "x", 2, 1, 1))
                sp.dma_start(x3_dram[b], act[:]).then_inc(x3_stored, 16)
                sp.wait_ge(scalar_done, scalar.at(b, "z_kept", CT - 1))
                sp.dma_start(z_dram[b], zbuf[:]).then_inc(z_stored, 16)

            with sp.Fori(0, B - 1) as b:
                batch(b, False)
            batch(B - 1, True)

            sp.wait_ge(x3_stored, 16 * B)
            sp.wait_ge(z_stored, 16 * B)
            sp.wait_ge(tensor_done, tensor.at(B - 1, "z", CT - 1))
            sp.wait_ge(vector_done, vector.at(B - 1, "z_stat", CT - 1, 1))
            for b in range(B):
                if b >= 2:
                    sp.wait_ge(bn_added, CT * (b - 1))
                sp.dma_start(zin[:, b % 2], z_dram[b]).then_inc(bn_in[b % 2], 16)
                sp.dma_start(xin3[:, b % 2], x3_dram[b]).then_inc(bn_in[b % 2], 16)
                if b >= 1:
                    sp.wait_ge(bn_added, CT * b)
                    sp.dma_start(out_v[b - 1], fin[:, (b - 1) % 2]).then_inc(stored[(b - 1) % 2], 16)
            sp.wait_ge(bn_added, CT * B)
            sp.dma_start(out_v[B - 1], fin[:, (B - 1) % 2]).then_inc(stored[(B - 1) % 2], 16)
            for s in stored:
                sp.wait_ge(s, 16 * B // 2)

        @block.gpsimd
        def _(pool):
            pe = nc.gpsimd
            made = 0

            def note(ins):
                nonlocal made
                made += 1
                ins.then_inc(consts_made, 1)
                pool.wait_ge(consts_made, made)

            note(pe.memset(ident[:], 0.0))
            note(pe.memset(ones[:], 1.0))
            note(pe.memset(gn_avg[:], 1.0 / 8))
            note(pe.memset(heads_mask[:], 1.0))
            note(pe.memset(raw[:], 0.0))
            note(pe.memset(pool_w[:], 1.0 / 9))
            note(pe.memset(pool_w[:, 0, :], 1.0 / 6))
            note(pe.memset(pool_w[:, :, 0], 1.0 / 6))
            note(pe.memset(pool_w[:, 0, 0:1], 1.0 / 4))
            note(pe.affine_select(out=ident[:], in_=ident[:], compare_op=ALU.not_equal, fill=1.0, base=0,
                                  pattern=[[-1, P]], channel_multiplier=1))
            for m, w in ((gn_avg, 8), (heads_mask, D)):
                v = m[:].rearrange("p (a w) -> p a w", w=w)
                note(pe.affine_select(out=v, in_=v, compare_op=ALU.is_ge, fill=0.0, base=0,
                                      pattern=[[-w, P // w], [0, w]], channel_multiplier=1))
                note(pe.affine_select(out=v, in_=v, compare_op=ALU.is_ge, fill=0.0, base=w - 1,
                                      pattern=[[w, P // w], [0, w]], channel_multiplier=-1))
            pe.memset(win_r[:, 0:1], 1.0).then_inc(pool_done, gps.count)

            with pool.Fori(0, B) as b:
                gps.start()
                for g in range(NG):
                    for jt in range(1, NT):
                        for h in range(2):
                            pool.wait_ge(scalar_done, scalar.at(b, "exp0", g, jt, h))
                            if g == 1 and jt == 1:
                                pool.wait_ge(tensor_done, tensor.at(b, "den0", 0))
                            if jt > 1:
                                pool.wait_ge(pool_done, gps.at(b, "add0", g, jt - 1, h))
                            first = p0[:, 0, h, :] if jt == 1 else acc0[:, h, :]
                            pe.tensor_tensor(acc0[:, h, :], first, p0[:, jt % 2, h, :], ALU.add
                                             ).then_inc(pool_done, gps.one("add0", g, jt, h))
                a5 = act[:].rearrange("p t (y c s) -> p t y c s", y=2 * POOLED, s=2)
                r5 = row_sum[:].rearrange("p t (y s) c -> p t y s c", s=2)
                x4 = xp[:].rearrange("p t (y c) -> p t y c", y=POOLED)
                pool.wait_ge(vector_done, vector.at(b, "x", 2, 1, 1))
                for k in range(5):
                    if k:
                        pool.wait_ge(pool_done, gps.at(b, "pool", k - 1, CT - 1))
                    for ct in range(CT):
                        o, i0, i1, op = (
                            (row_sum[:, ct], a5[:, ct, :, :, 0], a5[:, ct, :, :, 1], ALU.add),
                            (row_sum[:, ct, :, 1:], row_sum[:, ct, :, 1:], a5[:, ct, :, 0:POOLED - 1, 1], ALU.add),
                            (x4[:, ct], r5[:, ct, :, 0, :], r5[:, ct, :, 1, :], ALU.add),
                            (x4[:, ct, 1:], x4[:, ct, 1:], r5[:, ct, 0:POOLED - 1, 1, :], ALU.add),
                            (x4[:, ct], x4[:, ct], pool_w[:], ALU.mult),
                        )[k]
                        pe.tensor_tensor(o, i0, i1, op).then_inc(pool_done, gps.one("pool", k, ct))
                assert not gps.todo

        @block.scalar
        def _(act_e):
            sc = nc.scalar
            ID = ACT.Identity

            def tile_wait(b, *name):
                act_e.wait_ge(tensor_done, tensor.at(b, *name))
                return tile[slot(*name)][:]

            act_e.wait_ge(weights_in, 16 * 13)
            w0 = stage[:, 0:3 * U].rearrange("p (t h s d) -> p t s h d", t=CT, h=HEADS, s=3)
            for ct in range(CT):
                for s in range(3):
                    sc.activation(w0h[:, ct, s, :].rearrange("p (h d) -> p h d", h=HEADS), w0[:, ct, s], ID
                                  ).then_inc(setup_scalar, 1)
            sc.activation(wo0h[:].rearrange("p t n -> p (t n)"), stage[:, 3 * U:4 * U], ID).then_inc(setup_scalar, 1)
            act_e.wait_ge(consts_made, 14)
            sc.activation(ones_r[:], ones[:], ID).then_inc(setup_scalar, 1)
            sc.activation(max_in[:], raw[:], ID).then_inc(setup_scalar, 1)
            flat = lambda w: w[:].rearrange("p t n -> p (t n)")
            for k, dst in enumerate((flat(wqk[1, "q", "h"]), flat(wqk[1, "k", "h"]), acc0[:, 0, 0:U],
                                     flat(wqk[2, "q", "h"]), flat(wqk[2, "k", "h"]), acc0[:, 1, 0:U],
                                     flat(w3h), None, flat(wo3))):
                act_e.wait_ge(setup_tensor, k + 1)
                src = tile[k % SLOTS][:, 0:U]
                src3 = src.rearrange("p (t n) -> p t n", t=CT)
                if k == 7:
                    sc.activation(w3f[:, :, C:], src3, ID).then_inc(setup_scalar, 1)
                else:
                    sc.activation(dst, src, ID).then_inc(setup_scalar, 1)
                if k == 6:
                    sc.activation(w3f[:, :, 0:C], src3, ID).then_inc(setup_scalar, 1)
            for k in range(2):
                act_e.wait_ge(setup_tensor, 10 + k)
                sc.activation(flat(wqk[1 + k, "v", "h"]), tile[k][:, 0:U], ID).then_inc(setup_scalar, 1)
            sc.activation(pairs[:, 46:47], ones[:, 0:1], ID).then_inc(scalar_done, scalar.count)

            with act_e.Fori(0, B) as b:
                scalar.start()
                act_e.wait_ge(x_loaded, 16 * b + 16)
                act_e.wait_ge(z_stored, 16 * b)
                act_e.wait_ge(x3_stored, 16 * b)
                act_e.wait_ge(pool_done, gps.before(b, "pool", 4, CT - 1))
                act_e.wait_ge(tensor_done, tensor.before(b, "z", CT - 1))
                for ct in range(CT):
                    sc.activation(xh[:, ct, :], x_in[:, ct, :], ID).then_inc(scalar_done, scalar.one("x_hi", ct))

                def qk0_hi(t, g):
                    sc.activation(qk_r[:, t, 0, g, :], tile_wait(b, "qk0", t, g), ID, bias=col(("bq0", "bk0")[t], g)
                                  ).then_inc(scalar_done, scalar.one("qk0_hi", t, g))

                qk0_hi(0, 0)
                qk0_hi(1, 0)
                act_e.wait_ge(vector_done, vector.at(b, "x_lo", 1))
                for k in range(2):
                    sc.activation(v0[:, 4 * k:4 * k + 4, :].rearrange("p t n -> p (t n)"), tile_wait(b, "v0", k), ID
                                  ).then_inc(scalar_done, scalar.one("v0_kept", k))
                qk0_hi(0, 1)
                qk0_hi(1, 1)

                def exp0(g, jt, h):
                    if jt >= 2:
                        act_e.wait_ge(tensor_done, tensor.at(b, "pv0", g, jt - 2))
                        summed = max(jt - 2, 1)
                    elif g == 1:
                        act_e.wait_ge(tensor_done, tensor.at(b, "pv0", 0, NT - 2 + jt))
                        summed = NT - 2 + jt
                    if jt >= 2 or g == 1:
                        of = g if jt >= 2 else 0
                        if h < 2:
                            act_e.wait_ge(pool_done, gps.at(b, "add0", of, summed, h))
                        else:
                            act_e.wait_ge(vector_done, vector.at(b, "add0", of, summed, h))
                    sc.activation(p0[:, jt % 2, h, :], tile_wait(b, "st0", g, jt, h), ACT.Exp, scale=float(D) ** -0.5
                                  ).then_inc(scalar_done, scalar.one("exp0", g, jt, h))

                def pv0_out(g):
                    act_e.wait_ge(tensor_done, tensor.at(b, "pv0", g, NT - 1))
                    if g == 1:
                        act_e.wait_ge(vector_done, vector.at(b, "res_lo", 0))
                    sc.activation(raw[:], pv[:], ID).then_inc(scalar_done, scalar.one("pv0_out", g))

                def res_hi(g):
                    act_e.wait_ge(vector_done, vector.at(b, "res", g))
                    sc.activation(side[:, 0, g, :], raw[:], ID, bias=col("bv0", g)
                                  ).then_inc(scalar_done, scalar.one("res_hi", g))

                for g in range(NG):
                    if g == 0:
                        for s in stacked:
                            act_e.wait_ge(s, 16 * STACK_DMAS * b + 16 * STACK_DMAS)
                    for jt in range(NT):
                        if g == 1 and jt == 5:
                            res_hi(0)
                        for h in range(G):
                            exp0(g, jt, h)
                    pv0_out(g)
                res_hi(1)

                for layer in (1, 2):
                    if layer == 2:
                        act_e.wait_ge(vector_done, vector.at(b, "x", 1, 1, 1))
                        for ct in range(CT):
                            sc.activation(side[:, 0, ct, :], act[:, ct, :], ID
                                          ).then_inc(scalar_done, scalar.one("feat_hi", ct))
                    act_e.wait_ge(vector_done, vector.at(b, "var", layer))
                    sc.activation(vln, veps, ACT.Ln).then_inc(scalar_done, scalar.one("ln", layer))
                    act_e.wait_ge(scalar_done, scalar.at(b, "ln", layer))
                    sc.activation(y0, vln, ACT.Exp, scale=-0.5).then_inc(scalar_done, scalar.one("inv_std", layer))
                    act_e.wait_ge(vector_done, vector.at(b, "shift", layer))
                    for ct in range(CT):
                        sc.activation(xh[:, ct, :], act[:, ct, :], ID, bias=col("shift", ct), scale=col("scale", ct)
                                      ).then_inc(scalar_done, scalar.one("norm_hi", layer, ct))
                    for t in range(2):
                        for ct in range(CT):
                            sc.activation(qk_r[:, t, 0, ct, :], tile_wait(b, "qk", layer, t, ct), ID,
                                          bias=col(f"b{'qk'[t]}{layer}", ct)
                                          ).then_inc(scalar_done, scalar.one("qk_hi", layer, t, ct))
                    for k in range(2):
                        sc.activation(vh[:, 4 * k:4 * k + 4, :].rearrange("p t n -> p (t n)"),
                                      tile_wait(b, "v", layer, k), ID).then_inc(scalar_done, scalar.one("v_hi", layer, k))

                    def pv_out(half):
                        act_e.wait_ge(tensor_done, tensor.at(b, "pv", layer, 4 * half + 3))
                        if half:
                            act_e.wait_ge(vector_done, vector.at(b, "x", layer, 0, 1))
                        sc.activation(raw[:], pv[:], ID).then_inc(scalar_done, scalar.one("pv_out", layer, half))

                    scale = float(C) ** -0.5 if layer == 1 else 1.0
                    for n in range(NT):
                        if n >= 2:
                            act_e.wait_ge(tensor_done, tensor.at(b, "pv", layer, n - 2))
                            act_e.wait_ge(vector_done, vector.at(b, "exp_lo", layer, n - 2))
                            act_e.wait_ge(vector_done, vector.at(b, "add", layer, n - 2 + (n % 4 == 2)))
                        scores = tile_wait(b, "st", layer, n)
                        sc.activation(ph[:, n % 2, :], scores, ACT.Exp, scale=scale
                                      ).then_inc(scalar_done, scalar.one("exp_hi", layer, n))
                        sc.activation(p12[:, n % 2, :], scores, ACT.Exp, scale=scale
                                      ).then_inc(scalar_done, scalar.one("exp", layer, n))
                        if n == NT // 2:
                            pv_out(0)
                    pv_out(1)

                act_e.wait_ge(vector_done, vector.at(b, "x", 2, 1, 1))
                for ct in range(CT):
                    sc.activation(xh[:, ct, :], act[:, ct, :], ID).then_inc(scalar_done, scalar.one("x3_hi", ct))
                for k in range(2):
                    act_e.wait_ge(vector_done, vector.at(b, "kt_sub", k))
                    v = kt[:, 4 * k:4 * k + 4, :].rearrange("p t n -> p (t n)")
                    sc.activation(v, v, ACT.Exp).then_inc(scalar_done, scalar.one("kt_exp", k))
                act_e.wait_ge(vector_done, vector.at(b, "mix", 3))
                sc.activation(mix_e, logits, ACT.Exp).then_inc(scalar_done, scalar.one("mix_exp"))
                act_e.wait_ge(vector_done, vector.at(b, "mix_pi"))
                gt = tile_wait(b, "g")
                for ct in range(CT):
                    sc.activation(gh[:, ct, :], gt[:, ct * C:(ct + 1) * C], ID, scale=mix_pi[:, ct:ct + 1]
                                  ).then_inc(scalar_done, scalar.one("g_hi", ct))
                for ct in range(CT):
                    sc.activation(qk_r[:, 0, 0, ct, :], tile_wait(b, "smt", ct), ID
                                  ).then_inc(scalar_done, scalar.one("smt_hi", ct))
                for ct in range(CT):
                    sc.activation(zbuf[:, ct, :], tile_wait(b, "z", ct), ID
                                  ).then_inc(scalar_done, scalar.one("z_kept", ct))
                assert not scalar.todo

            act_e.wait_ge(bn_steps, 3)
            sc.activation(vln, veps, ACT.Ln).then_inc(bn_steps, 1)
            act_e.wait_ge(bn_steps, 4)
            sc.activation(y0, vln, ACT.Exp, scale=-0.5).then_inc(bn_steps, 1)
            act_e.wait_ge(bn_steps, 11)
            for b in range(B):
                act_e.wait_ge(bn_in[b % 2], 32 * (b // 2 + 1))
                for ct in range(CT):
                    sc.activation(zin[:, b % 2, ct, :], zin[:, b % 2, ct, :], ID, bias=col("bnshift", ct),
                                  scale=col("bnscale", ct)).then_inc(bn_scaled, 1)

        @block.vector
        def _(dve):
            ve = nc.vector
            TT, STT, TS = ve.tensor_tensor, ve.scalar_tensor_tensor, ve.tensor_scalar
            f = lambda ap: ap.bitcast(F32)
            flat = lambda w: w[:].rearrange("p t n -> p (t n)")

            dve.wait_ge(setup_scalar, 7)
            w0 = stage[:, 0:3 * U].rearrange("p (t h s d) -> p t s h d", t=CT, h=HEADS, s=3)
            for ct in range(CT):
                for s in range(3):
                    v = lambda w: w[:, ct, s, :].rearrange("p (h d) -> p h d", h=HEADS)
                    TT(v(w0l), w0[:, ct, s], f(v(w0h)), ALU.subtract).then_inc(setup_vector, 1)
            TT(flat(wo0l), stage[:, 3 * U:4 * U], f(flat(wo0h)), ALU.subtract).then_inc(setup_vector, 1)
            for k, hi, lo in ((0, wqk[1, "q", "h"], wqk[1, "q", "l"]), (1, wqk[1, "k", "h"], wqk[1, "k", "l"]),
                              (3, wqk[2, "q", "h"], wqk[2, "q", "l"]), (4, wqk[2, "k", "h"], wqk[2, "k", "l"]),
                              (6, w3h, w3l)):
                dve.wait_ge(setup_scalar, 10 + k + (k == 6))
                TT(flat(lo), tile[k % SLOTS][:, 0:U], f(flat(hi)), ALU.subtract).then_inc(setup_vector, 1)
            for k in range(2):
                dve.wait_ge(setup_scalar, 20 + k)
                TT(flat(wqk[1 + k, "v", "l"]), tile[k][:, 0:U], f(flat(wqk[1 + k, "v", "h"])), ALU.subtract
                   ).then_inc(setup_vector, 1)
            dve.wait_ge(setup_tensor, 12)
            dve.wait_ge(vectors_in, 16 * NVEC)
            for k in range(2):
                TT(col(f"bvo{k + 1}"), pv[:, 2 * k:2 * k + 2], col(f"bo{k + 1}"), ALU.add).then_inc(setup_vector, 1)
            for m in range(2):
                for dst, src in ((mix_own, m), (mix_other, 1 - m)):
                    v = lambda w: w[:].rearrange("p (h m e) -> p m h e", h=G, m=2)[:, m]
                    TS(v(dst), v(heads_mask), mixcol[:, src:src + 1], None, ALU.mult).then_inc(setup_vector, 1)
            TT(mask8[:], ident[0:NMAX, 0:NT], ident[0:NMAX, NT:NMAX], ALU.add).then_inc(setup_vector, 1)
            ve.memset(pairs[:, 47:48], 1.0).then_inc(vector_done, vector.count)

            with dve.Fori(0, B) as b:
                vector.start()

                def own(*step):
                    dve.wait_ge(vector_done, vector.at(b, *step))

                def tile_wait(*name):
                    dve.wait_ge(tensor_done, tensor.at(b, *name))
                    return tile[slot(*name)]

                def scalar_wait(*step):
                    dve.wait_ge(scalar_done, scalar.at(b, *step))

                dve.wait_ge(tensor_done, tensor.before(b, "z", CT - 1))
                for ct in range(CT):
                    scalar_wait("x_hi", ct)
                    TT(xl[:, ct, :], x_in[:, ct, :], f(xh[:, ct, :]), ALU.subtract
                       ).then_inc(vector_done, vector.one("x_lo", ct))

                def qk0_lo(t, g):
                    scalar_wait("qk0_hi", t, g)
                    STT(qk_r[:, t, 1, g, :], tile[slot("qk0", t, g)][:], col(("bq0", "bk0")[t], g),
                        f(qk_r[:, t, 0, g, :]), ALU.add, ALU.subtract).then_inc(vector_done, vector.one("qk0_lo", t, g))

                def max0(g, h, it):
                    t = tile_wait("s0", g, h, it)
                    ve.tensor_reduce(maxima[:, h * NT + it:h * NT + it + 1], t[:], X, ALU.max
                                     ).then_inc(vector_done, vector.one("max0", g, h, it))

                def negate(key, heads, last):
                    own(*last)
                    m3 = maxima[:, 0:heads * NT].rearrange("p (h t) -> p h t", h=heads)
                    hi = mh[:, 0:heads, :]
                    TS(hi, m3, -1.0, None, ALU.mult).then_inc(vector_done, vector.one("neg_hi", *key))
                    own("neg_hi", *key)
                    ve.tensor_copy(negmax[:, 0:heads, 0, :], f(hi)).then_inc(vector_done, vector.one("neg_copy", *key))
                    STT(negmax[:, 0:heads, 1, :], m3, -1.0, f(hi), ALU.mult, ALU.subtract
                        ).then_inc(vector_done, vector.one("neg_lo", *key))

                def spread(dst, src):
                    return TT(dst.rearrange("p (t n) -> p t n", t=NT),
                              src.rearrange("p (a n) -> p a n", a=1).broadcast_to((NMAX, NT, P)),
                              mask8[:].rearrange("p (t a) -> p t a", a=1).broadcast_to((NMAX, NT, P)), ALU.mult)

                def add0(g, jt, h):
                    scalar_wait("exp0", g, jt, h)
                    if g == 1 and jt == 1:
                        dve.wait_ge(tensor_done, tensor.at(b, "den0", 0))
                    if jt > 1:
                        own("add0", g, jt - 1, h)
                    first = p0[:, 0, h, :] if jt == 1 else acc0[:, h, :]
                    TT(acc0[:, h, :], first, p0[:, jt % 2, h, :], ALU.add).then_inc(vector_done, vector.one("add0", g, jt, h))

                def normalise0(g):
                    den = tile_wait("den0", g)
                    ve.reciprocal(den[:], den[:]).then_inc(vector_done, vector.one("rec0", g))
                    own("rec0", g)
                    scalar_wait("pv0_out", g)
                    TT(raw[:], raw[:], den[:], ALU.mult).then_inc(vector_done, vector.one("res", g))

                def res_lo(g):
                    scalar_wait("res_hi", g)
                    STT(side[:, 1, g, :], raw[:], col("bv0", g), f(side[:, 0, g, :]), ALU.add, ALU.subtract
                        ).then_inc(vector_done, vector.one("res_lo", g))

                qk0_lo(0, 0)
                qk0_lo(1, 0)
                for h in range(G):
                    for it in range(NT):
                        max0(0, h, it)
                    if h < 2:
                        qk0_lo(h, 1)
                for g in range(NG):
                    negate((g,), G, ("max0", g, G - 1, NT - 1))
                    t = tile_wait("m0", g)
                    for h in range(G):
                        spread(stack[IMAX:K0, 0, g, h, :], t[0:NMAX, h * P:(h + 1) * P]
                               ).then_inc(vector_done, vector.one("max_rows", g, h))
                    for jt in range(NT):
                        if g == 0:
                            for k in range(G):
                                max0(1, *divmod(G * jt + k, NT))
                        elif jt == 2:
                            normalise0(0)
                        elif jt == 6:
                            res_lo(0)
                        if jt:
                            add0(g, jt, 2)
                            add0(g, jt, 3)
                normalise0(1)
                res_lo(1)
                dve.wait_ge(act_loaded, 16 * b + 16)
                for ct in range(CT):
                    t = tile_wait("out0", ct)
                    STT(act[:, ct, :], t[:], col("bo0", ct), act[:, ct, :], ALU.add, ALU.add
                        ).then_inc(vector_done, vector.one("x1", ct))

                def statistics(layer):
                    for ct in range(CT):
                        for k in range(2):
                            ve.bn_stats(stats[:, ct, k, :], act[:, ct, k * HALF:(k + 1) * HALF]
                                        ).then_inc(vector_done, vector.one("stat", layer, 2 * ct + k))
                    own("stat", layer, 3)
                    ve.memset(pairs[:, 45:46], 0.0)
                    for ct in range(CT):
                        ve.bn_aggr(mv[:, ct, :], stats[:, ct]).then_inc(vector_done, vector.one("mv", layer, ct))

                for layer in (1, 2):
                    own(*(("x1", 1) if layer == 1 else ("x", 1, 1, 1)))
                    if layer == 2:
                        for ct in range(CT):
                            scalar_wait("feat_hi", ct)
                            TT(side[:, 1, ct, :], act[:, ct, :], f(side[:, 0, ct, :]), ALU.subtract
                               ).then_inc(vector_done, vector.one("feat_lo", ct))
                    statistics(layer)
                    own("mv", layer, 1)
                    if layer == 1:
                        t = tile_wait("gn", 0)
                        ve.tensor_copy(gmean, t[:, 0:2]).then_inc(vector_done, vector.one("gn", 0))
                        own("gn", 0)
                        TT(gdev, mv[:, :, 0], gmean, ALU.subtract).then_inc(vector_done, vector.one("gn", 1))
                        own("gn", 1)
                        TT(gsq, gdev, gdev, ALU.mult).then_inc(vector_done, vector.one("gn", 2))
                        own("gn", 2)
                        TT(gvar, gsq, mv[:, :, 1], ALU.add).then_inc(vector_done, vector.one("gn", 3))
                        t = tile_wait("gn", 1)
                        TS(veps, t[:, 0:2], 1e-6, None, ALU.add).then_inc(vector_done, vector.one("var", 1))
                        mean = gmean
                    else:
                        TS(veps, mv[:, :, 1], 1e-5, None, ALU.add).then_inc(vector_done, vector.one("var", 2))
                        mean = mv[:, :, 0]
                    scalar_wait("inv_std", layer)
                    own("var", layer)
                    TT(y1, y0, y0, ALU.mult).then_inc(vector_done, vector.one("newton", layer, 0))
                    own("newton", layer, 0)
                    STT(y2, y1, -0.5, veps, ALU.mult, ALU.mult).then_inc(vector_done, vector.one("newton", layer, 1))
                    own("newton", layer, 1)
                    if layer == 1:
                        STT(inv_std, y2, 1.5, y0, ALU.add, ALU.mult).then_inc(vector_done, vector.one("newton", 1, 2))
                        own("newton", 1, 2)
                        TT(col("scale"), inv_std, col("gnw"), ALU.mult).then_inc(vector_done, vector.one("scale", 1))
                        own("scale", 1)
                        TT(mscale, mean, col("scale"), ALU.mult).then_inc(vector_done, vector.one("offset", 1))
                        own("offset", 1)
                        TT(col("shift"), col("gnb"), mscale, ALU.subtract).then_inc(vector_done, vector.one("shift", 1))
                    else:
                        STT(col("scale"), y2, 1.5, y0, ALU.add, ALU.mult).then_inc(vector_done, vector.one("newton", 2, 2))
                        own("newton", 2, 2)
                        STT(col("shift"), mean, -1.0, col("scale"), ALU.mult, ALU.mult
                            ).then_inc(vector_done, vector.one("shift", 2))
                    own("shift", layer)
                    for ct in range(CT):
                        if ct:
                            own("norm_lo", layer, 0)
                        TS(tmp[:], act[:, ct, :], col("scale", ct), col("shift", ct), ALU.mult, ALU.add
                           ).then_inc(vector_done, vector.one("norm", layer, ct))
                        own("norm", layer, ct)
                        scalar_wait("norm_hi", layer, ct)
                        TT(xl[:, ct, :], tmp[:], f(xh[:, ct, :]), ALU.subtract
                           ).then_inc(vector_done, vector.one("norm_lo", layer, ct))
                    for t in range(2):
                        for ct in range(CT):
                            scalar_wait("qk_hi", layer, t, ct)
                            STT(qk_r[:, t, 1, ct, :], tile[slot("qk", layer, t, ct)][:], col(f"b{'qk'[t]}{layer}", ct),
                                f(qk_r[:, t, 0, ct, :]), ALU.add, ALU.subtract
                                ).then_inc(vector_done, vector.one("qk_lo", layer, t, ct))
                    for it in range(NT):
                        t = tile_wait("s", layer, it)
                        ve.tensor_reduce(maxima[:, it:it + 1], t[:], X, ALU.max
                                         ).then_inc(vector_done, vector.one("max", layer, it))
                    negate((layer, 0), 1, ("max", layer, NT - 1))
                    for k in range(2):
                        scalar_wait("v_hi", layer, k)
                        v = lambda w: w[:, 4 * k:4 * k + 4, :].rearrange("p t n -> p (t n)")
                        TT(v(vl), tile[slot("v", layer, k)][:], f(v(vh)), ALU.subtract
                           ).then_inc(vector_done, vector.one("v_lo", layer, k))
                    t = tile_wait("m", layer)
                    spread(max_in[0:NMAX, :], t[0:NMAX, 0:P]).then_inc(vector_done, vector.one("max_in", layer))

                    def reciprocal(half):
                        den = tile_wait("den", layer, half)
                        ve.reciprocal(den[:, 0:HALF], den[:, 0:HALF]).then_inc(vector_done, vector.one("rec", layer, half))

                    def finish(half):
                        own("rec", layer, half)
                        scalar_wait("pv_out", layer, half)
                        r3 = raw[:].rearrange("p (t n) -> p t n", t=CT)
                        TT(r3, r3, tile[slot("den", layer, half)][:, 0:HALF].rearrange("p (a n) -> p a n", a=1).broadcast_to((P, CT, HALF)),
                           ALU.mult).then_inc(vector_done, vector.one("out", layer, half))
                        own("out", layer, half)
                        for ct in range(CT):
                            a = act[:, ct, half * HALF:(half + 1) * HALF]
                            STT(a, r3[:, ct, :], col(f"bvo{layer}", ct), a, ALU.add, ALU.add
                                ).then_inc(vector_done, vector.one("x", layer, half, ct))

                    for n in range(NT):
                        if n == 5:
                            reciprocal(0)
                        if n == 6:
                            finish(0)
                        scalar_wait("exp", layer, n)
                        TT(pl[:, n % 2, :], p12[:, n % 2, :], f(ph[:, n % 2, :]), ALU.subtract
                           ).then_inc(vector_done, vector.one("exp_lo", layer, n))
                        if n % 4:
                            if n % 4 > 1:
                                own("add", layer, n - 1)
                            elif n == 5:
                                dve.wait_ge(tensor_done, tensor.at(b, "den", layer, 0))
                            first = p12[:, 0, :] if n % 4 == 1 else acc[:]
                            TT(acc[:], first, p12[:, n % 2, :], ALU.add).then_inc(vector_done, vector.one("add", layer, n))
                    reciprocal(1)
                    finish(1)

                own("x", 2, 1, 1)
                for ct in range(CT):
                    scalar_wait("x3_hi", ct)
                    TT(xl[:, ct, :], act[:, ct, :], f(xh[:, ct, :]), ALU.subtract
                       ).then_inc(vector_done, vector.one("x3_lo", ct))
                statistics(3)
                kw = kt[:].rearrange("p t (w e) -> p (t w) e", e=WIN)
                W4 = NT * C // WIN // 2

                def wide(ap):
                    return ap.rearrange("p (w a) -> p w a", a=1).broadcast_to((P, W4, WIN))

                for k in range(2):
                    t = tile_wait("kt", k)
                    TT(kt[:, 4 * k:4 * k + 4, :], t[:].rearrange("p (t n) -> p t n", t=4),
                       b3row[:, 0:C].rearrange("p (a n) -> p a n", a=1).broadcast_to((P, 4, C)), ALU.add
                       ).then_inc(vector_done, vector.one("kt_in", k))
                    own("kt_in", k)
                    w, wm = kw[:, k * W4:(k + 1) * W4, :], win[:, k * W4:(k + 1) * W4]
                    ve.tensor_reduce(wm, w, X, ALU.max).then_inc(vector_done, vector.one("win_max", k))
                    own("win_max", k)
                    TT(w, w, wide(wm), ALU.subtract).then_inc(vector_done, vector.one("kt_sub", k))
                t = tile_wait("qv")
                TT(qv[:], t[:].rearrange("p (t n) -> p t n", t=2),
                   b3row[:].rearrange("p (a n) -> p a n", a=1).broadcast_to((P, 2, 2 * C)), ALU.add
                   ).then_inc(vector_done, vector.one("qv_in"))

                def windows(k):
                    w, ws = kw[:, k * W4:(k + 1) * W4, :], win[:, k * W4:(k + 1) * W4]
                    wr = win_r[:, k * W4:(k + 1) * W4]
                    scalar_wait("kt_exp", k)
                    ve.tensor_reduce(ws, w, X, ALU.add).then_inc(vector_done, vector.one("win_sum", k))
                    own("win_sum", k)
                    ve.reciprocal(wr, ws).then_inc(vector_done, vector.one("win_rec", k))
                    own("win_rec", k)
                    TT(w, w, wide(wr), ALU.mult).then_inc(vector_done, vector.one("sm", k))

                windows(0)
                t = tile_wait("mt")
                TT(mtm[:], t[:, 0:CT * P].rearrange("p (t n) -> p t n", t=CT),
                   heads_mask[:].rearrange("p (a n) -> p a n", a=1).broadcast_to((P, CT, P)), ALU.mult
                   ).then_inc(vector_done, vector.one("mt_in"))
                TT(kbar, t[:, HALF:HALF + CT], col("b3"), ALU.add).then_inc(vector_done, vector.one("kbar"))
                windows(1)
                t = tile_wait("g")
                ve.tensor_copy(logits_in, t[:, HALF:HALF + 4]).then_inc(vector_done, vector.one("mix", 0))
                own("mix", 0)
                TT(larger, logits_in[:, 0:2], logits_in[:, 2:4], ALU.max).then_inc(vector_done, vector.one("mix", 1))
                own("mix", 1)
                TT(logits[:, 0:2], logits_in[:, 0:2], larger, ALU.subtract).then_inc(vector_done, vector.one("mix", 2))
                TT(logits[:, 2:4], logits_in[:, 2:4], larger, ALU.subtract).then_inc(vector_done, vector.one("mix", 3))
                scalar_wait("mix_exp")
                TT(mix_sum, mix_e[:, 0:2], mix_e[:, 2:4], ALU.add).then_inc(vector_done, vector.one("mix_sum"))
                own("mix_sum")
                ve.reciprocal(mix_rec, mix_sum).then_inc(vector_done, vector.one("mix_rec"))
                own("mix_rec")
                STT(mix_pi, mix_e[:, 0:2], float(D) ** -0.5, mix_rec, ALU.mult, ALU.mult
                    ).then_inc(vector_done, vector.one("mix_pi"))
                own("mix_pi")
                for ct in range(CT):
                    scalar_wait("g_hi", CT - 1)
                    STT(gl[:, ct, :], t[:, ct * C:(ct + 1) * C], mix_pi[:, ct:ct + 1], f(gh[:, ct, :]),
                        ALU.mult, ALU.subtract).then_inc(vector_done, vector.one("g_lo", ct))
                for ct in range(CT):
                    scalar_wait("smt_hi", ct)
                    TT(qk_r[:, 0, 1, ct, :], tile[slot("smt", ct)][:], f(qk_r[:, 0, 0, ct, :]), ALU.subtract
                       ).then_inc(vector_done, vector.one("smt_lo", ct))
                for ct in range(CT):
                    scalar_wait("z_kept", ct)
                    for k in range(2):
                        ve.bn_stats(bn_rows[:, ct, bass.ds(2 * b + k, 1), :], zbuf[:, ct, k * HALF:(k + 1) * HALF]
                                    ).then_inc(vector_done, vector.one("z_stat", ct, k))
                assert not vector.todo

            chain = 0

            def link(ins):
                nonlocal chain
                chain += 1
                ins.then_inc(bn_steps, 1)
                dve.wait_ge(bn_steps, chain)

            dve.wait_ge(vector_done, vector.at(B - 1, "z_stat", CT - 1, 1))
            for ct in range(CT):
                link(ve.bn_aggr(mv[:, ct, :], bn_rows[:, ct]))
            link(TS(veps, mv[:, :, 1], 1e-5, None, ALU.add))
            chain += 2
            dve.wait_ge(bn_steps, chain)
            link(TT(y1, y0, y0, ALU.mult))
            link(STT(y2, y1, -0.5, veps, ALU.mult, ALU.mult))
            link(STT(inv_std, y2, 1.5, y0, ALU.add, ALU.mult))
            link(TT(col("bnscale"), inv_std, col("bnw"), ALU.mult))
            link(TT(mscale, mv[:, :, 0], col("bnscale"), ALU.mult))
            link(TT(col("bnshift"), col("bnb"), mscale, ALU.subtract))
            for b in range(B):
                for ct in range(CT):
                    dve.wait_ge(bn_scaled, CT * b + ct + 1)
                    if b >= 2:
                        dve.wait_ge(stored[b % 2], 16 * (b // 2))
                    TT(fin[:, b % 2, ct, :], zin[:, b % 2, ct, :], xin3[:, b % 2, ct, :], ALU.add).then_inc(bn_added, 1)

        @block.tensor
        def _(pe):
            mm = nc.tensor.matmul
            halves = [slice(0, HALF), slice(HALF, N)]

            def three(out, lhs, rhs, first=True, last=True):
                n, parts = len(lhs[0]), ((0, 0), (0, 1), (1, 0))
                for kt_ in range(n):
                    for m, (a, c) in enumerate(parts):
                        ins = mm(out, lhs[a][kt_], rhs[c][kt_], start=first and kt_ == 0 and m == 0,
                                 stop=last and kt_ == n - 1 and m == 2)
                return ins

            pe.wait_ge(weights_in, 16 * 13)
            pe.wait_ge(consts_made, 14)
            for k in range(9):
                if k >= SLOTS:
                    pe.wait_ge(setup_scalar, 10 + k - SLOTS)
                    pe.wait_ge(setup_vector, (8, 9, 9, 10, 11, 11)[k - SLOTS])
                w = stage[:, (4 + k) * U:(5 + k) * U].rearrange("p (t n) -> p t n", t=CT)
                for ct in range(CT):
                    for ot in range(CT):
                        ins = nc.tensor.transpose(tile[k % SLOTS][:, ct * C + ot * P:ct * C + (ot + 1) * P],
                                                  w[:, ot, ct * P:(ct + 1) * P], ident[:])
                ins.then_inc(setup_tensor, 1)
            pe.wait_ge(setup_scalar, 19)
            pe.wait_ge(setup_vector, 12)
            pe.wait_ge(vectors_in, 16 * NVEC)
            for k in range(2):
                wv = stage[:, (13 + k) * U:(14 + k) * U].rearrange("p (t n) -> p t n", t=CT)
                wo = acc0[:, k, 0:U].rearrange("p (t n) -> p t n", t=CT)
                for ct in range(CT):
                    for et in range(CT):
                        ins = mm(tile[k][:, ct * C:(ct + 1) * C], wv[:, et, ct * P:(ct + 1) * P], wo[:, et, :],
                                 start=et == 0, stop=et == CT - 1)
                ins.then_inc(setup_tensor, 1)
            for k in range(2):
                wo = acc0[:, k, 0:U].rearrange("p (t n) -> p t n", t=CT)
                for ot in range(CT):
                    for et in range(CT):
                        ins = mm(pv[:, 2 * k + ot:2 * k + ot + 1], wo[:, et, ot * P:(ot + 1) * P],
                                 col(f"bv{k + 1}", et), start=et == 0, stop=et == CT - 1)
            ins.then_inc(setup_tensor, 1)
            pe.wait_ge(scalar_done, scalar.count)
            pe.wait_ge(vector_done, vector.count)
            mm(tile[0][:, 0:P], ones[:], ident[:], start=True, stop=True).then_inc(tensor_done, tensor.count)

            with pe.Fori(0, B) as b:
                tensor.start()

                def scalar_wait(*step):
                    pe.wait_ge(scalar_done, scalar.at(b, *step))

                def vector_wait(*step):
                    pe.wait_ge(vector_done, vector.at(b, *step))

                def free(*name):
                    engine, count = leaver(b, *name)
                    pe.wait_ge(scalar_done if engine == "scalar" else vector_done, count)
                    return tile[slot(*name)]

                kts = range(CT)

                def qk0(t, g):
                    o = free("qk0", t, g)
                    for s in halves:
                        ins = three(o[:, s], [[w[:, kt_, t, g * P:(g + 1) * P] for kt_ in kts] for w in (w0h, w0l)],
                                    [[v[:, kt_, s] for kt_ in kts] for v in (xh, xl)])
                    ins.then_inc(tensor_done, tensor.one("qk0", t, g))

                def s0(g, h, it):
                    if h == 0 and it == 0:
                        pe.wait_ge(stacked[g], 16 * STACK_DMAS * b + 16 * STACK_DMAS)
                    o = free("s0", g, h, it)
                    for s in halves:
                        ins = mm(o[:, s], stack[0:IMAX, 0, g, h, it * P:(it + 1) * P], stack[0:IMAX, 1, g, h, s],
                                 start=True, stop=True)
                    ins.then_inc(tensor_done, tensor.one("s0", g, h, it))

                def m0(g):
                    vector_wait("neg_lo", g)
                    o = free("m0", g)
                    for h in range(G):
                        ins = nc.tensor.transpose(o[0:NMAX, h * P:(h + 1) * P],
                                                  negmax[:, h].rearrange("p s t -> p (s t)"), ident[:])
                    ins.then_inc(tensor_done, tensor.one("m0", g))

                def st0(g, jt, h):
                    if jt == 0:
                        vector_wait("max_rows", g, h)
                    o = free("st0", g, jt, h)
                    for s in halves:
                        ins = mm(o[:, s], stack[0:K0, 1, g, h, jt * P:(jt + 1) * P], stack[0:K0, 0, g, h, s],
                                 start=True, stop=True)
                    ins.then_inc(tensor_done, tensor.one("st0", g, jt, h))

                def pv0(g, jt):
                    scalar_wait("exp0", g, jt, G - 1)
                    if jt == 0 and g == 1:
                        scalar_wait("pv0_out", 0)
                    for s in halves:
                        for h in range(G):
                            ins = mm(pv[D * h:D * h + D, s], v0[:, jt, g * P + D * h:g * P + D * h + D],
                                     p0[:, jt % 2, h, s], start=jt == 0, stop=jt == NT - 1)
                    ins.then_inc(tensor_done, tensor.one("pv0", g, jt))

                def den0(g):
                    pe.wait_ge(pool_done, gps.at(b, "add0", g, NT - 1, 1))
                    vector_wait("add0", g, NT - 1, G - 1)
                    o = free("den0", g)
                    for s in halves:
                        for h in range(G):
                            ins = mm(o[D * h:D * h + D, s], ones[:, 0:D], acc0[:, h, s], start=True, stop=True)
                    ins.then_inc(tensor_done, tensor.one("den0", g))

                scalar_wait("x_hi", CT - 1)
                vector_wait("x_lo", CT - 1)
                qk0(0, 0)
                qk0(1, 0)
                for k in range(2):
                    o = free("v0", k)
                    for q in range(4):
                        i = slice((4 * k + q) * P, (4 * k + q + 1) * P)
                        ins = three(o[:, q * C:(q + 1) * C], [[v[:, kt_, i] for kt_ in kts] for v in (xh, xl)],
                                    [[w[:, kt_, 2, :] for kt_ in kts] for w in (w0h, w0l)])
                    ins.then_inc(tensor_done, tensor.one("v0", k))
                for h in range(G):
                    for it in range(NT):
                        s0(0, h, it)
                    if h < 2:
                        qk0(h, 1)
                m0(0)
                for jt in range(NT):
                    for h in range(G):
                        st0(0, jt, h)
                    if jt:
                        pv0(0, jt - 1)
                    for k in range(G):
                        s0(1, *divmod(G * jt + k, NT))
                pv0(0, NT - 1)
                m0(1)
                for jt in range(NT):
                    for h in range(G):
                        st0(1, jt, h)
                    if jt:
                        pv0(1, jt - 1)
                    if jt == 1:
                        den0(0)
                pv0(1, NT - 1)
                den0(1)
                for g in range(NG):
                    scalar_wait("res_hi", g)
                    vector_wait("res_lo", g)
                for ct in range(CT):
                    o = free("out0", ct)
                    for s in halves:
                        ins = three(o[:, s], [[w[:, kt_, ct * P:(ct + 1) * P] for kt_ in kts] for w in (wo0h, wo0l)],
                                    [[side[:, part, kt_, s] for kt_ in kts] for part in range(2)])
                    ins.then_inc(tensor_done, tensor.one("out0", ct))

                for layer in (1, 2):
                    if layer == 1:
                        vector_wait("mv", 1, 1)
                        mm(free("gn", 0)[:, 0:2], gn_avg[:], mv[:, :, 0], start=True, stop=True
                           ).then_inc(tensor_done, tensor.one("gn", 0))
                        vector_wait("gn", 3)
                        mm(free("gn", 1)[:, 0:2], gn_avg[:], gvar, start=True, stop=True
                           ).then_inc(tensor_done, tensor.one("gn", 1))
                    scalar_wait("norm_hi", layer, 1)
                    vector_wait("norm_lo", layer, 1)
                    for t in range(2):
                        wh, wl = wqk[layer, "qk"[t], "h"], wqk[layer, "qk"[t], "l"]
                        for ct in range(CT):
                            o = free("qk", layer, t, ct)
                            for s in halves:
                                ins = three(o[:, s], [[w[:, kt_, ct * P:(ct + 1) * P] for kt_ in kts] for w in (wh, wl)],
                                            [[v[:, kt_, s] for kt_ in kts] for v in (xh, xl)])
                            ins.then_inc(tensor_done, tensor.one("qk", layer, t, ct))
                    scalar_wait("qk_hi", layer, 1, 1)
                    for it in range(NT):
                        o = free("s", layer, it)
                        for s in halves:
                            for kt_ in kts:
                                ins = mm(o[:, s], qk_r[:, 0, 0, kt_, it * P:(it + 1) * P], qk_r[:, 1, 0, kt_, s],
                                         start=kt_ == 0, stop=kt_ == CT - 1)
                        ins.then_inc(tensor_done, tensor.one("s", layer, it))
                    feat = (xh, xl) if layer == 1 else (side[:, 0], side[:, 1])
                    if layer == 2:
                        vector_wait("feat_lo", 1)
                    wh, wl = wqk[layer, "v", "h"], wqk[layer, "v", "l"]
                    for k in range(2):
                        o = free("v", layer, k)
                        for q in range(4):
                            j = slice((4 * k + q) * P, (4 * k + q + 1) * P)
                            ins = three(o[:, q * C:(q + 1) * C], [[v[:, kt_, j] for kt_ in kts] for v in feat],
                                        [[w[:, kt_, :] for kt_ in kts] for w in (wh, wl)])
                        ins.then_inc(tensor_done, tensor.one("v", layer, k))
                    vector_wait("neg_lo", layer, 0)
                    nc.tensor.transpose(free("m", layer)[0:NMAX, 0:P], negmax[:, 0].rearrange("p s t -> p (s t)"),
                                        ident[:]).then_inc(tensor_done, tensor.one("m", layer))
                    vector_wait("qk_lo", layer, 1, 1)
                    vector_wait("max_in", layer)

                    def scores(n):
                        half, jp = divmod(n, 4)
                        i = halves[half]
                        o = free("st", layer, n)
                        for q in range(2):
                            j = slice((2 * jp + q) * P, (2 * jp + q + 1) * P)
                            three(o[:, halves[q]], [[qk_r[:, 1, part, kt_, j] for kt_ in kts] for part in range(2)],
                                  [[qk_r[:, 0, part, kt_, i] for kt_ in kts] for part in range(2)], last=False)
                            ins = mm(o[:, halves[q]], ones_r[:], max_in[:, i], start=False, stop=True)
                        ins.then_inc(tensor_done, tensor.one("st", layer, n))

                    def values(n):
                        half, jp = divmod(n, 4)
                        scalar_wait("exp_hi", layer, n)
                        vector_wait("exp_lo", layer, n)
                        if n == 4:
                            scalar_wait("pv_out", layer, 0)
                        if n == 0:
                            vector_wait("v_lo", layer, 1)
                        for q in range(2):
                            j = 2 * jp + q
                            for ct in range(CT):
                                ins = three(pv[:, halves[ct]], [[v[:, j, ct * P:(ct + 1) * P]] for v in (vh, vl)],
                                            [[p[:, n % 2, halves[q]]] for p in (ph, pl)],
                                            first=jp == 0 and q == 0, last=jp == 3 and q == 1)
                        ins.then_inc(tensor_done, tensor.one("pv", layer, n))

                    def sums(half):
                        vector_wait("add", layer, 4 * half + 3)
                        o = free("den", layer, half)
                        for q in range(2):
                            ins = mm(o[:, 0:HALF], ones[:], acc[:, halves[q]], start=q == 0, stop=q == 1)
                        ins.then_inc(tensor_done, tensor.one("den", layer, half))

                    for n in range(NT):
                        scores(n)
                        if n:
                            values(n - 1)
                        if n == NT // 2:
                            sums(0)
                    values(NT - 1)
                    sums(1)

                scalar_wait("x3_hi", 1)
                vector_wait("x3_lo", 1)
                for k in range(2):
                    o = free("kt", k)
                    for q in range(4):
                        i = slice((4 * k + q) * P, (4 * k + q + 1) * P)
                        ins = three(o[:, q * C:(q + 1) * C], [[v[:, kt_, i] for kt_ in kts] for v in (xh, xl)],
                                    [[w[:, kt_, :] for kt_ in kts] for w in (w3h, w3l)])
                    ins.then_inc(tensor_done, tensor.one("kt", k))
                pe.wait_ge(pool_done, gps.at(b, "pool", 4, CT - 1))
                pe.wait_ge(w3_back, 32 * b + 32)
                o = free("qv")
                for k in range(2):
                    for kt_ in kts:
                        ins = mm(o[:, halves[k]], xp[:, kt_, k * P:(k + 1) * P], w3f[:, kt_, :],
                                 start=kt_ == 0, stop=kt_ == CT - 1)
                ins.then_inc(tensor_done, tensor.one("qv"))
                vector_wait("qv_in")
                o = free("mt")
                for ct in range(CT):
                    for k in range(2):
                        mm(o[:, ct * P:(ct + 1) * P], qv[:, k, ct * P:(ct + 1) * P],
                           qv[:, k, C + ct * P:C + (ct + 1) * P], start=k == 0, stop=k == 1)
                for ct in range(CT):
                    for kt_ in kts:
                        ins = mm(o[:, HALF + ct:HALF + ct + 1], w3f[:, kt_, ct * P:(ct + 1) * P], mv[:, kt_, 0:1],
                                 start=kt_ == 0, stop=kt_ == CT - 1)
                ins.then_inc(tensor_done, tensor.one("mt"))
                vector_wait("kbar")
                o = free("g")
                for ct in range(CT):
                    mm(o[:, ct * C:(ct + 1) * C], mtm[:, ct, :], wo3[:, ct, :], start=True, stop=True)
                mm(o[:, HALF:HALF + 2], mix_own[:], kbar, start=True, stop=True)
                mm(o[:, HALF + 2:HALF + 4], mix_other[:], kbar, start=True, stop=True
                   ).then_inc(tensor_done, tensor.one("g"))
                vector_wait("sm", 1)
                for ct in range(CT):
                    o = free("smt", ct)
                    for nt in range(NT):
                        ins = nc.tensor.transpose(o[:, nt * P:(nt + 1) * P], kt[:, nt, ct * P:(ct + 1) * P], ident[:])
                    ins.then_inc(tensor_done, tensor.one("smt", ct))
                scalar_wait("smt_hi", 1)
                vector_wait("smt_lo", 1)
                for ct in range(CT):
                    o = free("z", ct)
                    for s in halves:
                        ins = three(o[:, s], [[g_[:, kt_, ct * P:(ct + 1) * P] for kt_ in kts] for g_ in (gh, gl)],
                                    [[qk_r[:, 0, part, kt_, s] for kt_ in kts] for part in range(2)])
                    ins.then_inc(tensor_done, tensor.one("z", ct))
                assert not tensor.todo


_INS = ["x", "L0_conv_w_proj", "L0_conv_b_proj", "L0_conv_w_out", "L0_conv_b_out", "L1_conv_gn_w", "L1_conv_gn_b",
        "L1_conv_wq", "L1_conv_bq", "L1_conv_wk", "L1_conv_bk", "L1_conv_wv", "L1_conv_bv", "L1_conv_wo", "L1_conv_bo",
        "L2_conv_f_w", "L2_conv_f_b", "L2_conv_g_w", "L2_conv_g_b", "L2_conv_h_w", "L2_conv_h_b", "L2_conv_o_w",
        "L2_conv_o_b", "L3_conv_w_qk", "L3_conv_b_qk", "L3_conv_w_v", "L3_conv_b_v", "L3_conv_mix_weight",
        "L3_conv_w_out", "L3_conv_bn_weight", "L3_conv_bn_bias"]


def kernel(**inputs):
    import numpy as _np
    import concourse.bacc as _bacc
    from concourse import mybir as _mybir
    from concourse.bass_utils import run_bass_kernel_spmd as _run

    nc = _bacc.Bacc("TRN2", target_bir_lowering=False, num_devices=1)
    arrays, args = {}, []
    for name in _INS:
        a = _np.ascontiguousarray(inputs[name])
        arrays[f"in_{name}_dram"] = a
        args.append(nc.dram_tensor(f"in_{name}_dram", a.shape, _mybir.dt.from_np(a.dtype), kind="ExternalInput").ap())
    args.append(nc.dram_tensor("out_dram", (B, C, 32, 32), F32, kind="ExternalOutput").ap())
    conv_seq_kernel(nc, *args)
    r = _run(nc, [arrays], core_ids=[0])
    return r.results[0]["out_dram"]
```

```python
from contextlib import ExitStack

import concourse.bass as bass
from concourse import mybir

F32 = mybir.dt.float32
F32R = mybir.dt.float32r
ALU = mybir.AluOpType
ACT = mybir.ActivationFunctionType
X = mybir.AxisListType.X

P = 128
B = 8
C = 256
N = 1024
CT = C // P
NT = N // P
HALF = N // 2
HEADS = 8
D = C // HEADS
G = P // D
NG = HEADS // G
IMAX = 96
NMAX = 2 * NT
K0 = IMAX + NMAX
SEG = D // NT
SLOTS = 3
WIN = 16
POOLED = 16
N2 = POOLED * POOLED


def adder(g, jt, h):
    if jt in (0, NT - 1):
        return None
    on_pool = 2 + (jt % 2 == 0) if g == 0 else 1 + (jt % 2 == 0)
    return "pool" if h < on_pool else "vector"


def tensor_steps():
    s = [("qk0", t, g) for g in range(NG) for t in range(2)]
    for h in range(G):
        s += [("s0", 0, h, it) for it in range(NT // 2)] + ([("v0", h - 1)] if h in (1, 2) else [])
        s += [("s0", 0, h, it) for it in range(NT // 2, NT)]
    s += [("m0", 0)]
    for jt in range(NT):
        for k in range(G):
            s += [("st0", 0, jt, k), ("s0", 1, *divmod(G * jt + k, NT))]
        s += [("pv0", 0, jt - 1)] if jt else []
    s += [("m0", 1), ("pv0", 0, NT - 1)]
    for jt in range(NT):
        s += [("st0", 1, jt, h) for h in range(G)]
        s += [("pv0", 1, jt - 1)] if jt else [("den0", 0)]
        s += [("ex0", 0), ("ex0+", 0)] if jt == 2 else []
    s += [("den0", 1), ("pv0", 1, NT - 1), ("ex0", 1), ("ex0+", 1), ("out0", 0), ("out0", 1)]
    for layer in (1, 2):
        s += [("gn", 0), ("gn", 1)] if layer == 1 else [("v", 2, 0)]
        s += [("qk", layer, t, ct) for t in range(2) for ct in range(CT)]
        s += [("v", 1, 0)] if layer == 1 else []
        s += [("s", layer, it) for it in range(4)] + [("v", layer, 1)] + [("s", layer, it) for it in range(4, NT)]
        s += [("m", layer), ("st", layer, 0)]
        for n in range(1, NT):
            s += [("st", layer, n), ("pv", layer, n - 1)]
            s += [("den", layer, 0)] if n == NT // 2 else []
        s += [("den", layer, 1), ("pv", layer, NT - 1)]
    s += [("kt", 0), ("kt", 1), ("qv",), ("mt",), ("g",), ("smt", 0), ("smt", 1), ("z", 0), ("z", 1)]
    return s


def scalar_steps():
    s = [("qk0_hi", t, g) for g in range(NG) for t in range(2)]
    s += [("v0_kept", 0), ("v0_kept", 1)]
    s += [("exp0", 0, jt, h) for jt in range(NT) for h in range(G)] + [("pv0_out", 0)]
    for jt in range(NT):
        s += [("res_hi", 0, 0), ("res_hi", 0, 1)] if jt == 5 else []
        s += [("exp0", 1, jt, h) for h in range(G)]
    s += [("pv0_out", 1), ("res_hi", 1, 0), ("res_hi", 1, 1)]
    for layer in (1, 2):
        s += [("ln", layer), ("inv_std", layer)] + [("norm_hi", layer, k, ct) for k in range(2) for ct in range(CT)]
        s += [("qk_hi", layer, t, ct) for t in range(2) for ct in range(CT)]
        s += [("v_hi", 1, 0)] if layer == 1 else []
        s += [("v_hi", layer, 1)]
        for n in range(NT - 1):
            s += [("exp_hi", layer, n), ("exp", layer, n)]
            s += [("pv_out", layer, 0)] if n == NT // 2 else []
        s += [("feat_hi", layer + 1, 0, ct) for ct in range(CT)] + [("exp", layer, NT - 1), ("exp_hi", layer, NT - 1)]
        s += [("pv_out", layer, 1)] + ([("v_hi", 2, 0)] if layer == 1 else [])
        s += [("feat_hi", layer + 1, 1, ct) for ct in range(CT)]
    s += [("kt_exp", 0), ("kt_exp", 1), ("x_hi", 0), ("x_hi", 1), ("mix_exp",), ("g_hi", 0), ("g_hi", 1)]
    s += [("smt_hi", 0), ("smt_hi", 1), ("z_kept", 0), ("z_kept", 1)]
    return s


def vector_steps():
    s = [("qk0_lo", t, g) for g in range(NG) for t in range(2)]
    s += [("max0", 0, h, it) for h in range(G) for it in range(NT)]
    for g in range(NG):
        s += [("neg_hi", g), ("neg_copy", g), ("neg_lo", g)] + [("max_rows", g, h) for h in range(G)]
        s += [("rec0", 0)] if g == 1 else []
        for jt in range(NT):
            mine = [("add0", g, jt, h) for h in range(G) if adder(g, jt, h) == "vector"]
            if g == 0:
                due = [("add0", g, jt - 1, h) for h in range(G) if adder(g, jt - 1, h) == "vector"] if jt else []
                for k in range(G):
                    s += [("max0", 1, *divmod(G * jt + k, NT))]
                    s += due[k // 2:k // 2 + 1] if k % 2 == 0 else []
            else:
                s += mine
            if g == 1:
                s += [("rows0", 0, 0), ("rows0", 0, 1)] if jt == 1 else []
                s += [("res", 0, 0), ("res", 0, 1)] if jt == 2 else []
                s += [("res_lo", 0, 0), ("res_lo", 0, 1)] if jt == 5 else []
    s += [("rec0", 1), ("rows0", 1, 0), ("rows0", 1, 1), ("res", 1, 0), ("res", 1, 1)]
    s += [("res_lo", 1, 0), ("res_lo", 1, 1)]
    for k in range(2):
        s += [("x1", k, ct) for ct in range(CT)] + [("stat", 1, k, ct) for ct in range(CT)]
    for layer in (1, 2):
        s += [("mv", layer, 0), ("mv", layer, 1)]
        s += [("gn", k) for k in range(4)] if layer == 1 else []
        s += [("var", layer)]
        s += [("feat_lo", 2, 1, ct) for ct in range(CT)] + [("v_lo", 2, 0)] if layer == 2 else []
        s += [("newton", layer, 0), ("newton", layer, 1), ("newton", layer, 2)]
        s += [("scale", layer), ("offset", layer), ("shift", layer)] if layer == 1 else [("shift", layer)]
        for k in range(2):
            s += [("norm", layer, k, ct) for ct in range(CT)] + [("norm_lo", layer, k, ct) for ct in range(CT)]
        s += [("qk_lo", layer, t, ct) for t in range(2) for ct in range(CT)]
        s += [("v_lo", 1, 0)] if layer == 1 else []
        s += [("max", layer, it) for it in range(4)] + [("v_lo", layer, 1)] + [("max", layer, it) for it in range(4, NT)]
        s += [("neg_hi", layer, 0), ("neg_copy", layer, 0), ("neg_lo", layer, 0), ("max_in", layer)]
        for n in range(NT - 1):
            s += [("rec", layer, 0)] if n == 5 else []
            s += [("out", layer, 0), ("x", layer, 0, 0), ("x", layer, 0, 1)] if n == 6 else []
            s += [("exp_lo", layer, n)] + ([("add", layer, n)] if n % 4 else [])
        s += [("stat", layer + 1, 0, ct) for ct in range(CT)] + [("feat_lo", layer + 1, 0, ct) for ct in range(CT)]
        s += [("add", layer, NT - 1), ("exp_lo", layer, NT - 1)]
        s += [("rec", layer, 1), ("out", layer, 1), ("x", layer, 1, 0), ("x", layer, 1, 1)]
        s += [("stat", 2, 1, ct) for ct in range(CT)] if layer == 1 else []
    s += [("feat_lo", 3, 1, ct) for ct in range(CT)]
    s += [("kt_in", 0), ("win_max", 0), ("kt_sub", 0)] + [("stat", 3, 1, ct) for ct in range(CT)]
    s += [("mv", 3, 0), ("mv", 3, 1), ("kt_in", 1), ("win_max", 1), ("kt_sub", 1), ("qv_in",)]
    s += [("win_sum", 0), ("win_rec", 0), ("sm", 0), ("mt_in",), ("kbar",)]
    s += [("win_sum", 1), ("win_rec", 1), ("sm", 1)]
    s += [("mix", k) for k in range(4)] + [("mix_sum",), ("mix_rec",), ("mix_pi",)]
    s += [("g_lo", 0), ("g_lo", 1), ("smt_lo", 0), ("smt_lo", 1), ("x_lo", 0), ("x_lo", 1)]
    s += [("z_stat", ct, k) for ct in range(CT) for k in range(2)]
    return s


def pool_steps():
    s = [("add0", g, jt, h) for g in range(NG) for jt in range(1, NT) for h in range(G) if adder(g, jt, h) == "pool"]
    s += [("pool", k, ct) for k in range(5) for ct in range(CT)]
    return s


class Steps:

    def __init__(self, names):
        assert len(set(names)) == len(names)
        self.names, self.count, self.place = names, len(names), {n: k + 1 for k, n in enumerate(names)}

    def at(self, b, *name):
        return (b + 1) * self.count + self.place[name]

    def before(self, b, *name):
        return b * self.count + self.place[name]

    def start(self):
        self.todo = list(self.names)

    def one(self, *name):
        assert self.todo.pop(0) == name, name
        return 1


def last_reader(name):
    kind, rest = name[0], name[1:]
    return {
        "qk0": ("vector", "qk0_lo", *rest), "v0": ("scalar", "v0_kept", *rest),
        "s0": ("vector", "max0", *rest), "m0": ("vector", "max_rows", *rest, G - 1),
        "st0": ("scalar", "exp0", *rest), "den0": ("vector", "rec0", *rest),
        "ex0": ("vector", "res", *rest, 1), "out0": ("vector", "x1", *rest, CT - 1),
        "gn": ("vector", "gn", 0) if rest == (0,) else ("vector", "var", 1),
        "qk": ("vector", "qk_lo", *rest), "s": ("vector", "max", *rest), "v": ("vector", "v_lo", *rest),
        "m": ("vector", "max_in", *rest), "st": ("scalar", "exp" if rest[-1:] != (NT - 1,) else "exp_hi", *rest), "den": ("vector", "out", *rest),
        "kt": ("vector", "kt_in", *rest), "qv": ("vector", "qv_in"), "mt": ("vector", "kbar"),
        "g": ("vector", "g_lo", CT - 1), "smt": ("vector", "smt_lo", *rest), "z": ("scalar", "z_kept", *rest),
    }[kind]


def conv_seq_kernel(nc, x, L0_w_proj, L0_b_proj, L0_w_out, L0_b_out, L1_gn_w, L1_gn_b, L1_wq, L1_bq,
                    L1_wk, L1_bk, L1_wv, L1_bv, L1_wo, L1_bo, L2_f_w, L2_f_b, L2_g_w, L2_g_b, L2_h_w,
                    L2_h_b, L2_o_w, L2_o_b, L3_w_qk, L3_b_qk, L3_w_v, L3_b_v, L3_mix, L3_w_out,
                    L3_bn_w, L3_bn_b, out):
    tensor, scalar, vector, gps = (Steps(f()) for f in (tensor_steps, scalar_steps, vector_steps, pool_steps))
    tiles = [n for n in tensor.names if not n[0].startswith("pv") and not n[0].endswith("+")]
    place = {n: k for k, n in enumerate(tiles)}

    def slot(*name):
        return place[name] % SLOTS

    def leaver(b, *name):
        k = place[name]
        former = tiles[k - SLOTS] if k >= SLOTS else [n for n in tiles if slot(*n) == k][-1]
        engine, *step = last_reader(former)
        steps = {"scalar": scalar, "vector": vector}[engine]
        return engine, (steps.at if k >= SLOTS else steps.before)(b, *step)

    x_v = x.rearrange("b (t p) h w -> b p t (h w)", p=P)
    out_v = out.rearrange("b (t p) h w -> b p t (h w)", p=P)
    z_dram = nc.dram_tensor("z_scratch", (B, P, CT, N), F32, kind="Internal").ap()
    w3f_dram = nc.dram_tensor("w3f_scratch", (P, CT, 2 * C), F32, kind="Internal").ap()
    wo3_dram = nc.dram_tensor("wo3_scratch", (P, CT, C), F32, kind="Internal").ap()
    x3_dram = nc.dram_tensor("x3_scratch", (B, P, CT, N), F32, kind="Internal").ap()

    with ExitStack() as ctx:
        def sb(name, shape, dt=F32):
            return ctx.enter_context(nc.sbuf_tensor(name, shape, dt))

        def sem(name):
            return ctx.enter_context(nc.semaphore(name))

        def share(*uses):
            made = {}
            for use in uses[:-1]:
                with ExitStack() as short:
                    for name, shape, dt in use:
                        made[name] = short.enter_context(nc.sbuf_tensor(name, shape, dt))
            for name, shape, dt in uses[-1]:
                made[name] = sb(name, shape, dt)
            return made

        w0h = sb("w0h", [P, CT, 3, C], F32R)
        w0l = sb("w0l", [P, CT, 3, C], F32R)
        wo0h = sb("wo0h", [P, CT, C], F32R)
        wo0l = sb("wo0l", [P, CT, C], F32R)
        wqk = {(l, t, s): sb(f"w_{l}{t}{s}", [P, CT, C], F32R) for l in (1, 2) for t in "qkv" for s in "hl"}
        w3h = sb("w3h", [P, CT, C], F32R)
        w3l = sb("w3l", [P, CT, C], F32R)
        ident = sb("ident", [P, P])
        ones = sb("ones", [P, P])
        ones_r = sb("ones_r", [P, P], F32R)
        gn_avg = sb("gn_avg", [P, P])
        heads_mask = sb("heads_mask", [P, P])
        mix_own = sb("mix_own", [P, P])
        mix_other = sb("mix_other", [P, P])
        mixcol = sb("mixcol", [P, 2])
        mask8 = sb("mask8", [NMAX, NT])
        segment = sb("segment", [P, 2 * D - SEG])
        seg_own = sb("seg_own", [P, NT])
        cols = sb("cols", [P, 48])
        b3row = sb("b3row", [P, 2 * C])
        pool_w = sb("pool_w", [P, POOLED, POOLED])
        small = sb("small", [P, 128])
        max_in = sb("max_in", [P, N], F32R)
        bn_rows = sb("bn_rows", [P, CT, 2 * B, 6])
        raw = sb("raw", [P, N])
        rec0 = sb("rec0", [P, P])
        act = sb("act", [P, CT, N])

        shared = share([("x_in", [P, CT, N], F32)], [("v0", [P, NT, C], F32)])
        x_in, v0 = shared["x_in"], shared["v0"]
        shared = share([("xh", [P, CT, N], F32R), ("xl", [P, CT, N], F32R)], [("acc0", [P, G, N], F32)])
        xh, xl, acc0 = shared["xh"], shared["xl"], shared["acc0"]
        shared = share([("side_front", [P, 3 * N], F32), ("rows0", [P, NT, P], F32)],
                       [("side", [P, 2, CT, N], F32R)])
        side, rows0 = shared["side"], shared["rows0"]
        shared = share([("stage", [P, 32 * C], F32)],
                       [("p0", [P, 2, G, N], F32)],
                       [("qk_r", [P, 2, 2, CT, N], F32R)])
        stage, p0, qk_r = shared["stage"], shared["p0"], shared["qk_r"]
        shared = share([("vh", [P, NT, C], F32R), ("vl", [P, NT, C], F32R), ("ph", [P, 2, N], F32R),
                        ("pl", [P, 2, N], F32R), ("p12", [P, 2, N], F32), ("tmp", [P, N], F32),
                        ("acc", [P, N], F32)],
                       [("kt", [P, NT, C], F32), ("zbuf", [P, CT, N], F32), ("qv", [P, 2, 2 * C], F32),
                        ("xp", [P, CT, N2], F32), ("row_sum", [P, CT, 32, POOLED], F32),
                        ("mtm", [P, CT, P], F32), ("gh", [P, CT, C], F32R), ("gl", [P, CT, C], F32R),
                        ("gap", [P, 17 * C], F32), ("w3f", [P, CT, 2 * C], F32), ("wo3", [P, CT, C], F32)],
                       [("zin", [P, 2, CT, N], F32), ("xin3", [P, 2, CT, N], F32), ("fin", [P, 2, CT, N], F32)],
                       [("stack", [P, 2, NG, G, N], F32R)])
        vh, vl, ph, pl, p12, tmp, acc = (shared[n] for n in ("vh", "vl", "ph", "pl", "p12", "tmp", "acc"))
        kt, zbuf, qv, xp, row_sum, mtm, gh, gl, w3f, wo3 = (
            shared[n] for n in ("kt", "zbuf", "qv", "xp", "row_sum", "mtm", "gh", "gl", "w3f", "wo3"))
        zin, xin3, fin, stack = (shared[n] for n in ("zin", "xin3", "fin", "stack"))

        tile = [ctx.enter_context(nc.psum_tensor(f"tile{k}", [P, N], F32)) for k in range(SLOTS)]
        pv = ctx.enter_context(nc.psum_tensor("pv", [P, N], F32))

        names = ["bq0", "bk0", "bv0", "bo0", "gnw", "gnb", "bq1", "bk1", "bv1", "bo1", "bq2", "bk2",
                 "bv2", "bo2", "b3", "bnw", "bnb", "bvo1", "bvo2", "scale", "shift", "bnscale", "bnshift"]

        def col(name, ct=None):
            k = 2 * names.index(name)
            return cols[:, k:k + 2] if ct is None else cols[:, k + ct:k + ct + 1]

        maxima = small[:, 0:G * NT]
        negmax = small[:, 32:32 + G * NMAX].rearrange("p (h s t) -> p h s t", h=G, s=2)
        stats = small[:, 96:120].rearrange("p (t k s) -> p t k s", t=CT, k=2)
        mv = small[:, 120:124].rearrange("p (t s) -> p t s", t=CT)
        mh = sb("mh", [P, G, NT], F32R)
        pairs = sb("pairs", [P, 48])
        (gmean, gdev, gsq, gvar, veps, vln, y0, y1, y2, inv_std, mscale) = (
            pairs[:, 2 * k:2 * k + 2] for k in range(11))
        kbar, larger, mix_sum, mix_rec, mix_pi = (pairs[:, 22 + 2 * k:24 + 2 * k] for k in range(5))
        logits, mix_e, logits_in = pairs[:, 32:36], pairs[:, 36:40], pairs[:, 40:44]
        win = sb("win", [P, NT * C // WIN])
        win_r = sb("win_r", [P, NT * C // WIN])

        weights_in = sem("weights_in"); vectors_in = sem("vectors_in"); consts_made = sem("consts_made")
        setup_tensor = sem("setup_tensor"); setup_scalar = sem("setup_scalar"); setup_vector = sem("setup_vector")
        tensor_done = sem("tensor_done"); scalar_done = sem("scalar_done")
        vector_done = sem("vector_done"); pool_done = sem("pool_done")
        w3_kept = sem("w3_kept"); w3_back = sem("w3_back")
        x_loaded = sem("x_loaded"); act_loaded = sem("act_loaded")
        stacked = [[sem(f"stacked{g}{h}") for h in range(G)] for g in range(NG)]
        key_ones_in = sem("key_ones_in")
        x3_stored = sem("x3_stored"); z_stored = sem("z_stored")
        bn_in = [sem("bn_in0"), sem("bn_in1")]; bn_steps = sem("bn_steps"); bn_scaled = sem("bn_scaled")
        bn_added = sem("bn_added"); stored = [sem("stored0"), sem("stored1")]
        NVEC = 3 * G + 14 + G + 2
        U = CT * C

        ctx.enter_context(nc.allow_non_contiguous_dma(reason="vectors of a few hundred elements"))
        block = ctx.enter_context(nc.Block())

        @block.sync
        def _(sp):
            sp.dma_start(stage[:, 0:3 * U].rearrange("p (t n) -> p t n", t=CT),
                         L0_w_proj.rearrange("(t p) n -> p t n", p=P)).then_inc(weights_in, 16)
            for k, w in enumerate((L0_w_out, L1_wq, L1_wk, L1_wo, L2_f_w, L2_g_w, L2_o_w, L3_w_qk,
                                   L3_w_v, L3_w_out, L1_wv, L2_h_w)):
                sp.dma_start(stage[:, (3 + k) * U:(4 + k) * U].rearrange("p (t n) -> p t n", t=CT),
                             w.rearrange("(t p) n -> p t n", p=P)).then_inc(weights_in, 16)
            sp.dma_start(x_in[:], x_v[0]).then_inc(x_loaded, 16)
            hb = L0_b_proj.rearrange("(t h s d) -> s h d t", t=CT, h=G, s=3)
            for s, name in enumerate(("bq0", "bk0", "bv0")):
                for h in range(G):
                    sp.dma_start(col(name)[D * h:D * h + D, :], hb[s, h]).then_inc(vectors_in, 16)
            for name, v in (("bo0", L0_b_out), ("gnw", L1_gn_w), ("gnb", L1_gn_b), ("bq1", L1_bq),
                            ("bk1", L1_bk), ("bv1", L1_bv), ("bo1", L1_bo), ("bq2", L2_f_b), ("bk2", L2_g_b),
                            ("bv2", L2_h_b), ("bo2", L2_o_b), ("b3", L3_b_qk), ("bnw", L3_bn_w), ("bnb", L3_bn_b)):
                sp.dma_start(col(name), v.rearrange("(t p) -> p t", p=P)).then_inc(vectors_in, 16)
            for h in range(G):
                sp.dma_start(mixcol[D * h:D * h + D, :], L3_mix.rearrange("m d -> d m")).then_inc(vectors_in, 16)
            for k, v in enumerate((L3_b_qk, L3_b_v)):
                sp.dma_start(b3row[:, k * C:(k + 1) * C],
                             v.rearrange("(a n) -> a n", a=1).broadcast_to((P, C))).then_inc(vectors_in, 16)

            sp.wait_ge(setup_scalar, 19)
            sp.dma_start(w3f_dram, w3f[:]).then_inc(w3_kept, 16)
            sp.dma_start(wo3_dram, wo3[:]).then_inc(w3_kept, 16)
            sp.wait_ge(w3_kept, 32)

            def batch(b, last):
                for g in range(NG):
                    sp.wait_ge(vector_done, vector.at(b, "qk0_lo", 1, g))
                    parts = qk_r[:].rearrange("p t s c n -> p (t s) c n")
                    for h in range(G):
                        for k, pair in enumerate((slice(0, 4, 2), slice(0, 4, 3), slice(1, 3))):
                            sp.dma_start(stack[D * k:D * k + D, :, g, h, :].bitcast(F32),
                                         parts[D * h:D * h + D, pair, g, :].bitcast(F32)
                                         ).then_inc(stacked[g][h], 16)
                sp.dma_start(stack[IMAX:K0, 1].rearrange("p g h (a n) -> p (g h a) n", n=P).bitcast(F32),
                             ones[0:NMAX, :].rearrange("p (a n) -> p a n", a=1)
                             .broadcast_to((NMAX, NG * G * N // P, P))).then_inc(key_ones_in, 16)
                sp.dma_start(act[:], x_v[b]).then_inc(act_loaded, 16)
                sp.wait_ge(tensor_done, tensor.at(b, "pv0", 1, NT - 1))
                sp.dma_start(w3f[:], w3f_dram).then_inc(w3_back, 16)
                sp.dma_start(wo3[:], wo3_dram).then_inc(w3_back, 16)
                sp.dma_start(x_in[:], x_v[0 if last else b + 1]).then_inc(x_loaded, 16)
                sp.wait_ge(vector_done, vector.at(b, "x", 2, 1, 1))
                sp.dma_start(x3_dram[b], act[:]).then_inc(x3_stored, 16)
                sp.wait_ge(scalar_done, scalar.at(b, "z_kept", CT - 1))
                sp.dma_start(z_dram[b], zbuf[:]).then_inc(z_stored, 16)

            with sp.Fori(0, B - 1) as b:
                batch(b, False)
            batch(B - 1, True)

            sp.wait_ge(x3_stored, 16 * B)
            sp.wait_ge(z_stored, 16 * B)
            sp.wait_ge(tensor_done, tensor.at(B - 1, "z", CT - 1))
            sp.wait_ge(vector_done, vector.at(B - 1, "z_stat", CT - 1, 1))
            for b in range(B):
                if b >= 2:
                    sp.wait_ge(bn_added, CT * (b - 1))
                sp.dma_start(zin[:, b % 2], z_dram[b]).then_inc(bn_in[b % 2], 16)
                sp.dma_start(xin3[:, b % 2], x3_dram[b]).then_inc(bn_in[b % 2], 16)
                if b >= 1:
                    sp.wait_ge(bn_added, CT * b)
                    sp.dma_start(out_v[b - 1], fin[:, (b - 1) % 2]).then_inc(stored[(b - 1) % 2], 16)
            sp.wait_ge(bn_added, CT * B)
            sp.dma_start(out_v[B - 1], fin[:, (B - 1) % 2]).then_inc(stored[(B - 1) % 2], 16)
            for s in stored:
                sp.wait_ge(s, 16 * B // 2)

        @block.gpsimd
        def _(pool):
            pe = nc.gpsimd
            made = 0

            def note(ins):
                nonlocal made
                made += 1
                ins.then_inc(consts_made, 1)
                pool.wait_ge(consts_made, made)

            note(pe.memset(ident[:], 0.0))
            note(pe.memset(ones[:], 1.0))
            note(pe.memset(gn_avg[:], 1.0 / 8))
            note(pe.memset(heads_mask[:], 1.0))
            note(pe.memset(raw[:], 0.0))
            note(pe.memset(pool_w[:], 1.0 / 9))
            note(pe.memset(pool_w[:, 0, :], 1.0 / 6))
            note(pe.memset(pool_w[:, :, 0], 1.0 / 6))
            note(pe.memset(pool_w[:, 0, 0:1], 1.0 / 4))
            note(pe.affine_select(out=ident[:], in_=ident[:], compare_op=ALU.not_equal, fill=1.0, base=0,
                                  pattern=[[-1, P]], channel_multiplier=1))
            for m, w in ((gn_avg, 8), (heads_mask, D)):
                v = m[:].rearrange("p (a w) -> p a w", w=w)
                note(pe.affine_select(out=v, in_=v, compare_op=ALU.is_ge, fill=0.0, base=0,
                                      pattern=[[-w, P // w], [0, w]], channel_multiplier=1))
                note(pe.affine_select(out=v, in_=v, compare_op=ALU.is_ge, fill=0.0, base=w - 1,
                                      pattern=[[w, P // w], [0, w]], channel_multiplier=-1))
            note(pe.memset(segment[:], 0.0))
            note(pe.memset(segment[:, D - SEG:D], 1.0))
            pe.memset(win_r[:, 0:1], 1.0).then_inc(pool_done, gps.count)

            with pool.Fori(0, B) as b:
                gps.start()
                for g in range(NG):
                    for jt in range(1, NT - 1):
                        for h in range(G):
                            if adder(g, jt, h) != "pool":
                                continue
                            pool.wait_ge(scalar_done, scalar.at(b, "exp0", g, jt, h))
                            if g == 1 and jt == 1:
                                pool.wait_ge(tensor_done, tensor.at(b, "den0", 0))
                            if jt > 1:
                                if adder(g, jt - 1, h) == "pool":
                                    pool.wait_ge(pool_done, gps.at(b, "add0", g, jt - 1, h))
                                else:
                                    pool.wait_ge(vector_done, vector.at(b, "add0", g, jt - 1, h))
                            first = p0[:, 0, h, :] if jt == 1 else acc0[:, h, :]
                            pe.tensor_tensor(acc0[:, h, :], first, p0[:, jt % 2, h, :], ALU.add
                                             ).then_inc(pool_done, gps.one("add0", g, jt, h))
                a5 = act[:].rearrange("p t (y c s) -> p t y c s", y=2 * POOLED, s=2)
                r5 = row_sum[:].rearrange("p t (y s) c -> p t y s c", s=2)
                x4 = xp[:].rearrange("p t (y c) -> p t y c", y=POOLED)
                pool.wait_ge(vector_done, vector.at(b, "x", 2, 1, 1))
                for k in range(5):
                    if k:
                        pool.wait_ge(pool_done, gps.at(b, "pool", k - 1, CT - 1))
                    for ct in range(CT):
                        o, i0, i1, op = (
                            (row_sum[:, ct], a5[:, ct, :, :, 0], a5[:, ct, :, :, 1], ALU.add),
                            (row_sum[:, ct, :, 1:], row_sum[:, ct, :, 1:], a5[:, ct, :, 0:POOLED - 1, 1], ALU.add),
                            (x4[:, ct], r5[:, ct, :, 0, :], r5[:, ct, :, 1, :], ALU.add),
                            (x4[:, ct, 1:], x4[:, ct, 1:], r5[:, ct, 0:POOLED - 1, 1, :], ALU.add),
                            (x4[:, ct], x4[:, ct], pool_w[:], ALU.mult),
                        )[k]
                        pe.tensor_tensor(o, i0, i1, op).then_inc(pool_done, gps.one("pool", k, ct))
                assert not gps.todo

        @block.scalar
        def _(act_e):
            sc = nc.scalar
            ID = ACT.Identity

            def tile_wait(b, *name):
                act_e.wait_ge(tensor_done, tensor.at(b, *name))
                return tile[slot(*name)][:]

            act_e.wait_ge(weights_in, 16 * 13)
            w0 = stage[:, 0:3 * U].rearrange("p (t h s d) -> p t s h d", t=CT, h=HEADS, s=3)
            for ct in range(CT):
                for s in range(3):
                    sc.activation(w0h[:, ct, s, :].rearrange("p (h d) -> p h d", h=HEADS), w0[:, ct, s], ID
                                  ).then_inc(setup_scalar, 1)
            sc.activation(wo0h[:].rearrange("p t n -> p (t n)"), stage[:, 3 * U:4 * U], ID).then_inc(setup_scalar, 1)
            act_e.wait_ge(consts_made, 16)
            sc.activation(ones_r[:], ones[:], ID).then_inc(setup_scalar, 1)
            sc.activation(max_in[:], raw[:], ID).then_inc(setup_scalar, 1)
            flat = lambda w: w[:].rearrange("p t n -> p (t n)")
            for k, dst in enumerate((flat(wqk[1, "q", "h"]), flat(wqk[1, "k", "h"]), acc0[:, 0, 0:U],
                                     flat(wqk[2, "q", "h"]), flat(wqk[2, "k", "h"]), acc0[:, 1, 0:U],
                                     flat(w3h), None, flat(wo3))):
                act_e.wait_ge(setup_tensor, k + 1)
                src = tile[k % SLOTS][:, 0:U]
                src3 = src.rearrange("p (t n) -> p t n", t=CT)
                if k == 7:
                    sc.activation(w3f[:, :, C:], src3, ID).then_inc(setup_scalar, 1)
                else:
                    sc.activation(dst, src, ID).then_inc(setup_scalar, 1)
                if k == 6:
                    sc.activation(w3f[:, :, 0:C], src3, ID).then_inc(setup_scalar, 1)
            for k in range(2):
                act_e.wait_ge(setup_tensor, 10 + k)
                sc.activation(flat(wqk[1 + k, "v", "h"]), tile[k][:, 0:U], ID).then_inc(setup_scalar, 1)
            act_e.wait_ge(x_loaded, 16)
            act_e.wait_ge(setup_tensor, 12)
            for ct in range(CT):
                sc.activation(xh[:, ct, :], x_in[:, ct, :], ID).then_inc(setup_scalar, 1)
            sc.activation(pairs[:, 46:47], ones[:, 0:1], ID).then_inc(scalar_done, scalar.count)

            with act_e.Fori(0, B) as b:
                scalar.start()
                def qk0_hi(t, g):
                    sc.activation(qk_r[:, t, 0, g, :], tile_wait(b, "qk0", t, g), ID, bias=col(("bq0", "bk0")[t], g)
                                  ).then_inc(scalar_done, scalar.one("qk0_hi", t, g))

                for g in range(NG):
                    for t in range(2):
                        if g == 0 and t == 1:
                            act_e.wait_ge(z_stored, 16 * b)
                            act_e.wait_ge(x3_stored, 16 * b)
                            act_e.wait_ge(pool_done, gps.before(b, "pool", 4, CT - 1))
                        qk0_hi(t, g)
                act_e.wait_ge(vector_done, vector.before(b, "x_lo", 1))
                for k in range(2):
                    sc.activation(v0[:, 4 * k:4 * k + 4, :].rearrange("p t n -> p (t n)"), tile_wait(b, "v0", k), ID
                                  ).then_inc(scalar_done, scalar.one("v0_kept", k))

                def summed(g, jt, h):
                    if jt == NT - 1:
                        act_e.wait_ge(tensor_done, tensor.at(b, "den0", g))
                    elif adder(g, max(jt, 1), h) == "pool":
                        act_e.wait_ge(pool_done, gps.at(b, "add0", g, max(jt, 1), h))
                    else:
                        act_e.wait_ge(vector_done, vector.at(b, "add0", g, max(jt, 1), h))

                def exp0(g, jt, h):
                    if jt >= 2:
                        act_e.wait_ge(tensor_done, tensor.at(b, "pv0", g, jt - 2))
                        summed(g, jt - 2, h)
                    elif g == 1:
                        act_e.wait_ge(tensor_done, tensor.at(b, "pv0", 0, NT - 2 + jt))
                        summed(0, NT - 2 + jt, h)
                    sc.activation(p0[:, jt % 2, h, :], tile_wait(b, "st0", g, jt, h), ACT.Exp, scale=float(D) ** -0.5
                                  ).then_inc(scalar_done, scalar.one("exp0", g, jt, h))

                def res_hi(g):
                    for k in range(2):
                        act_e.wait_ge(vector_done, vector.at(b, "res", g, k))
                        s = slice(k * HALF, (k + 1) * HALF)
                        sc.activation(side[:, 0, g, s], raw[:, s], ID, bias=col("bv0", g)
                                      ).then_inc(scalar_done, scalar.one("res_hi", g, k))

                for g in range(NG):
                    if g == 0:
                        for s in stacked[0] + stacked[1]:
                            act_e.wait_ge(s, 48 * b + 48)
                    for jt in range(NT):
                        if g == 1 and jt == 5:
                            res_hi(0)
                        for h in range(G):
                            exp0(g, jt, h)
                    act_e.wait_ge(tensor_done, tensor.at(b, "pv0", g, NT - 1))
                    if g == 1:
                        act_e.wait_ge(vector_done, vector.at(b, "res_lo", 0, 1))
                    sc.activation(raw[:], pv[:], ID).then_inc(scalar_done, scalar.one("pv0_out", g))
                res_hi(1)

                for layer in (1, 2):
                    act_e.wait_ge(vector_done, vector.at(b, "var", layer))
                    sc.activation(vln, veps, ACT.Ln).then_inc(scalar_done, scalar.one("ln", layer))
                    act_e.wait_ge(scalar_done, scalar.at(b, "ln", layer))
                    sc.activation(y0, vln, ACT.Exp, scale=-0.5).then_inc(scalar_done, scalar.one("inv_std", layer))
                    act_e.wait_ge(vector_done, vector.at(b, "shift", layer))
                    for k in range(2):
                        for ct in range(CT):
                            s = slice(k * HALF, (k + 1) * HALF)
                            sc.activation(xh[:, ct, s], act[:, ct, s], ID, bias=col("shift", ct), scale=col("scale", ct)
                                          ).then_inc(scalar_done, scalar.one("norm_hi", layer, k, ct))
                    for t in range(2):
                        for ct in range(CT):
                            sc.activation(qk_r[:, t, 0, ct, :], tile_wait(b, "qk", layer, t, ct), ID,
                                          bias=col(f"b{'qk'[t]}{layer}", ct)
                                          ).then_inc(scalar_done, scalar.one("qk_hi", layer, t, ct))

                    def v_hi(l, k):
                        sc.activation(vh[:, 4 * k:4 * k + 4, :].rearrange("p t n -> p (t n)"),
                                      tile_wait(b, "v", l, k), ID).then_inc(scalar_done, scalar.one("v_hi", l, k))

                    def feat_hi(k):
                        dst = side[:, 0] if layer == 1 else xh
                        for ct in range(CT):
                            act_e.wait_ge(vector_done, vector.at(b, "x", layer, k, ct))
                            s = slice(k * HALF, (k + 1) * HALF)
                            sc.activation(dst[:, ct, s], act[:, ct, s], ID
                                          ).then_inc(scalar_done, scalar.one("feat_hi", layer + 1, k, ct))

                    if layer == 1:
                        v_hi(1, 0)
                    v_hi(layer, 1)

                    def pv_out(half):
                        act_e.wait_ge(tensor_done, tensor.at(b, "pv", layer, 4 * half + 3))
                        if half:
                            act_e.wait_ge(vector_done, vector.at(b, "x", layer, 0, 1))
                        sc.activation(raw[:], pv[:], ID).then_inc(scalar_done, scalar.one("pv_out", layer, half))

                    scale = float(C) ** -0.5 if layer == 1 else 1.0
                    for n in range(NT):
                        if n >= 2:
                            act_e.wait_ge(tensor_done, tensor.at(b, "pv", layer, n - 2))
                            act_e.wait_ge(vector_done, vector.at(b, "exp_lo", layer, n - 2))
                            act_e.wait_ge(vector_done, vector.at(b, "add", layer, n - 2 + (n % 4 == 2)))
                        if n == NT - 1:
                            feat_hi(0)
                        scores = tile_wait(b, "st", layer, n)
                        for name in ("exp_hi", "exp") if n < NT - 1 else ("exp", "exp_hi"):
                            dst = ph if name == "exp_hi" else p12
                            sc.activation(dst[:, n % 2, :], scores, ACT.Exp, scale=scale
                                          ).then_inc(scalar_done, scalar.one(name, layer, n))
                        if n == NT // 2:
                            pv_out(0)
                    pv_out(1)
                    if layer == 1:
                        v_hi(2, 0)
                    feat_hi(1)

                for k in range(2):
                    act_e.wait_ge(vector_done, vector.at(b, "kt_sub", k))
                    v = kt[:, 4 * k:4 * k + 4, :].rearrange("p t n -> p (t n)")
                    sc.activation(v, v, ACT.Exp).then_inc(scalar_done, scalar.one("kt_exp", k))
                act_e.wait_ge(x_loaded, 16 * b + 32)
                for ct in range(CT):
                    sc.activation(xh[:, ct, :], x_in[:, ct, :], ID).then_inc(scalar_done, scalar.one("x_hi", ct))
                act_e.wait_ge(vector_done, vector.at(b, "mix", 3))
                sc.activation(mix_e, logits, ACT.Exp).then_inc(scalar_done, scalar.one("mix_exp"))
                act_e.wait_ge(vector_done, vector.at(b, "mix_pi"))
                gt = tile_wait(b, "g")
                for ct in range(CT):
                    sc.activation(gh[:, ct, :], gt[:, ct * C:(ct + 1) * C], ID, scale=mix_pi[:, ct:ct + 1]
                                  ).then_inc(scalar_done, scalar.one("g_hi", ct))
                for ct in range(CT):
                    sc.activation(qk_r[:, 0, 0, ct, :], tile_wait(b, "smt", ct), ID
                                  ).then_inc(scalar_done, scalar.one("smt_hi", ct))
                for ct in range(CT):
                    sc.activation(zbuf[:, ct, :], tile_wait(b, "z", ct), ID
                                  ).then_inc(scalar_done, scalar.one("z_kept", ct))
                assert not scalar.todo

            act_e.wait_ge(bn_steps, 3)
            sc.activation(vln, veps, ACT.Ln).then_inc(bn_steps, 1)
            act_e.wait_ge(bn_steps, 4)
            sc.activation(y0, vln, ACT.Exp, scale=-0.5).then_inc(bn_steps, 1)
            act_e.wait_ge(bn_steps, 11)
            for b in range(B):
                act_e.wait_ge(bn_in[b % 2], 32 * (b // 2 + 1))
                for ct in range(CT):
                    sc.activation(zin[:, b % 2, ct, :], zin[:, b % 2, ct, :], ID, bias=col("bnshift", ct),
                                  scale=col("bnscale", ct)).then_inc(bn_scaled, 1)

        @block.vector
        def _(dve):
            ve = nc.vector
            TT, STT, TS = ve.tensor_tensor, ve.scalar_tensor_tensor, ve.tensor_scalar
            f = lambda ap: ap.bitcast(F32)
            flat = lambda w: w[:].rearrange("p t n -> p (t n)")

            dve.wait_ge(setup_scalar, 7)
            w0 = stage[:, 0:3 * U].rearrange("p (t h s d) -> p t s h d", t=CT, h=HEADS, s=3)
            for ct in range(CT):
                for s in range(3):
                    v = lambda w: w[:, ct, s, :].rearrange("p (h d) -> p h d", h=HEADS)
                    TT(v(w0l), w0[:, ct, s], f(v(w0h)), ALU.subtract).then_inc(setup_vector, 1)
            TT(flat(wo0l), stage[:, 3 * U:4 * U], f(flat(wo0h)), ALU.subtract).then_inc(setup_vector, 1)
            for k, hi, lo in ((0, wqk[1, "q", "h"], wqk[1, "q", "l"]), (1, wqk[1, "k", "h"], wqk[1, "k", "l"]),
                              (3, wqk[2, "q", "h"], wqk[2, "q", "l"]), (4, wqk[2, "k", "h"], wqk[2, "k", "l"]),
                              (6, w3h, w3l)):
                dve.wait_ge(setup_scalar, 10 + k + (k == 6))
                TT(flat(lo), tile[k % SLOTS][:, 0:U], f(flat(hi)), ALU.subtract).then_inc(setup_vector, 1)
            for k in range(2):
                dve.wait_ge(setup_scalar, 20 + k)
                TT(flat(wqk[1 + k, "v", "l"]), tile[k][:, 0:U], f(flat(wqk[1 + k, "v", "h"])), ALU.subtract
                   ).then_inc(setup_vector, 1)
            dve.wait_ge(setup_tensor, 12)
            dve.wait_ge(vectors_in, 16 * NVEC)
            for k in range(2):
                TT(col(f"bvo{k + 1}"), pv[:, 2 * k:2 * k + 2], col(f"bo{k + 1}"), ALU.add).then_inc(setup_vector, 1)
            for m in range(2):
                for dst, src in ((mix_own, m), (mix_other, 1 - m)):
                    v = lambda w: w[:].rearrange("p (h m e) -> p m h e", h=G, m=2)[:, m]
                    TS(v(dst), v(heads_mask), mixcol[:, src:src + 1], None, ALU.mult).then_inc(setup_vector, 1)
            first_rows = ident[:].rearrange("p (h t e) -> p h t e", h=G, e=SEG)[:, :, :, 0]
            TT(seg_own[:], first_rows[:, 0], first_rows[:, 1], ALU.add).then_inc(setup_vector, 1)
            for h in range(2, G):
                dve.wait_ge(setup_vector, 19 + h)
                TT(seg_own[:], seg_own[:], first_rows[:, h], ALU.add).then_inc(setup_vector, 1)
            TT(mask8[:], ident[0:NMAX, 0:NT], ident[0:NMAX, NT:NMAX], ALU.add).then_inc(setup_vector, 1)
            for ct in range(CT):
                dve.wait_ge(setup_scalar, 22 + ct)
                TT(xl[:, ct, :], x_in[:, ct, :], f(xh[:, ct, :]), ALU.subtract).then_inc(setup_vector, 1)
            ve.memset(pairs[:, 47:48], 1.0).then_inc(vector_done, vector.count)

            with dve.Fori(0, B) as b:
                vector.start()

                def own(*step):
                    dve.wait_ge(vector_done, vector.at(b, *step))

                def tile_wait(*name):
                    dve.wait_ge(tensor_done, tensor.at(b, *name))
                    return tile[slot(*name)]

                def scalar_wait(*step):
                    dve.wait_ge(scalar_done, scalar.at(b, *step))

                def qk0_lo(t, g):
                    scalar_wait("qk0_hi", t, g)
                    STT(qk_r[:, t, 1, g, :], tile[slot("qk0", t, g)][:], col(("bq0", "bk0")[t], g),
                        f(qk_r[:, t, 0, g, :]), ALU.add, ALU.subtract).then_inc(vector_done, vector.one("qk0_lo", t, g))

                def max0(g, h, it):
                    t = tile_wait("s0", g, h, it)
                    ve.tensor_reduce(maxima[:, h * NT + it:h * NT + it + 1], t[:], X, ALU.max
                                     ).then_inc(vector_done, vector.one("max0", g, h, it))

                def negate(key, heads, last):
                    own(*last)
                    m3 = maxima[:, 0:heads * NT].rearrange("p (h t) -> p h t", h=heads)
                    hi = mh[:, 0:heads, :]
                    TS(hi, m3, -1.0, None, ALU.mult).then_inc(vector_done, vector.one("neg_hi", *key))
                    own("neg_hi", *key)
                    ve.tensor_copy(negmax[:, 0:heads, 0, :], f(hi)).then_inc(vector_done, vector.one("neg_copy", *key))
                    STT(negmax[:, 0:heads, 1, :], m3, -1.0, f(hi), ALU.mult, ALU.subtract
                        ).then_inc(vector_done, vector.one("neg_lo", *key))

                def spread(dst, src):
                    return TT(dst.rearrange("p (t n) -> p t n", t=NT),
                              src.rearrange("p (a n) -> p a n", a=1).broadcast_to((NMAX, NT, P)),
                              mask8[:].rearrange("p (t a) -> p t a", a=1).broadcast_to((NMAX, NT, P)), ALU.mult)

                def add0(g, jt, h):
                    scalar_wait("exp0", g, jt, h)
                    if g == 1 and jt == 1:
                        dve.wait_ge(tensor_done, tensor.at(b, "den0", 0))
                    if jt > 1:
                        if adder(g, jt - 1, h) == "vector":
                            own("add0", g, jt - 1, h)
                        else:
                            dve.wait_ge(pool_done, gps.at(b, "add0", g, jt - 1, h))
                    first = p0[:, 0, h, :] if jt == 1 else acc0[:, h, :]
                    TT(acc0[:, h, :], first, p0[:, jt % 2, h, :], ALU.add).then_inc(vector_done, vector.one("add0", g, jt, h))

                def inverse0(g):
                    den = tile_wait("den0", g)
                    ve.reciprocal(rec0[:], den[:, 0:P]).then_inc(vector_done, vector.one("rec0", g))

                def inverse_rows(g):
                    own("rec0", g)
                    for k in range(2):
                        t = slice(k * NT // 2, (k + 1) * NT // 2)
                        TT(rows0[:, t, :], rec0[:].rearrange("p (a n) -> p a n", a=1).broadcast_to((P, NT // 2, P)),
                           seg_own[:, t].rearrange("p (t a) -> p t a", a=1).broadcast_to((P, NT // 2, P)), ALU.mult
                           ).then_inc(vector_done, vector.one("rows0", g, k))

                def normalise0(g):
                    scalar_wait("pv0_out", g)
                    for k, name in enumerate(("ex0", "ex0+")):
                        dve.wait_ge(tensor_done, tensor.at(b, name, g))
                        s = slice(k * HALF, (k + 1) * HALF)
                        TT(raw[:, s], raw[:, s], tile[slot("ex0", g)][:, s], ALU.mult
                           ).then_inc(vector_done, vector.one("res", g, k))

                def res_lo(g):
                    for k in range(2):
                        scalar_wait("res_hi", g, k)
                        s = slice(k * HALF, (k + 1) * HALF)
                        STT(side[:, 1, g, s], raw[:, s], col("bv0", g), f(side[:, 0, g, s]), ALU.add, ALU.subtract
                            ).then_inc(vector_done, vector.one("res_lo", g, k))

                for g in range(NG):
                    for t in range(2):
                        qk0_lo(t, g)
                for h in range(G):
                    for it in range(NT):
                        max0(0, h, it)
                for g in range(NG):
                    negate((g,), G, ("max0", g, G - 1, NT - 1))
                    t = tile_wait("m0", g)
                    for h in range(G):
                        spread(stack[IMAX:K0, 0, g, h, :], t[0:NMAX, h * P:(h + 1) * P]
                               ).then_inc(vector_done, vector.one("max_rows", g, h))
                    if g == 1:
                        inverse0(0)
                    for jt in range(NT):
                        mine = [h for h in range(G) if adder(g, jt, h) == "vector"]
                        if g == 0:
                            due = [h for h in range(G) if jt and adder(g, jt - 1, h) == "vector"]
                            for k in range(G):
                                max0(1, *divmod(G * jt + k, NT))
                                for h in due[k // 2:k // 2 + 1] if k % 2 == 0 else []:
                                    add0(g, jt - 1, h)
                        else:
                            for h in mine:
                                add0(g, jt, h)
                            if jt == 1:
                                inverse_rows(0)
                            elif jt == 2:
                                normalise0(0)
                            elif jt == 5:
                                res_lo(0)
                inverse0(1)
                inverse_rows(1)
                normalise0(1)
                res_lo(1)

                def statistics(layer, k):
                    for ct in range(CT):
                        ve.bn_stats(stats[:, ct, k, :], act[:, ct, k * HALF:(k + 1) * HALF]
                                    ).then_inc(vector_done, vector.one("stat", layer, k, ct))

                def aggregate(layer):
                    own("stat", layer, 1, CT - 1)
                    ve.memset(pairs[:, 45:46], 0.0)
                    for ct in range(CT):
                        ve.bn_aggr(mv[:, ct, :], stats[:, ct]).then_inc(vector_done, vector.one("mv", layer, ct))

                dve.wait_ge(act_loaded, 16 * b + 16)
                for k in range(2):
                    t = tile_wait("out0", k)
                    for ct in range(CT):
                        a = act[:, ct, k * HALF:(k + 1) * HALF]
                        STT(a, t[:, ct * HALF:(ct + 1) * HALF], col("bo0", ct), a, ALU.add, ALU.add
                            ).then_inc(vector_done, vector.one("x1", k, ct))
                    own("x1", k, CT - 1)
                    statistics(1, k)

                for layer in (1, 2):
                    aggregate(layer)

                    def v_lo(l, k):
                        scalar_wait("v_hi", l, k)
                        v = lambda w: w[:, 4 * k:4 * k + 4, :].rearrange("p t n -> p (t n)")
                        TT(v(vl), tile[slot("v", l, k)][:], f(v(vh)), ALU.subtract
                           ).then_inc(vector_done, vector.one("v_lo", l, k))

                    def feat_lo(l, k):
                        hi, lo = (side[:, 0], side[:, 1]) if l == 2 else (xh, xl)
                        for ct in range(CT):
                            scalar_wait("feat_hi", l, k, ct)
                            s = slice(k * HALF, (k + 1) * HALF)
                            TT(lo[:, ct, s], act[:, ct, s], f(hi[:, ct, s]), ALU.subtract
                               ).then_inc(vector_done, vector.one("feat_lo", l, k, ct))

                    own("mv", layer, 1)
                    if layer == 1:
                        t = tile_wait("gn", 0)
                        ve.tensor_copy(gmean, t[:, 0:2]).then_inc(vector_done, vector.one("gn", 0))
                        own("gn", 0)
                        TT(gdev, mv[:, :, 0], gmean, ALU.subtract).then_inc(vector_done, vector.one("gn", 1))
                        own("gn", 1)
                        TT(gsq, gdev, gdev, ALU.mult).then_inc(vector_done, vector.one("gn", 2))
                        own("gn", 2)
                        TT(gvar, gsq, mv[:, :, 1], ALU.add).then_inc(vector_done, vector.one("gn", 3))
                        t = tile_wait("gn", 1)
                        TS(veps, t[:, 0:2], 1e-6, None, ALU.add).then_inc(vector_done, vector.one("var", 1))
                        mean = gmean
                    else:
                        TS(veps, mv[:, :, 1], 1e-5, None, ALU.add).then_inc(vector_done, vector.one("var", 2))
                        mean = mv[:, :, 0]
                        feat_lo(2, 1)
                        v_lo(2, 0)
                    scalar_wait("inv_std", layer)
                    own("var", layer)
                    TT(y1, y0, y0, ALU.mult).then_inc(vector_done, vector.one("newton", layer, 0))
                    own("newton", layer, 0)
                    STT(y2, y1, -0.5, veps, ALU.mult, ALU.mult).then_inc(vector_done, vector.one("newton", layer, 1))
                    own("newton", layer, 1)
                    if layer == 1:
                        STT(inv_std, y2, 1.5, y0, ALU.add, ALU.mult).then_inc(vector_done, vector.one("newton", 1, 2))
                        own("newton", 1, 2)
                        TT(col("scale"), inv_std, col("gnw"), ALU.mult).then_inc(vector_done, vector.one("scale", 1))
                        own("scale", 1)
                        TT(mscale, mean, col("scale"), ALU.mult).then_inc(vector_done, vector.one("offset", 1))
                        own("offset", 1)
                        TT(col("shift"), col("gnb"), mscale, ALU.subtract).then_inc(vector_done, vector.one("shift", 1))
                    else:
                        STT(col("scale"), y2, 1.5, y0, ALU.add, ALU.mult).then_inc(vector_done, vector.one("newton", 2, 2))
                        own("newton", 2, 2)
                        STT(col("shift"), mean, -1.0, col("scale"), ALU.mult, ALU.mult
                            ).then_inc(vector_done, vector.one("shift", 2))
                    own("shift", layer)
                    for k in range(2):
                        s = slice(k * HALF, (k + 1) * HALF)
                        for ct in range(CT):
                            if k:
                                own("norm_lo", layer, 0, ct)
                            TS(tmp[:, ct * HALF:(ct + 1) * HALF], act[:, ct, s], col("scale", ct), col("shift", ct),
                               ALU.mult, ALU.add).then_inc(vector_done, vector.one("norm", layer, k, ct))
                        for ct in range(CT):
                            own("norm", layer, k, ct)
                            scalar_wait("norm_hi", layer, k, ct)
                            TT(xl[:, ct, s], tmp[:, ct * HALF:(ct + 1) * HALF], f(xh[:, ct, s]), ALU.subtract
                               ).then_inc(vector_done, vector.one("norm_lo", layer, k, ct))
                    for t in range(2):
                        for ct in range(CT):
                            scalar_wait("qk_hi", layer, t, ct)
                            STT(qk_r[:, t, 1, ct, :], tile[slot("qk", layer, t, ct)][:], col(f"b{'qk'[t]}{layer}", ct),
                                f(qk_r[:, t, 0, ct, :]), ALU.add, ALU.subtract
                                ).then_inc(vector_done, vector.one("qk_lo", layer, t, ct))
                    if layer == 1:
                        v_lo(1, 0)
                    for it in range(NT):
                        if it == 4:
                            v_lo(layer, 1)
                        t = tile_wait("s", layer, it)
                        ve.tensor_reduce(maxima[:, it:it + 1], t[:], X, ALU.max
                                         ).then_inc(vector_done, vector.one("max", layer, it))
                    negate((layer, 0), 1, ("max", layer, NT - 1))
                    t = tile_wait("m", layer)
                    spread(max_in[0:NMAX, :], t[0:NMAX, 0:P]).then_inc(vector_done, vector.one("max_in", layer))

                    def reciprocal(half):
                        den = tile_wait("den", layer, half)
                        ve.reciprocal(den[:, 0:HALF], den[:, 0:HALF]).then_inc(vector_done, vector.one("rec", layer, half))

                    def finish(half):
                        own("rec", layer, half)
                        scalar_wait("pv_out", layer, half)
                        r3 = raw[:].rearrange("p (t n) -> p t n", t=CT)
                        TT(r3, r3, tile[slot("den", layer, half)][:, 0:HALF].rearrange("p (a n) -> p a n", a=1).broadcast_to((P, CT, HALF)),
                           ALU.mult).then_inc(vector_done, vector.one("out", layer, half))
                        own("out", layer, half)
                        for ct in range(CT):
                            a = act[:, ct, half * HALF:(half + 1) * HALF]
                            STT(a, r3[:, ct, :], col(f"bvo{layer}", ct), a, ALU.add, ALU.add
                                ).then_inc(vector_done, vector.one("x", layer, half, ct))

                    def exp_lo(n):
                        scalar_wait("exp" if n < NT - 1 else "exp_hi", layer, n)
                        TT(pl[:, n % 2, :], p12[:, n % 2, :], f(ph[:, n % 2, :]), ALU.subtract
                           ).then_inc(vector_done, vector.one("exp_lo", layer, n))

                    def add(n):
                        if n % 4 > 1:
                            own("add", layer, n - 1)
                        elif n == 5:
                            dve.wait_ge(tensor_done, tensor.at(b, "den", layer, 0))
                        first = p12[:, 0, :] if n % 4 == 1 else acc[:]
                        scalar_wait("exp", layer, n)
                        TT(acc[:], first, p12[:, n % 2, :], ALU.add).then_inc(vector_done, vector.one("add", layer, n))

                    for n in range(NT - 1):
                        if n == 5:
                            reciprocal(0)
                        if n == 6:
                            finish(0)
                        exp_lo(n)
                        if n % 4:
                            add(n)
                    own("x", layer, 0, 1)
                    statistics(layer + 1, 0)
                    feat_lo(layer + 1, 0)
                    add(NT - 1)
                    exp_lo(NT - 1)
                    reciprocal(1)
                    finish(1)
                    own("x", layer, 1, 1)
                    if layer == 1:
                        statistics(2, 1)

                feat_lo(3, 1)
                kw = kt[:].rearrange("p t (w e) -> p (t w) e", e=WIN)
                W4 = NT * C // WIN // 2

                def wide(ap):
                    return ap.rearrange("p (w a) -> p w a", a=1).broadcast_to((P, W4, WIN))

                for k in range(2):
                    t = tile_wait("kt", k)
                    TT(kt[:, 4 * k:4 * k + 4, :], t[:].rearrange("p (t n) -> p t n", t=4),
                       b3row[:, 0:C].rearrange("p (a n) -> p a n", a=1).broadcast_to((P, 4, C)), ALU.add
                       ).then_inc(vector_done, vector.one("kt_in", k))
                    own("kt_in", k)
                    w, wm = kw[:, k * W4:(k + 1) * W4, :], win[:, k * W4:(k + 1) * W4]
                    ve.tensor_reduce(wm, w, X, ALU.max).then_inc(vector_done, vector.one("win_max", k))
                    own("win_max", k)
                    TT(w, w, wide(wm), ALU.subtract).then_inc(vector_done, vector.one("kt_sub", k))
                    if k == 0:
                        statistics(3, 1)
                        aggregate(3)
                t = tile_wait("qv")
                TT(qv[:], t[:].rearrange("p (t n) -> p t n", t=2),
                   b3row[:].rearrange("p (a n) -> p a n", a=1).broadcast_to((P, 2, 2 * C)), ALU.add
                   ).then_inc(vector_done, vector.one("qv_in"))

                def windows(k):
                    w, ws = kw[:, k * W4:(k + 1) * W4, :], win[:, k * W4:(k + 1) * W4]
                    wr = win_r[:, k * W4:(k + 1) * W4]
                    scalar_wait("kt_exp", k)
                    ve.tensor_reduce(ws, w, X, ALU.add).then_inc(vector_done, vector.one("win_sum", k))
                    own("win_sum", k)
                    ve.reciprocal(wr, ws).then_inc(vector_done, vector.one("win_rec", k))
                    own("win_rec", k)
                    TT(w, w, wide(wr), ALU.mult).then_inc(vector_done, vector.one("sm", k))

                windows(0)
                t = tile_wait("mt")
                TT(mtm[:], t[:, 0:CT * P].rearrange("p (t n) -> p t n", t=CT),
                   heads_mask[:].rearrange("p (a n) -> p a n", a=1).broadcast_to((P, CT, P)), ALU.mult
                   ).then_inc(vector_done, vector.one("mt_in"))
                TT(kbar, t[:, HALF:HALF + CT], col("b3"), ALU.add).then_inc(vector_done, vector.one("kbar"))
                windows(1)
                t = tile_wait("g")
                ve.tensor_copy(logits_in, t[:, HALF:HALF + 4]).then_inc(vector_done, vector.one("mix", 0))
                own("mix", 0)
                TT(larger, logits_in[:, 0:2], logits_in[:, 2:4], ALU.max).then_inc(vector_done, vector.one("mix", 1))
                own("mix", 1)
                TT(logits[:, 0:2], logits_in[:, 0:2], larger, ALU.subtract).then_inc(vector_done, vector.one("mix", 2))
                TT(logits[:, 2:4], logits_in[:, 2:4], larger, ALU.subtract).then_inc(vector_done, vector.one("mix", 3))
                scalar_wait("mix_exp")
                TT(mix_sum, mix_e[:, 0:2], mix_e[:, 2:4], ALU.add).then_inc(vector_done, vector.one("mix_sum"))
                own("mix_sum")
                ve.reciprocal(mix_rec, mix_sum).then_inc(vector_done, vector.one("mix_rec"))
                own("mix_rec")
                STT(mix_pi, mix_e[:, 0:2], float(D) ** -0.5, mix_rec, ALU.mult, ALU.mult
                    ).then_inc(vector_done, vector.one("mix_pi"))
                own("mix_pi")
                for ct in range(CT):
                    scalar_wait("g_hi", CT - 1)
                    STT(gl[:, ct, :], t[:, ct * C:(ct + 1) * C], mix_pi[:, ct:ct + 1], f(gh[:, ct, :]),
                        ALU.mult, ALU.subtract).then_inc(vector_done, vector.one("g_lo", ct))
                for ct in range(CT):
                    scalar_wait("smt_hi", ct)
                    TT(qk_r[:, 0, 1, ct, :], tile[slot("smt", ct)][:], f(qk_r[:, 0, 0, ct, :]), ALU.subtract
                       ).then_inc(vector_done, vector.one("smt_lo", ct))
                for ct in range(CT):
                    scalar_wait("x_hi", ct)
                    TT(xl[:, ct, :], x_in[:, ct, :], f(xh[:, ct, :]), ALU.subtract
                       ).then_inc(vector_done, vector.one("x_lo", ct))
                for ct in range(CT):
                    scalar_wait("z_kept", ct)
                    for k in range(2):
                        ve.bn_stats(bn_rows[:, ct, bass.ds(2 * b + k, 1), :], zbuf[:, ct, k * HALF:(k + 1) * HALF]
                                    ).then_inc(vector_done, vector.one("z_stat", ct, k))
                assert not vector.todo

            chain = 0

            def link(ins):
                nonlocal chain
                chain += 1
                ins.then_inc(bn_steps, 1)
                dve.wait_ge(bn_steps, chain)

            dve.wait_ge(vector_done, vector.at(B - 1, "z_stat", CT - 1, 1))
            for ct in range(CT):
                link(ve.bn_aggr(mv[:, ct, :], bn_rows[:, ct]))
            link(TS(veps, mv[:, :, 1], 1e-5, None, ALU.add))
            chain += 2
            dve.wait_ge(bn_steps, chain)
            link(TT(y1, y0, y0, ALU.mult))
            link(STT(y2, y1, -0.5, veps, ALU.mult, ALU.mult))
            link(STT(inv_std, y2, 1.5, y0, ALU.add, ALU.mult))
            link(TT(col("bnscale"), inv_std, col("bnw"), ALU.mult))
            link(TT(mscale, mv[:, :, 0], col("bnscale"), ALU.mult))
            link(TT(col("bnshift"), col("bnb"), mscale, ALU.subtract))
            for b in range(B):
                for ct in range(CT):
                    dve.wait_ge(bn_scaled, CT * b + ct + 1)
                    if b >= 2:
                        dve.wait_ge(stored[b % 2], 16 * (b // 2))
                    TT(fin[:, b % 2, ct, :], zin[:, b % 2, ct, :], xin3[:, b % 2, ct, :], ALU.add).then_inc(bn_added, 1)

        @block.tensor
        def _(pe):
            mm = nc.tensor.matmul
            halves = [slice(0, HALF), slice(HALF, N)]

            def three(out, lhs, rhs, first=True, last=True, low=None):
                n = len(lhs[0])
                for m, (a, c) in enumerate(((0, 0), (1, 0), (0, 1))):
                    if c and low:
                        low()
                    for kt_ in range(n):
                        ins = mm(out, lhs[a][kt_], rhs[c][kt_], start=first and kt_ == 0 and m == 0,
                                 stop=last and kt_ == n - 1 and m == 2)
                return ins

            pe.wait_ge(weights_in, 16 * 13)
            pe.wait_ge(consts_made, 16)
            for k in range(9):
                if k >= SLOTS:
                    pe.wait_ge(setup_scalar, 10 + k - SLOTS)
                    pe.wait_ge(setup_vector, (8, 9, 9, 10, 11, 11)[k - SLOTS])
                w = stage[:, (4 + k) * U:(5 + k) * U].rearrange("p (t n) -> p t n", t=CT)
                for ct in range(CT):
                    for ot in range(CT):
                        ins = nc.tensor.transpose(tile[k % SLOTS][:, ct * C + ot * P:ct * C + (ot + 1) * P],
                                                  w[:, ot, ct * P:(ct + 1) * P], ident[:])
                ins.then_inc(setup_tensor, 1)
            pe.wait_ge(setup_scalar, 19)
            pe.wait_ge(setup_vector, 12)
            pe.wait_ge(vectors_in, 16 * NVEC)
            for k in range(2):
                wv = stage[:, (13 + k) * U:(14 + k) * U].rearrange("p (t n) -> p t n", t=CT)
                wo = acc0[:, k, 0:U].rearrange("p (t n) -> p t n", t=CT)
                for ct in range(CT):
                    for et in range(CT):
                        ins = mm(tile[k][:, ct * C:(ct + 1) * C], wv[:, et, ct * P:(ct + 1) * P], wo[:, et, :],
                                 start=et == 0, stop=et == CT - 1)
                ins.then_inc(setup_tensor, 1)
            for k in range(2):
                wo = acc0[:, k, 0:U].rearrange("p (t n) -> p t n", t=CT)
                for ot in range(CT):
                    for et in range(CT):
                        ins = mm(pv[:, 2 * k + ot:2 * k + ot + 1], wo[:, et, ot * P:(ot + 1) * P],
                                 col(f"bv{k + 1}", et), start=et == 0, stop=et == CT - 1)
            ins.then_inc(setup_tensor, 1)
            pe.wait_ge(scalar_done, scalar.count)
            pe.wait_ge(vector_done, vector.count)
            mm(tile[0][:, 0:P], ones[:], ident[:], start=True, stop=True).then_inc(tensor_done, tensor.count)

            with pe.Fori(0, B) as b:
                tensor.start()

                def scalar_wait(*step):
                    pe.wait_ge(scalar_done, scalar.at(b, *step))

                def vector_wait(*step):
                    pe.wait_ge(vector_done, vector.at(b, *step))

                def free(*name):
                    engine, count = leaver(b, *name)
                    pe.wait_ge(scalar_done if engine == "scalar" else vector_done, count)
                    return tile[slot(*name)]

                kts = range(CT)

                def qk0(t, g):
                    o = free("qk0", t, g)
                    for s in halves:
                        ins = three(o[:, s], [[w[:, kt_, t, g * P:(g + 1) * P] for kt_ in kts] for w in (w0h, w0l)],
                                    [[v[:, kt_, s] for kt_ in kts] for v in (xh, xl)])
                    ins.then_inc(tensor_done, tensor.one("qk0", t, g))

                def s0(g, h, it):
                    if it == 0:
                        pe.wait_ge(stacked[g][h], 48 * b + 48)
                    o = free("s0", g, h, it)
                    for s in halves:
                        ins = mm(o[:, s], stack[0:IMAX, 0, g, h, it * P:(it + 1) * P], stack[0:IMAX, 1, g, h, s],
                                 start=True, stop=True)
                    ins.then_inc(tensor_done, tensor.one("s0", g, h, it))

                def m0(g):
                    vector_wait("neg_lo", g)
                    o = free("m0", g)
                    for h in range(G):
                        ins = nc.tensor.transpose(o[0:NMAX, h * P:(h + 1) * P],
                                                  negmax[:, h].rearrange("p s t -> p (s t)"), ident[:])
                    ins.then_inc(tensor_done, tensor.one("m0", g))

                def st0(g, jt, h):
                    if jt == 0:
                        vector_wait("max_rows", g, h)
                        if g == 0 and h == 0:
                            pe.wait_ge(key_ones_in, 16 * b + 16)
                    o = free("st0", g, jt, h)
                    for s in halves:
                        ins = mm(o[:, s], stack[0:K0, 1, g, h, jt * P:(jt + 1) * P], stack[0:K0, 0, g, h, s],
                                 start=True, stop=True)
                    ins.then_inc(tensor_done, tensor.one("st0", g, jt, h))

                def pv0(g, jt, part):
                    scalar_wait("exp0", g, jt, G - 1)
                    if jt == 0 and g == 1:
                        scalar_wait("pv0_out", 0)
                    for s in halves[part:part + 1]:
                        for h in range(G):
                            ins = mm(pv[D * h:D * h + D, s], v0[:, jt, g * P + D * h:g * P + D * h + D],
                                     p0[:, jt % 2, h, s], start=jt == 0, stop=jt == NT - 1)
                    if part:
                        ins.then_inc(tensor_done, tensor.one("pv0", g, jt))

                def den0(g):
                    for h in range(G):
                        if adder(g, NT - 2, h) == "pool":
                            pe.wait_ge(pool_done, gps.at(b, "add0", g, NT - 2, h))
                        else:
                            vector_wait("add0", g, NT - 2, h)
                    scalar_wait("exp0", g, NT - 1, G - 1)
                    o = free("den0", g)
                    for q in range(NT):
                        seg = segment[:, D - SEG - SEG * q:2 * D - SEG - SEG * q]
                        i = slice(q * P, (q + 1) * P)
                        for k, src in enumerate((acc0, p0[:, (NT - 1) % 2])):
                            for h in range(G):
                                ins = mm(o[D * h:D * h + D, 0:P], seg, src[:, h, i],
                                         start=q == 0 and k == 0, stop=q == NT - 1 and k == 1)
                    ins.then_inc(tensor_done, tensor.one("den0", g))

                def ex0(g):
                    o = free("ex0", g)
                    for k, name in enumerate(("ex0", "ex0+")):
                        vector_wait("rows0", g, k)
                        mm(o[:, halves[k]], heads_mask[:], rows0[:, k * NT // 2:(k + 1) * NT // 2, :],
                           start=True, stop=True).then_inc(tensor_done, tensor.one(name, g))

                pe.wait_ge(scalar_done, scalar.before(b, "x_hi", CT - 1))
                pe.wait_ge(vector_done, vector.before(b, "x_lo", CT - 1))
                for g in range(NG):
                    for t in range(2):
                        qk0(t, g)

                def v0_tile(k):
                    o = free("v0", k)
                    for q in range(4):
                        i = slice((4 * k + q) * P, (4 * k + q + 1) * P)
                        ins = three(o[:, q * C:(q + 1) * C], [[v[:, kt_, i] for kt_ in kts] for v in (xh, xl)],
                                    [[w[:, kt_, 2, :] for kt_ in kts] for w in (w0h, w0l)])
                    ins.then_inc(tensor_done, tensor.one("v0", k))

                for h in range(G):
                    for it in range(NT):
                        if it == NT // 2 and h in (1, 2):
                            v0_tile(h - 1)
                        s0(0, h, it)
                m0(0)
                for jt in range(NT):
                    for k in range(G):
                        st0(0, jt, k)
                        s0(1, *divmod(G * jt + k, NT))
                        if jt and k % 2:
                            pv0(0, jt - 1, k // 2)
                m0(1)
                pv0(0, NT - 1, 0)
                pv0(0, NT - 1, 1)
                for jt in range(NT):
                    for h in range(G):
                        st0(1, jt, h)
                        if jt and h % 2:
                            pv0(1, jt - 1, h // 2)
                    if jt == 0:
                        den0(0)
                    if jt == 2:
                        ex0(0)
                den0(1)
                pv0(1, NT - 1, 0)
                pv0(1, NT - 1, 1)
                ex0(1)
                for k in range(2):
                    scalar_wait("res_hi", 1, k)
                    vector_wait("res_lo", 1, k)
                    o = free("out0", k)
                    for ct in range(CT):
                        ins = three(o[:, halves[ct]], [[w[:, kt_, ct * P:(ct + 1) * P] for kt_ in kts] for w in (wo0h, wo0l)],
                                    [[side[:, part, kt_, halves[k]] for kt_ in kts] for part in range(2)])
                    ins.then_inc(tensor_done, tensor.one("out0", k))

                for layer in (1, 2):
                    if layer == 1:
                        vector_wait("mv", 1, 1)
                        mm(free("gn", 0)[:, 0:2], gn_avg[:], mv[:, :, 0], start=True, stop=True
                           ).then_inc(tensor_done, tensor.one("gn", 0))
                        vector_wait("gn", 3)
                        mm(free("gn", 1)[:, 0:2], gn_avg[:], gvar, start=True, stop=True
                           ).then_inc(tensor_done, tensor.one("gn", 1))

                    def v_tile(k):
                        if layer == 2 and k == 1:
                            vector_wait("feat_lo", 2, 1, CT - 1)
                        feat = (xh, xl) if layer == 1 else (side[:, 0], side[:, 1])
                        wh, wl = wqk[layer, "v", "h"], wqk[layer, "v", "l"]
                        o = free("v", layer, k)
                        for q in range(4):
                            j = slice((4 * k + q) * P, (4 * k + q + 1) * P)
                            ins = three(o[:, q * C:(q + 1) * C], [[v[:, kt_, j] for kt_ in kts] for v in feat],
                                        [[w[:, kt_, :] for kt_ in kts] for w in (wh, wl)])
                        ins.then_inc(tensor_done, tensor.one("v", layer, k))

                    if layer == 2:
                        vector_wait("feat_lo", 2, 0, CT - 1)
                        v_tile(0)
                    for t in range(2):
                        wh, wl = wqk[layer, "qk"[t], "h"], wqk[layer, "qk"[t], "l"]
                        for ct in range(CT):
                            o = free("qk", layer, t, ct)
                            for k, s in enumerate(halves):
                                low = None
                                if t == 0 and ct == 0:
                                    scalar_wait("norm_hi", layer, k, CT - 1)
                                    low = lambda: vector_wait("norm_lo", layer, k, CT - 1)
                                ins = three(o[:, s], [[w[:, kt_, ct * P:(ct + 1) * P] for kt_ in kts] for w in (wh, wl)],
                                            [[v[:, kt_, s] for kt_ in kts] for v in (xh, xl)], low=low)
                            ins.then_inc(tensor_done, tensor.one("qk", layer, t, ct))
                    if layer == 1:
                        v_tile(0)
                    scalar_wait("qk_hi", layer, 1, 1)
                    for it in range(NT):
                        if it == 4:
                            v_tile(1)
                        o = free("s", layer, it)
                        for s in halves:
                            for kt_ in kts:
                                ins = mm(o[:, s], qk_r[:, 0, 0, kt_, it * P:(it + 1) * P], qk_r[:, 1, 0, kt_, s],
                                         start=kt_ == 0, stop=kt_ == CT - 1)
                        ins.then_inc(tensor_done, tensor.one("s", layer, it))

                    def negated():
                        vector_wait("neg_lo", layer, 0)
                        nc.tensor.transpose(free("m", layer)[0:NMAX, 0:P], negmax[:, 0].rearrange("p s t -> p (s t)"),
                                            ident[:]).then_inc(tensor_done, tensor.one("m", layer))

                    def scores(n):
                        half, jp = divmod(n, 4)
                        o = free("st", layer, n)
                        for q in range(2):
                            j = slice((2 * jp + q) * P, (2 * jp + q + 1) * P)
                            three(o[:, halves[q]], [[qk_r[:, 1, part, kt_, j] for kt_ in kts] for part in range(2)],
                                  [[qk_r[:, 0, part, kt_, halves[half]] for kt_ in kts] for part in range(2)], last=False)

                    def less_maxima(n):
                        for q in range(2):
                            ins = mm(tile[slot("st", layer, n)][:, halves[q]], ones_r[:], max_in[:, halves[n // 4]],
                                     start=False, stop=True)
                        ins.then_inc(tensor_done, tensor.one("st", layer, n))

                    def values(n):
                        half, jp = divmod(n, 4)
                        scalar_wait("exp_hi", layer, n)
                        vector_wait("exp_lo", layer, n)
                        if n == 4:
                            scalar_wait("pv_out", layer, 0)
                        if n == 0:
                            vector_wait("v_lo", layer, 1)
                        for q in range(2):
                            j = 2 * jp + q
                            for ct in range(CT):
                                ins = three(pv[:, halves[ct]], [[v[:, j, ct * P:(ct + 1) * P]] for v in (vh, vl)],
                                            [[p[:, n % 2, halves[q]]] for p in (ph, pl)],
                                            first=jp == 0 and q == 0, last=jp == 3 and q == 1)
                        ins.then_inc(tensor_done, tensor.one("pv", layer, n))

                    def sums(half):
                        vector_wait("add", layer, 4 * half + 3)
                        o = free("den", layer, half)
                        for q in range(2):
                            ins = mm(o[:, 0:HALF], ones[:], acc[:, halves[q]], start=q == 0, stop=q == 1)
                        ins.then_inc(tensor_done, tensor.one("den", layer, half))

                    vector_wait("qk_lo", layer, 1, 1)
                    scores(0)
                    negated()
                    scores(1)
                    vector_wait("max_in", layer)
                    less_maxima(0)
                    for n in range(1, NT):
                        if n > 1:
                            scores(n)
                        less_maxima(n)
                        values(n - 1)
                        if n == NT // 2:
                            sums(0)
                    sums(1)
                    values(NT - 1)

                for k in range(2):
                    vector_wait("feat_lo", 3, k, CT - 1)
                    o = free("kt", k)
                    for q in range(4):
                        i = slice((4 * k + q) * P, (4 * k + q + 1) * P)
                        ins = three(o[:, q * C:(q + 1) * C], [[v[:, kt_, i] for kt_ in kts] for v in (xh, xl)],
                                    [[w[:, kt_, :] for kt_ in kts] for w in (w3h, w3l)])
                    ins.then_inc(tensor_done, tensor.one("kt", k))
                pe.wait_ge(pool_done, gps.at(b, "pool", 4, CT - 1))
                pe.wait_ge(w3_back, 32 * b + 32)
                o = free("qv")
                for k in range(2):
                    for kt_ in kts:
                        ins = mm(o[:, halves[k]], xp[:, kt_, k * P:(k + 1) * P], w3f[:, kt_, :],
                                 start=kt_ == 0, stop=kt_ == CT - 1)
                ins.then_inc(tensor_done, tensor.one("qv"))
                vector_wait("qv_in")
                o = free("mt")
                for ct in range(CT):
                    for k in range(2):
                        mm(o[:, ct * P:(ct + 1) * P], qv[:, k, ct * P:(ct + 1) * P],
                           qv[:, k, C + ct * P:C + (ct + 1) * P], start=k == 0, stop=k == 1)
                for ct in range(CT):
                    for kt_ in kts:
                        ins = mm(o[:, HALF + ct:HALF + ct + 1], w3f[:, kt_, ct * P:(ct + 1) * P], mv[:, kt_, 0:1],
                                 start=kt_ == 0, stop=kt_ == CT - 1)
                ins.then_inc(tensor_done, tensor.one("mt"))
                vector_wait("kbar")
                o = free("g")
                for ct in range(CT):
                    mm(o[:, ct * C:(ct + 1) * C], mtm[:, ct, :], wo3[:, ct, :], start=True, stop=True)
                mm(o[:, HALF:HALF + 2], mix_own[:], kbar, start=True, stop=True)
                mm(o[:, HALF + 2:HALF + 4], mix_other[:], kbar, start=True, stop=True
                   ).then_inc(tensor_done, tensor.one("g"))
                vector_wait("sm", 1)
                for ct in range(CT):
                    o = free("smt", ct)
                    for nt in range(NT):
                        ins = nc.tensor.transpose(o[:, nt * P:(nt + 1) * P], kt[:, nt, ct * P:(ct + 1) * P], ident[:])
                    ins.then_inc(tensor_done, tensor.one("smt", ct))
                scalar_wait("smt_hi", 1)
                vector_wait("smt_lo", 1)
                for ct in range(CT):
                    o = free("z", ct)
                    for s in halves:
                        ins = three(o[:, s], [[g_[:, kt_, ct * P:(ct + 1) * P] for kt_ in kts] for g_ in (gh, gl)],
                                    [[qk_r[:, 0, part, kt_, s] for kt_ in kts] for part in range(2)])
                    ins.then_inc(tensor_done, tensor.one("z", ct))
                assert not tensor.todo


_INS = ["x", "L0_conv_w_proj", "L0_conv_b_proj", "L0_conv_w_out", "L0_conv_b_out", "L1_conv_gn_w", "L1_conv_gn_b",
        "L1_conv_wq", "L1_conv_bq", "L1_conv_wk", "L1_conv_bk", "L1_conv_wv", "L1_conv_bv", "L1_conv_wo", "L1_conv_bo",
        "L2_conv_f_w", "L2_conv_f_b", "L2_conv_g_w", "L2_conv_g_b", "L2_conv_h_w", "L2_conv_h_b", "L2_conv_o_w",
        "L2_conv_o_b", "L3_conv_w_qk", "L3_conv_b_qk", "L3_conv_w_v", "L3_conv_b_v", "L3_conv_mix_weight",
        "L3_conv_w_out", "L3_conv_bn_weight", "L3_conv_bn_bias"]


def kernel(**inputs):
    import numpy as _np
    import concourse.bacc as _bacc
    from concourse import mybir as _mybir
    from concourse.bass_utils import run_bass_kernel_spmd as _run

    nc = _bacc.Bacc("TRN2", target_bir_lowering=False, num_devices=1)
    arrays, args = {}, []
    for name in _INS:
        a = _np.ascontiguousarray(inputs[name])
        arrays[f"in_{name}_dram"] = a
        args.append(nc.dram_tensor(f"in_{name}_dram", a.shape, _mybir.dt.from_np(a.dtype), kind="ExternalInput").ap())
    args.append(nc.dram_tensor("out_dram", (B, C, 32, 32), F32, kind="ExternalOutput").ap())
    conv_seq_kernel(nc, *args)
    r = _run(nc, [arrays], core_ids=[0])
    return r.results[0]["out_dram"]
```

```python
from contextlib import ExitStack

import concourse.bass as bass
from concourse import mybir

F32 = mybir.dt.float32
F32R = mybir.dt.float32r
ALU = mybir.AluOpType
ACT = mybir.ActivationFunctionType
X = mybir.AxisListType.X

P = 128
B = 8
C = 256
N = 1024
CT = C // P
NT = N // P
HALF = N // 2
HEADS = 8
D = C // HEADS
G = P // D
NG = HEADS // G
IMAX = 96
NMAX = 2 * NT
K0 = IMAX + NMAX
HT = NT // 2
SEG = D // HT
UNITS = [(g, half) for g in range(NG) for half in range(2)]
SUMMED = 6
POOL_BOTH = (1, 2, 4)
DEPTH = 4
SLOTS = 3
WIN = 16
POOLED = 16
N2 = POOLED * POOLED


def adder(g, half, jt, pair):
    if jt == 0 or jt >= SUMMED:
        return None
    if (g, half) == UNITS[-1]:
        return "pool" if pair == 0 and jt % 2 == 0 else "vector"
    return "pool" if pair == 0 or jt in POOL_BOTH else "vector"


def next_unit(g, half):
    k = UNITS.index((g, half)) + 1
    return UNITS[k] if k < len(UNITS) else None


def last_unit(g, half):
    k = UNITS.index((g, half))
    return UNITS[k - 1] if k else None


def rows_of(unit, k):
    g, half = unit
    h, t = divmod(k, HT)
    return g, h, HT * half + t


def tensor_steps():
    s = [("qk0", t, g) for g in range(NG) for t in range(2)]
    for k in range(G * HT):
        s += [("v0", k // 3 - 1)] if k in (3, 6, 9, 12) else []
        s += [("s0", *rows_of(UNITS[0], k))]
    s += [("m0", 0, 0)]
    for u in UNITS:
        for jt in range(NT):
            for pair in range(2):
                s += [("st0", *u, jt, pair)]
                s += [("s0", *rows_of(next_unit(*u), 2 * jt + pair))] if next_unit(*u) else []
                s += [("pv0", *u, 0)] if (jt, pair) == (1, 0) else []
            s += [("pv0", *u, jt - 1)] if jt > 1 else []
            s += [("ex0", *last_unit(*u))] if last_unit(*u) and jt == 1 else []
            s += [("out0", 0)] if u == UNITS[-1] and jt == 4 else []
        s += [("pv0", *u, NT - 1), ("m0", *next_unit(*u)), ("den0", *u)] if next_unit(*u) else (
            [("den0", *u), ("pv0", *u, NT - 1)])
    s += [("ex0", *UNITS[-1]), ("out0", 1)]
    for layer in (1, 2):
        s += [("gn",), ("pv_groups",)] if layer == 1 else [("v", 2, 0)]
        s += [("qk", layer, t, ct) for t in range(2) for ct in range(CT)]
        s += [("v", 1, 0)] if layer == 1 else []
        s += [("s", layer, it) for it in range(NT)] + [("v", layer, 1)]
        s += [("m", layer), ("st", layer, 0), ("st", layer, 1)]
        for n in range(2, NT):
            s += [("st", layer, n), ("pv", layer, n - 2)]
            s += [("den", layer, 0)] if n == 5 else []
        s += [("pv", layer, NT - 2)]
        s += [("den", layer, 1), ("pv", layer, NT - 1)]
    s += [("kt", 0), ("kt", 1), ("qv",), ("mt",), ("g",), ("smt", 0), ("smt", 1), ("z", 0), ("z", 1)]
    return s


def scalar_steps():
    s = [("qk0_hi", t, g) for g in range(NG) for t in range(2)]
    s += [("v0_kept", k) for k in range(4)]
    for u in UNITS:
        for jt in range(NT):
            s += [("pv0_out", *last_unit(*u))] if last_unit(*u) and jt == 0 else []
            s += [("exp0", *u, jt, pair) for pair in range(2)]
            s += [("res_hi", *last_unit(*u))] if last_unit(*u) and jt == 2 else []
    s += [("pv0_out", *UNITS[-1]), ("res_hi", *UNITS[-1])]
    for layer in (1, 2):
        s += [("std", layer)] + [("norm_hi", layer, k, ct) for k in range(2) for ct in range(CT)]
        s += [("qk_hi", layer, t, ct) for t in range(2) for ct in range(CT)]
        s += [("v_hi", 1, 0)] if layer == 1 else []
        s += [("v_hi", layer, 1), ("exp_table", layer)]
        for n in range(NT - 1):
            s += [("exp_hi", layer, n), ("exp", layer, n)]
            s += [("pv_out", layer, 0)] if n == NT // 2 else []
        s += [("feat_hi", layer + 1, 0, ct) for ct in range(CT)] + [("exp", layer, NT - 1), ("exp_hi", layer, NT - 1)]
        s += [("pv_out", layer, 1)] + ([("v_hi", 2, 0)] if layer == 1 else [])
        s += [("feat_hi", layer + 1, 1, ct) for ct in range(CT)]
    s += [("kt_exp", 0), ("x_hi", 0), ("x_hi", 1), ("kt_exp", 1), ("mix_exp",), ("smt_hi", 0), ("g_hi", 0), ("g_hi", 1)]
    s += [("smt_hi", 1), ("z_kept", 0), ("z_kept", 1)]
    return s


def vector_steps():
    s = [("qk0_lo", t, g) for g in range(NG) for t in range(2)]
    s += [("max0", *rows_of(UNITS[0], k)) for k in range(G * HT)]
    s += [(n, 0, 0) for n in ("neg_hi", "neg_copy", "neg_lo")] + [("max_rows", 0, 0, h) for h in range(G)]
    for u in UNITS:
        last, following = last_unit(*u), next_unit(*u)
        for jt in range(NT):
            s += [("rec0", *last), ("rows0", *last)] if last and jt == 0 else []
            s += [("res", *last)] if last and jt == 2 else []
            for pair in range(2):
                s += [("max0", *rows_of(following, 2 * jt + pair))] if following else []
                s += [("add0", *u, jt - 1, pair)] if jt and adder(*u, jt - 1, pair) == "vector" else []
            s += [("res_lo", *last)] if last and jt == 3 else []
            s += [("x1", 0, ct) for ct in range(CT)] if u == UNITS[-1] and jt == 5 else []
        if following:
            s += [(n, *following) for n in ("neg_hi", "neg_copy", "neg_lo")]
            s += [("max_rows", *following, h) for h in range(G)]
    s += [("stat", 1, 0, ct) for ct in range(CT)]
    s += [(n, *UNITS[-1]) for n in ("rec0", "rows0", "res", "res_lo")]
    s += [("x1", 1, ct) for ct in range(CT)] + [("stat", 1, 1, ct) for ct in range(CT)]
    for layer in (1, 2):
        s += [("mv", layer, 0), ("mv", layer, 1)]
        s += [("gn_dev",), ("gn",)] if layer == 1 else []
        s += [("var", layer)]
        s += [("inv_std", layer), ("newton", layer, 0), ("newton", layer, 1), ("newton", layer, 2)]
        s += [("scale", layer), ("offset", layer), ("shift", layer)] if layer == 1 else [("shift", layer)]
        for k in range(2):
            s += [("norm", layer, k, ct) for ct in range(CT)] + [("norm_lo", layer, k, ct) for ct in range(CT)]
        s += [("v_lo", 2, 0)] + [("feat_lo", 2, 1, ct) for ct in range(CT)] if layer == 2 else []
        s += [("qk_lo", layer, t, ct) for t in range(2) for ct in range(CT)]
        s += [("v_lo", 1, 0)] if layer == 1 else []
        s += [("max", layer, it) for it in range(NT)]
        s += [("neg_hi", layer), ("neg_copy", layer), ("neg_lo", layer), ("max_in", layer), ("v_lo", layer, 1)]
        for n in range(NT - 1):
            s += [("rec", layer, 0)] if n == 5 else []
            s += [("out", layer, 0), ("x", layer, 0, 0), ("x", layer, 0, 1)] if n == 6 else []
            s += [("exp_lo", layer, n)] + ([("add", layer, n)] if n % 4 else [])
            s += [("fold", layer)] if n == 3 else []
        s += [("stat", layer + 1, 0, ct) for ct in range(CT)] + [("feat_lo", layer + 1, 0, ct) for ct in range(CT)]
        s += [("add", layer, NT - 1), ("exp_lo", layer, NT - 1)]
        s += [("rec", layer, 1), ("out", layer, 1), ("x", layer, 1, 0), ("x", layer, 1, 1)]
        s += [("stat", 2, 1, ct) for ct in range(CT)] if layer == 1 else []
    s += [("feat_lo", 3, 1, ct) for ct in range(CT)]
    s += [("win_max", 0), ("kt_sub", 0)] + [("stat", 3, 1, ct) for ct in range(CT)]
    s += [("mv", 3, 0), ("mv", 3, 1), ("win_max", 1), ("kt_sub", 1), ("x_lo", 0), ("x_lo", 1), ("qv_in",)]
    s += [("win_sum", 0), ("win_rec", 0), ("mt_in",), ("kbar",)]
    s += [("win_sum", 1), ("win_rec", 1), ("sm", 1)]
    s += [("mix", k) for k in range(4)] + [("mix_sum",), ("mix_rec",), ("mix_pi",)]
    s += [("smt_lo", 0), ("g_lo", 0), ("g_lo", 1), ("smt_lo", 1)]
    s += [("z_stat", ct, k) for ct in range(CT) for k in range(2)]
    return s


def pool_steps():
    s = [("add0", *u, jt, pair) for u in UNITS for jt in range(NT) for pair in range(2)
         if adder(*u, jt, pair) == "pool"]
    s += [("pool", k, ct) for k in range(10) for ct in range(CT)] + [("sm", 0)]
    return s


class Steps:

    def __init__(self, names):
        assert len(set(names)) == len(names)
        self.names, self.count, self.place = names, len(names), {n: k + 1 for k, n in enumerate(names)}

    def at(self, b, *name):
        return (b + 1) * self.count + self.place[name]

    def before(self, b, *name):
        return b * self.count + self.place[name]

    def start(self):
        self.todo = list(self.names)

    def one(self, *name):
        assert self.todo.pop(0) == name, name
        return 1


def last_reader(name):
    kind, rest = name[0], name[1:]
    return {
        "qk0": ("vector", "qk0_lo", *rest), "v0": ("scalar", "v0_kept", *rest),
        "s0": ("vector", "max0", *rest), "m0": ("vector", "max_rows", *rest, G - 1),
        "st0": ("scalar", "exp0", *rest), "den0": ("vector", "rec0", *rest),
        "ex0": ("vector", "res", *rest), "out0": ("vector", "x1", *rest, CT - 1),
        "gn": ("vector", "offset", 1),
        "qk": ("vector", "qk_lo", *rest), "s": ("vector", "max", *rest), "v": ("vector", "v_lo", *rest),
        "m": ("vector", "max_in", *rest), "st": ("scalar", "exp" if rest[-1:] != (NT - 1,) else "exp_hi", *rest), "den": ("vector", "out", *rest),
        "kt": ("vector", "kt_sub", *rest), "qv": ("vector", "qv_in"), "mt": ("vector", "kbar"),
        "g": ("vector", "g_lo", CT - 1), "smt": ("vector", "smt_lo", *rest), "z": ("scalar", "z_kept", *rest),
    }[kind]


def conv_seq_kernel(nc, x, L0_w_proj, L0_b_proj, L0_w_out, L0_b_out, L1_gn_w, L1_gn_b, L1_wq, L1_bq,
                    L1_wk, L1_bk, L1_wv, L1_bv, L1_wo, L1_bo, L2_f_w, L2_f_b, L2_g_w, L2_g_b, L2_h_w,
                    L2_h_b, L2_o_w, L2_o_b, L3_w_qk, L3_b_qk, L3_w_v, L3_b_v, L3_mix, L3_w_out,
                    L3_bn_w, L3_bn_b, out):
    tensor, scalar, vector, gps = (Steps(f()) for f in (tensor_steps, scalar_steps, vector_steps, pool_steps))
    tiles = [n for n in tensor.names if not n[0].startswith("pv")]
    place = {n: k for k, n in enumerate(tiles)}

    def slot(*name):
        return place[name] % SLOTS

    def leaver(b, *name):
        k = place[name]
        former = tiles[k - SLOTS] if k >= SLOTS else [n for n in tiles if slot(*n) == k][-1]
        engine, *step = last_reader(former)
        steps = {"scalar": scalar, "vector": vector}[engine]
        return engine, (steps.at if k >= SLOTS else steps.before)(b, *step)

    x_v = x.rearrange("b (t p) h w -> b p t (h w)", p=P)
    out_v = out.rearrange("b (t p) h w -> b p t (h w)", p=P)
    z_dram = nc.dram_tensor("z_scratch", (B, P, CT, N), F32, kind="Internal").ap()
    w3f_dram = nc.dram_tensor("w3f_scratch", (P, CT, 2 * C), F32, kind="Internal").ap()
    wo3_dram = nc.dram_tensor("wo3_scratch", (P, CT, C), F32, kind="Internal").ap()
    x3_dram = nc.dram_tensor("x3_scratch", (B, P, CT, N), F32, kind="Internal").ap()

    with ExitStack() as ctx:
        def sb(name, shape, dt=F32):
            return ctx.enter_context(nc.sbuf_tensor(name, shape, dt))

        def sem(name):
            return ctx.enter_context(nc.semaphore(name))

        def share(*uses):
            made = {}
            for use in uses[:-1]:
                with ExitStack() as short:
                    for name, shape, dt in use:
                        made[name] = short.enter_context(nc.sbuf_tensor(name, shape, dt))
            for name, shape, dt in uses[-1]:
                made[name] = sb(name, shape, dt)
            return made

        w0h = sb("w0h", [P, CT, 3, C], F32R)
        w0l = sb("w0l", [P, CT, 3, C], F32R)
        wo0h = sb("wo0h", [P, CT, C], F32R)
        wo0l = sb("wo0l", [P, CT, C], F32R)
        wqk = {(l, t, s): sb(f"w_{l}{t}{s}", [P, CT, C], F32R) for l in (1, 2) for t in "qkv" for s in "hl"}
        w3h = sb("w3h", [P, CT, C], F32R)
        w3l = sb("w3l", [P, CT, C], F32R)
        ident = sb("ident", [P, P])
        ones = sb("ones", [P, P])
        ones_r = sb("ones_r", [P, P], F32R)
        gn_avg = sb("gn_avg", [P, P])
        gn_rest = sb("gn_rest", [P, P])
        heads_mask = sb("heads_mask", [P, P])
        mix_own = sb("mix_own", [P, P])
        mix_other = sb("mix_other", [P, P])
        mixcol = sb("mixcol", [P, 2])
        mask8 = sb("mask8", [NMAX, NT])
        segment = sb("segment", [P, 2 * D - SEG])
        seg_own = sb("seg_own", [P, HT])
        cols = sb("cols", [P, 48])
        b3_parts = sb("b3_parts", [P, C], F32R)
        b3row = sb("b3row", [P, 2 * C])
        pool_w = sb("pool_w", [P, POOLED, POOLED])
        small = sb("small", [P, 128])
        max_in = sb("max_in", [P, N], F32R)
        bn_rows = sb("bn_rows", [P, CT, 2 * B, 6])
        raw = sb("raw", [P, N])
        rec0 = sb("rec0", [P, P])
        act = sb("act", [P, CT, N])

        shared = share([("x_in", [P, CT, N], F32)], [("v0", [P, NT, C], F32)])
        x_in, v0 = shared["x_in"], shared["v0"]
        shared = share([("xh", [P, CT, N], F32R), ("xl", [P, CT, N], F32R)],
                       [("fin_split", [P, 2, CT, N], F32)], [("acc0", [P, 2, 2, N], F32)])
        xh, xl, acc0, fin_split = (shared[n] for n in ("xh", "xl", "acc0", "fin_split"))
        shared = share([("side_front", [P, 3 * N + HALF], F32), ("rows0", [P, HT, P], F32)],
                       [("fin_side", [P, 2, CT, N], F32)], [("side", [P, 2, CT, N], F32R)])
        side, rows0, fin_side = shared["side"], shared["rows0"], shared["fin_side"]
        shared = share([("stage", [P, 32 * C], F32)],
                       [("p0", [P, DEPTH, 2, N], F32)],
                       [("fin_qk", [P, 2, 2, CT, N], F32)],
                       [("qk_r", [P, 2, 2, CT, N], F32R)])
        stage, p0, qk_r, fin_qk = (shared[n] for n in ("stage", "p0", "qk_r", "fin_qk"))
        shared = share([("vh", [P, NT, C], F32R), ("vl", [P, NT, C], F32R), ("ph", [P, 2, N], F32R),
                        ("pl", [P, 2, N], F32R), ("p12", [P, 2, N], F32), ("tmp", [P, N], F32),
                        ("acc", [P, N], F32)],
                       [("kt", [P, NT, C], F32), ("zbuf", [P, CT, N], F32), ("qv", [P, 2, 2 * C], F32),
                        ("mtm", [P, CT, P], F32), ("gh", [P, CT, C], F32R), ("gl", [P, CT, C], F32R),
                        ("gap", [P, 23 * C], F32), ("w3f", [P, CT, 2 * C], F32), ("wo3", [P, CT, C], F32),
                        ("xp", [P, CT, N2], F32), ("row_sum", [P, CT, 32, POOLED], F32)],
                       [("before_fin", [P, 4 * N], F32), ("fin_rest", [P, 3, 2, CT, N], F32)],
                       [("stack", [P, 2, NG, G, N], F32R)])
        vh, vl, ph, pl, p12, tmp, acc = (shared[n] for n in ("vh", "vl", "ph", "pl", "p12", "tmp", "acc"))
        kt, zbuf, qv, xp, row_sum, mtm, gh, gl, w3f, wo3 = (
            shared[n] for n in ("kt", "zbuf", "qv", "xp", "row_sum", "mtm", "gh", "gl", "w3f", "wo3"))
        fin_rest, stack = shared["fin_rest"], shared["stack"]
        fin = [(v[:, 0], v[:, 1]) for v in (fin_side, fin_qk[:, 1], fin_split, fin_qk[:, 0],
                                            fin_rest[:, 0], fin_rest[:, 1], fin_rest[:, 2])]
        fin.append((zbuf[:], act[:]))
        FIN_ORDER = [B - 1, *range(B - 1)]

        tile = [ctx.enter_context(nc.psum_tensor(f"tile{k}", [P, N], F32)) for k in range(SLOTS)]
        pv = ctx.enter_context(nc.psum_tensor("pv", [P, N], F32))

        names = ["bq0", "bk0", "bv0", "bo0", "gnw", "gnb", "bq1", "bk1", "bv1", "bo1", "bq2", "bk2",
                 "bv2", "bo2", "b3", "bnw", "bnb", "bvo1", "bvo2", "scale", "shift", "bnscale", "bnshift"]

        def col(name, ct=None):
            k = 2 * names.index(name)
            return cols[:, k:k + 2] if ct is None else cols[:, k + ct:k + ct + 1]

        maxima = small[:, 0:G * NT]
        negmax = small[:, 32:32 + G * NMAX].rearrange("p (h s t) -> p h s t", h=G, s=2)
        stats = small[:, 96:120].rearrange("p (t k s) -> p t k s", t=CT, k=2)
        mv = small[:, 120:124].rearrange("p (t s) -> p t s", t=CT)
        mh = sb("mh", [P, G, NT], F32R)
        pairs = sb("pairs", [P, 48])
        gdev, gsq, veps, y0, y1, y2, inv_std, mscale = (pairs[:, 2 * k:2 * k + 2] for k in range(8))
        kbar, larger, mix_sum, mix_rec, mix_pi = (pairs[:, 22 + 2 * k:24 + 2 * k] for k in range(5))
        logits, mix_e, logits_in = pairs[:, 32:36], pairs[:, 36:40], pairs[:, 40:44]
        win = sb("win", [P, NT * C // WIN])
        win_r = sb("win_r", [P, NT * C // WIN])

        weights_in = [sem(f"weights_in{k}") for k in range(13)]; vectors_in = sem("vectors_in"); consts_made = sem("consts_made")
        setup_tensor = sem("setup_tensor"); setup_scalar = sem("setup_scalar"); setup_vector = sem("setup_vector")
        tensor_done = sem("tensor_done"); scalar_done = sem("scalar_done")
        vector_done = sem("vector_done"); pool_done = sem("pool_done")
        w3_kept = sem("w3_kept"); w3_back = sem("w3_back")
        x_loaded = sem("x_loaded"); act_loaded = sem("act_loaded")
        stacked = [[sem(f"stacked{g}{h}") for h in range(G)] for g in range(NG)]
        key_ones_in = sem("key_ones_in")
        x3_stored = sem("x3_stored"); z_stored = sem("z_stored")
        bn_in = [sem(f"bn_in{b}") for b in range(B - 1)]; bn_steps = sem("bn_steps"); bn_scaled = sem("bn_scaled")
        bn_added = sem("bn_added"); stored = sem("stored")
        NVEC = 3 * G + 14 + G + 2
        U = CT * C

        ctx.enter_context(nc.allow_non_contiguous_dma(reason="vectors of a few hundred elements"))
        block = ctx.enter_context(nc.Block())

        @block.sync
        def _(sp):
            sp.dma_start(stage[:, 0:3 * U].rearrange("p (t n) -> p t n", t=CT),
                         L0_w_proj.rearrange("(t p) n -> p t n", p=P)).then_inc(weights_in[0], 16)
            for k, w in enumerate((L0_w_out, L1_wq, L1_wk, L1_wo, L2_f_w, L2_g_w, L2_o_w, L3_w_qk,
                                   L3_w_v, L3_w_out, L1_wv, L2_h_w)):
                sp.dma_start(stage[:, (3 + k) * U:(4 + k) * U].rearrange("p (t n) -> p t n", t=CT),
                             w.rearrange("(t p) n -> p t n", p=P)).then_inc(weights_in[1 + k], 16)
            sp.dma_start(x_in[:], x_v[0]).then_inc(x_loaded, 16)
            hb = L0_b_proj.rearrange("(t h s d) -> s h d t", t=CT, h=G, s=3)
            for s, name in enumerate(("bq0", "bk0", "bv0")):
                for h in range(G):
                    sp.dma_start(col(name)[D * h:D * h + D, :], hb[s, h]).then_inc(vectors_in, 16)
            for name, v in (("bo0", L0_b_out), ("gnw", L1_gn_w), ("gnb", L1_gn_b), ("bq1", L1_bq),
                            ("bk1", L1_bk), ("bv1", L1_bv), ("bo1", L1_bo), ("bq2", L2_f_b), ("bk2", L2_g_b),
                            ("bv2", L2_h_b), ("bo2", L2_o_b), ("b3", L3_b_qk), ("bnw", L3_bn_w), ("bnb", L3_bn_b)):
                sp.dma_start(col(name), v.rearrange("(t p) -> p t", p=P)).then_inc(vectors_in, 16)
            for h in range(G):
                sp.dma_start(mixcol[D * h:D * h + D, :], L3_mix.rearrange("m d -> d m")).then_inc(vectors_in, 16)
            for k, v in enumerate((L3_b_qk, L3_b_v)):
                sp.dma_start(b3row[:, k * C:(k + 1) * C],
                             v.rearrange("(a n) -> a n", a=1).broadcast_to((P, C))).then_inc(vectors_in, 16)

            sp.wait_ge(setup_scalar, 19)
            sp.dma_start(w3f_dram, w3f[:]).then_inc(w3_kept, 16)
            sp.dma_start(wo3_dram, wo3[:]).then_inc(w3_kept, 16)
            sp.wait_ge(w3_kept, 32)

            def batch(b, last):
                for g in range(NG):
                    sp.wait_ge(vector_done, vector.at(b, "qk0_lo", 1, g))
                    parts = qk_r[:].rearrange("p t s c n -> p (t s) c n")
                    for h in range(G):
                        for k, pair in enumerate((slice(0, 4, 2), slice(0, 4, 3), slice(1, 3))):
                            sp.dma_start(stack[D * k:D * k + D, :, g, h, :].bitcast(F32),
                                         parts[D * h:D * h + D, pair, g, :].bitcast(F32)
                                         ).then_inc(stacked[g][h], 16)
                sp.dma_start(stack[IMAX:K0, 1].rearrange("p g h (a n) -> p (g h a) n", n=P).bitcast(F32),
                             ones[0:NMAX, :].rearrange("p (a n) -> p a n", a=1)
                             .broadcast_to((NMAX, NG * G * N // P, P))).then_inc(key_ones_in, 16)
                sp.dma_start(act[:], x_v[b]).then_inc(act_loaded, 16)
                sp.wait_ge(tensor_done, tensor.at(b, "pv0", *UNITS[-1], NT - 1))
                sp.dma_start(w3f[:], w3f_dram).then_inc(w3_back, 16)
                sp.dma_start(wo3[:], wo3_dram).then_inc(w3_back, 16)
                sp.dma_start(x_in[:], x_v[0 if last else b + 1]).then_inc(x_loaded, 16)
                if last:
                    return
                sp.wait_ge(vector_done, vector.at(b, "x", 2, 1, 1))
                sp.dma_start(x3_dram[b], act[:]).then_inc(x3_stored, 16)
                sp.wait_ge(scalar_done, scalar.at(b, "z_kept", CT - 1))
                sp.dma_start(z_dram[b], zbuf[:]).then_inc(z_stored, 16)

            with sp.Fori(0, B - 1) as b:
                batch(b, False)
            batch(B - 1, True)

            sp.wait_ge(x3_stored, 16 * (B - 1))
            sp.wait_ge(z_stored, 16 * (B - 1))
            for b, (z_in, x3_in) in enumerate(fin[:B - 1]):
                if b == 0:
                    sp.wait_ge(tensor_done, tensor.at(B - 1, "v", 2, 1))
                elif b == 1:
                    sp.wait_ge(tensor_done, tensor.at(B - 1, "st", 2, NT - 1))
                elif b == 2:
                    sp.wait_ge(vector_done, vector.at(B - 1, "x_lo", CT - 1))
                elif b == 3:
                    sp.wait_ge(tensor_done, tensor.at(B - 1, "z", CT - 1))
                sp.dma_start(z_in, z_dram[b]).then_inc(bn_in[b], 16)
                sp.dma_start(x3_in, x3_dram[b]).then_inc(bn_in[b], 16)
            for k, b in enumerate(FIN_ORDER):
                for ct in range(CT):
                    sp.wait_ge(bn_added, CT * k + ct + 1)
                    sp.dma_start(out_v[b][:, ct], fin[b][0][:, ct, :]).then_inc(stored, 16)
            sp.wait_ge(stored, 16 * CT * B)

        @block.gpsimd
        def _(pool):
            pe = nc.gpsimd
            made = 0

            def note(ins):
                nonlocal made
                made += 1
                ins.then_inc(consts_made, 1)
                pool.wait_ge(consts_made, made)

            note(pe.memset(ident[:], 0.0))
            note(pe.memset(ones[:], 1.0))
            note(pe.memset(gn_avg[:], 1.0 / 8))
            note(pe.memset(heads_mask[:], 1.0))
            note(pe.memset(raw[:], 0.0))
            note(pe.memset(pool_w[:], 1.0 / 9))
            note(pe.memset(pool_w[:, 0, :], 1.0 / 6))
            note(pe.memset(pool_w[:, :, 0], 1.0 / 6))
            note(pe.memset(pool_w[:, 0, 0:1], 1.0 / 4))
            note(pe.affine_select(out=ident[:], in_=ident[:], compare_op=ALU.not_equal, fill=1.0, base=0,
                                  pattern=[[-1, P]], channel_multiplier=1))
            for m, w in ((gn_avg, 8), (heads_mask, D)):
                v = m[:].rearrange("p (a w) -> p a w", w=w)
                note(pe.affine_select(out=v, in_=v, compare_op=ALU.is_ge, fill=0.0, base=0,
                                      pattern=[[-w, P // w], [0, w]], channel_multiplier=1))
                note(pe.affine_select(out=v, in_=v, compare_op=ALU.is_ge, fill=0.0, base=w - 1,
                                      pattern=[[w, P // w], [0, w]], channel_multiplier=-1))
            note(pe.memset(segment[:], 0.0))
            note(pe.memset(segment[:, D - SEG:D], 1.0))
            pe.memset(win_r[:, 0:1], 1.0).then_inc(pool_done, gps.count)

            with pool.Fori(0, B) as b:
                gps.start()
                for u in UNITS:
                    for jt in range(1, SUMMED):
                        for pair in range(2):
                            if adder(*u, jt, pair) != "pool":
                                continue
                            pool.wait_ge(scalar_done, scalar.at(b, "exp0", *u, jt, pair))
                            if u[0] == 1 and jt == 1:
                                pool.wait_ge(tensor_done, tensor.at(b, "den0", 0, u[1]))
                            if jt > 1:
                                if adder(*u, jt - 1, pair) == "pool":
                                    pool.wait_ge(pool_done, gps.at(b, "add0", *u, jt - 1, pair))
                                else:
                                    pool.wait_ge(vector_done, vector.at(b, "add0", *u, jt - 1, pair))
                            total = acc0[:, u[1], pair, :]
                            first = p0[:, 0, pair, :] if jt == 1 else total
                            pe.tensor_tensor(total, first, p0[:, jt % DEPTH, pair, :], ALU.add
                                             ).then_inc(pool_done, gps.one("add0", *u, jt, pair))
                a5 = act[:].rearrange("p t (y c s) -> p t y c s", y=2 * POOLED, s=2)
                r5 = row_sum[:].rearrange("p t (y s) c -> p t y s c", s=2)
                x4 = xp[:].rearrange("p t (y c) -> p t y c", y=POOLED)
                for k in range(10):
                    half, part = divmod(k, 5)
                    if part == 0:
                        pool.wait_ge(vector_done, vector.at(b, "x", 2, half, 1))
                        y = slice(half * POOLED, (half + 1) * POOLED)
                        rows = slice(half * POOLED // 2, (half + 1) * POOLED // 2)
                        below = slice(max(rows.start, 1), rows.stop)
                        above = slice(below.start - 1, below.stop - 1)
                    if k:
                        pool.wait_ge(pool_done, gps.at(b, "pool", k - 1, CT - 1))
                    for ct in range(CT):
                        o, i0, i1, op = (
                            (row_sum[:, ct, y], a5[:, ct, y, :, 0], a5[:, ct, y, :, 1], ALU.add),
                            (row_sum[:, ct, y, 1:], row_sum[:, ct, y, 1:], a5[:, ct, y, 0:POOLED - 1, 1], ALU.add),
                            (x4[:, ct, rows], r5[:, ct, rows, 0, :], r5[:, ct, rows, 1, :], ALU.add),
                            (x4[:, ct, below], x4[:, ct, below], r5[:, ct, above, 1, :], ALU.add),
                            (x4[:, ct, rows], x4[:, ct, rows], pool_w[:, rows], ALU.mult),
                        )[part]
                        pe.tensor_tensor(o, i0, i1, op).then_inc(pool_done, gps.one("pool", k, ct))
                pool.wait_ge(vector_done, vector.at(b, "win_rec", 0))
                w4 = NT * C // WIN // 2
                w = kt[:, 0:NT // 2, :].rearrange("p t (w e) -> p (t w) e", e=WIN)
                pe.tensor_tensor(w, w, win_r[:, 0:w4].rearrange("p (w a) -> p w a", a=1).broadcast_to((P, w4, WIN)),
                                 ALU.mult).then_inc(pool_done, gps.one("sm", 0))
                assert not gps.todo

        @block.scalar
        def _(act_e):
            sc = nc.scalar
            ID = ACT.Identity

            def tile_wait(b, *name):
                act_e.wait_ge(tensor_done, tensor.at(b, *name))
                return tile[slot(*name)][:]

            act_e.wait_ge(weights_in[0], 16)
            w0 = stage[:, 0:3 * U].rearrange("p (t h s d) -> p t s h d", t=CT, h=HEADS, s=3)
            for ct in range(CT):
                for s in range(3):
                    sc.activation(w0h[:, ct, s, :].rearrange("p (h d) -> p h d", h=HEADS), w0[:, ct, s], ID
                                  ).then_inc(setup_scalar, 1)
            act_e.wait_ge(weights_in[1], 16)
            sc.activation(wo0h[:].rearrange("p t n -> p (t n)"), stage[:, 3 * U:4 * U], ID).then_inc(setup_scalar, 1)
            act_e.wait_ge(consts_made, 16)
            sc.activation(ones_r[:], ones[:], ID).then_inc(setup_scalar, 1)
            sc.activation(max_in[:], raw[:], ID).then_inc(setup_scalar, 1)
            flat = lambda w: w[:].rearrange("p t n -> p (t n)")
            for k, dst in enumerate((flat(wqk[1, "q", "h"]), flat(wqk[1, "k", "h"]), acc0[:, 0, 0, 0:U],
                                     flat(wqk[2, "q", "h"]), flat(wqk[2, "k", "h"]), acc0[:, 0, 1, 0:U],
                                     flat(w3h), None, flat(wo3))):
                act_e.wait_ge(setup_tensor, k + 1)
                src = tile[k % SLOTS][:, 0:U]
                src3 = src.rearrange("p (t n) -> p t n", t=CT)
                if k == 7:
                    sc.activation(w3f[:, :, C:], src3, ID).then_inc(setup_scalar, 1)
                else:
                    sc.activation(dst, src, ID).then_inc(setup_scalar, 1)
                if k == 6:
                    sc.activation(w3f[:, :, 0:C], src3, ID).then_inc(setup_scalar, 1)
            for k in range(2):
                act_e.wait_ge(setup_tensor, 10 + k)
                sc.activation(flat(wqk[1 + k, "v", "h"]), tile[k][:, 0:U], ID).then_inc(setup_scalar, 1)
            act_e.wait_ge(vectors_in, 16 * NVEC)
            sc.activation(b3_parts[:], b3row[:, 0:C], ID).then_inc(setup_scalar, 1)
            act_e.wait_ge(x_loaded, 16)
            act_e.wait_ge(setup_tensor, 12)
            for ct in range(CT):
                sc.activation(xh[:, ct, :], x_in[:, ct, :], ID).then_inc(setup_scalar, 1)
            sc.activation(pairs[:, 46:47], ones[:, 0:1], ID).then_inc(scalar_done, scalar.count)

            with act_e.Fori(0, B) as b:
                scalar.start()
                def qk0_hi(t, g):
                    sc.activation(qk_r[:, t, 0, g, :], tile_wait(b, "qk0", t, g), ID, bias=col(("bq0", "bk0")[t], g)
                                  ).then_inc(scalar_done, scalar.one("qk0_hi", t, g))

                for g in range(NG):
                    for t in range(2):
                        qk0_hi(t, g)
                act_e.wait_ge(vector_done, vector.before(b, "x_lo", 1))
                for k in range(4):
                    sc.activation(v0[:, 2 * k:2 * k + 2, :].rearrange("p t n -> p (t n)"), tile_wait(b, "v0", k)[:, 0:HALF],
                                  ID).then_inc(scalar_done, scalar.one("v0_kept", k))

                def summed(u, jt, pair):
                    if jt >= SUMMED:
                        act_e.wait_ge(tensor_done, tensor.at(b, "den0", *u))
                    elif adder(*u, max(jt, 1), pair) == "pool":
                        act_e.wait_ge(pool_done, gps.at(b, "add0", *u, max(jt, 1), pair))
                    else:
                        act_e.wait_ge(vector_done, vector.at(b, "add0", *u, max(jt, 1), pair))

                def exp0(u, jt, pair):
                    former = (u, jt - DEPTH) if jt >= DEPTH else (last_unit(*u), jt + NT - DEPTH)
                    if former[0]:
                        act_e.wait_ge(tensor_done, tensor.at(b, "pv0", *former[0], former[1]))
                        summed(*former, pair)
                    sc.activation(p0[:, jt % DEPTH, pair, :], tile_wait(b, "st0", *u, jt, pair), ACT.Exp,
                                  scale=float(D) ** -0.5).then_inc(scalar_done, scalar.one("exp0", *u, jt, pair))

                def pv0_out(g, half):
                    act_e.wait_ge(tensor_done, tensor.at(b, "pv0", g, half, NT - 1))
                    if g == 1:
                        act_e.wait_ge(vector_done, vector.at(b, "res_lo", 0, half))
                    s = slice(half * HALF, (half + 1) * HALF)
                    sc.activation(raw[:, s], pv[:, s], ID).then_inc(scalar_done, scalar.one("pv0_out", g, half))

                def res_hi(g, half):
                    act_e.wait_ge(vector_done, vector.at(b, "res", g, half))
                    s = slice(half * HALF, (half + 1) * HALF)
                    sc.activation(side[:, 0, g, s], raw[:, s], ID, bias=col("bv0", g)
                                  ).then_inc(scalar_done, scalar.one("res_hi", g, half))

                for s in stacked[0] + stacked[1]:
                    act_e.wait_ge(s, 48 * b + 48)
                for u in UNITS:
                    last = last_unit(*u)
                    for jt in range(NT):
                        if last and jt == 0:
                            pv0_out(*last)
                        for pair in range(2):
                            exp0(u, jt, pair)
                        if last and jt == 2:
                            res_hi(*last)
                pv0_out(*UNITS[-1])
                res_hi(*UNITS[-1])

                for layer in (1, 2):
                    act_e.wait_ge(vector_done, vector.at(b, "var", layer))
                    sc.activation(y2, veps, ACT.Sqrt).then_inc(scalar_done, scalar.one("std", layer))
                    act_e.wait_ge(vector_done, vector.at(b, "shift", layer))
                    for k in range(2):
                        for ct in range(CT):
                            s = slice(k * HALF, (k + 1) * HALF)
                            sc.activation(xh[:, ct, s], act[:, ct, s], ID, bias=col("shift", ct), scale=col("scale", ct)
                                          ).then_inc(scalar_done, scalar.one("norm_hi", layer, k, ct))
                    for t in range(2):
                        for ct in range(CT):
                            sc.activation(qk_r[:, t, 0, ct, :], tile_wait(b, "qk", layer, t, ct), ID,
                                          bias=col(f"b{'qk'[t]}{layer}", ct)
                                          ).then_inc(scalar_done, scalar.one("qk_hi", layer, t, ct))

                    def v_hi(l, k):
                        sc.activation(vh[:, 4 * k:4 * k + 4, :].rearrange("p t n -> p (t n)"),
                                      tile_wait(b, "v", l, k), ID).then_inc(scalar_done, scalar.one("v_hi", l, k))

                    def feat_hi(k):
                        dst = side[:, 0] if layer == 1 else xh
                        for ct in range(CT):
                            act_e.wait_ge(vector_done, vector.at(b, "x", layer, k, ct))
                            s = slice(k * HALF, (k + 1) * HALF)
                            sc.activation(dst[:, ct, s], act[:, ct, s], ID
                                          ).then_inc(scalar_done, scalar.one("feat_hi", layer + 1, k, ct))

                    if layer == 1:
                        v_hi(1, 0)
                    v_hi(layer, 1)
                    sc.activation(pairs[:, 46:47], ones[:, 0:1], ACT.Exp).then_inc(scalar_done, scalar.one("exp_table", layer))

                    def pv_out(half):
                        act_e.wait_ge(tensor_done, tensor.at(b, "pv", layer, 4 * half + 3))
                        if half:
                            act_e.wait_ge(vector_done, vector.at(b, "x", layer, 0, 1))
                        sc.activation(raw[:], pv[:], ID).then_inc(scalar_done, scalar.one("pv_out", layer, half))

                    scale = float(C) ** -0.5 if layer == 1 else 1.0
                    for n in range(NT):
                        if n >= 2:
                            act_e.wait_ge(tensor_done, tensor.at(b, "pv", layer, n - 2))
                            act_e.wait_ge(vector_done, vector.at(b, "exp_lo", layer, n - 2))
                            act_e.wait_ge(vector_done, vector.at(b, "add", layer, n - 2 + (n % 4 == 2)))
                        if n == NT - 1:
                            feat_hi(0)
                        scores = tile_wait(b, "st", layer, n)
                        for name in ("exp_hi", "exp") if n < NT - 1 else ("exp", "exp_hi"):
                            dst = ph if name == "exp_hi" else p12
                            sc.activation(dst[:, n % 2, :], scores, ACT.Exp, scale=scale
                                          ).then_inc(scalar_done, scalar.one(name, layer, n))
                        if n == NT // 2:
                            pv_out(0)
                    pv_out(1)
                    if layer == 1:
                        v_hi(2, 0)
                    feat_hi(1)

                for k in range(2):
                    act_e.wait_ge(vector_done, vector.at(b, "kt_sub", k))
                    v = kt[:, 4 * k:4 * k + 4, :].rearrange("p t n -> p (t n)")
                    sc.activation(v, v, ACT.Exp).then_inc(scalar_done, scalar.one("kt_exp", k))
                    if k == 0:
                        act_e.wait_ge(x_loaded, 16 * b + 32)
                        act_e.wait_ge(tensor_done, tensor.at(b, "kt", 1))
                        for ct in range(CT):
                            sc.activation(xh[:, ct, :], x_in[:, ct, :], ID
                                          ).then_inc(scalar_done, scalar.one("x_hi", ct))
                act_e.wait_ge(vector_done, vector.at(b, "mix", 3))
                sc.activation(mix_e, logits, ACT.Exp).then_inc(scalar_done, scalar.one("mix_exp"))

                def smt_hi(ct):
                    sc.activation(qk_r[:, 0, 0, ct, :], tile_wait(b, "smt", ct), ID
                                  ).then_inc(scalar_done, scalar.one("smt_hi", ct))

                smt_hi(0)
                act_e.wait_ge(vector_done, vector.at(b, "mix_pi"))
                gt = tile_wait(b, "g")
                for ct in range(CT):
                    sc.activation(gh[:, ct, :], gt[:, ct * C:(ct + 1) * C], ID, scale=mix_pi[:, ct:ct + 1]
                                  ).then_inc(scalar_done, scalar.one("g_hi", ct))
                smt_hi(1)
                for ct in range(CT):
                    sc.activation(zbuf[:, ct, :], tile_wait(b, "z", ct), ID
                                  ).then_inc(scalar_done, scalar.one("z_kept", ct))
                assert not scalar.todo

            act_e.wait_ge(bn_steps, 3)
            sc.activation(y2, veps, ACT.Sqrt).then_inc(bn_steps, 1)
            act_e.wait_ge(bn_steps, 11)
            for b in FIN_ORDER:
                if b < B - 1:
                    act_e.wait_ge(bn_in[b], 32)
                z = fin[b][0]
                for ct in range(CT):
                    sc.activation(z[:, ct, :], z[:, ct, :], ID, bias=col("bnshift", ct),
                                  scale=col("bnscale", ct)).then_inc(bn_scaled, 1)

        @block.vector
        def _(dve):
            ve = nc.vector
            TT, STT, TS = ve.tensor_tensor, ve.scalar_tensor_tensor, ve.tensor_scalar
            f = lambda ap: ap.bitcast(F32)
            flat = lambda w: w[:].rearrange("p t n -> p (t n)")

            dve.wait_ge(setup_scalar, 7)
            w0 = stage[:, 0:3 * U].rearrange("p (t h s d) -> p t s h d", t=CT, h=HEADS, s=3)
            for ct in range(CT):
                for s in range(3):
                    v = lambda w: w[:, ct, s, :].rearrange("p (h d) -> p h d", h=HEADS)
                    TT(v(w0l), w0[:, ct, s], f(v(w0h)), ALU.subtract).then_inc(setup_vector, 1)
            TT(flat(wo0l), stage[:, 3 * U:4 * U], f(flat(wo0h)), ALU.subtract).then_inc(setup_vector, 1)
            for k, hi, lo in ((0, wqk[1, "q", "h"], wqk[1, "q", "l"]), (1, wqk[1, "k", "h"], wqk[1, "k", "l"]),
                              (3, wqk[2, "q", "h"], wqk[2, "q", "l"]), (4, wqk[2, "k", "h"], wqk[2, "k", "l"]),
                              (6, w3h, w3l)):
                dve.wait_ge(setup_scalar, 10 + k + (k == 6))
                TT(flat(lo), tile[k % SLOTS][:, 0:U], f(flat(hi)), ALU.subtract).then_inc(setup_vector, 1)
            for k in range(2):
                dve.wait_ge(setup_scalar, 20 + k)
                TT(flat(wqk[1 + k, "v", "l"]), tile[k][:, 0:U], f(flat(wqk[1 + k, "v", "h"])), ALU.subtract
                   ).then_inc(setup_vector, 1)
            dve.wait_ge(setup_tensor, 12)
            dve.wait_ge(vectors_in, 16 * NVEC)
            for k in range(2):
                TT(col(f"bvo{k + 1}"), pv[:, 2 * k:2 * k + 2], col(f"bo{k + 1}"), ALU.add).then_inc(setup_vector, 1)
            for m in range(2):
                for dst, src in ((mix_own, m), (mix_other, 1 - m)):
                    v = lambda w: w[:].rearrange("p (h m e) -> p m h e", h=G, m=2)[:, m]
                    TS(v(dst), v(heads_mask), mixcol[:, src:src + 1], None, ALU.mult).then_inc(setup_vector, 1)
            TT(gn_rest[:], ident[:], gn_avg[:], ALU.subtract).then_inc(setup_vector, 1)
            first_rows = ident[:].rearrange("p (h t e) -> p h t e", h=G, e=SEG)[:, :, :, 0]
            TT(seg_own[:], first_rows[:, 0], first_rows[:, 1], ALU.add).then_inc(setup_vector, 1)
            for h in range(2, G):
                dve.wait_ge(setup_vector, 20 + h)
                TT(seg_own[:], seg_own[:], first_rows[:, h], ALU.add).then_inc(setup_vector, 1)
            TT(mask8[:], ident[0:NMAX, 0:NT], ident[0:NMAX, NT:NMAX], ALU.add).then_inc(setup_vector, 1)
            dve.wait_ge(setup_scalar, 22)
            TT(tmp[:, 0:C], b3row[:, 0:C], f(b3_parts[:]), ALU.subtract).then_inc(setup_vector, 1)
            TS(acc[:, 0:C], f(b3_parts[:]), ident[:, 0:1], None, ALU.mult).then_inc(setup_vector, 1)
            dve.wait_ge(setup_vector, 27)
            STT(b3_parts[:], tmp[:, 0:C], ident[:, D:D + 1], acc[:, 0:C], ALU.mult, ALU.add).then_inc(setup_vector, 1)
            for ct in range(CT):
                dve.wait_ge(setup_scalar, 23 + ct)
                TT(xl[:, ct, :], x_in[:, ct, :], f(xh[:, ct, :]), ALU.subtract).then_inc(setup_vector, 1)
            ve.memset(small[:], 0.0)
            ve.memset(pairs[:, 47:48], 1.0).then_inc(vector_done, vector.count)

            with dve.Fori(0, B) as b:
                vector.start()

                def own(*step):
                    dve.wait_ge(vector_done, vector.at(b, *step))

                def tile_wait(*name):
                    dve.wait_ge(tensor_done, tensor.at(b, *name))
                    return tile[slot(*name)]

                def scalar_wait(*step):
                    dve.wait_ge(scalar_done, scalar.at(b, *step))

                def qk0_lo(t, g):
                    scalar_wait("qk0_hi", t, g)
                    STT(qk_r[:, t, 1, g, :], tile[slot("qk0", t, g)][:], col(("bq0", "bk0")[t], g),
                        f(qk_r[:, t, 0, g, :]), ALU.add, ALU.subtract).then_inc(vector_done, vector.one("qk0_lo", t, g))

                def max0(g, h, it):
                    t = tile_wait("s0", g, h, it)
                    ve.tensor_reduce(maxima[:, h * NT + it:h * NT + it + 1], t[:], X, ALU.max
                                     ).then_inc(vector_done, vector.one("max0", g, h, it))

                def negate(key, heads, ts, last):
                    own(*last)
                    m3 = maxima[:, 0:heads * NT].rearrange("p (h t) -> p h t", h=heads)[:, :, ts]
                    hi = mh[:, 0:heads, ts]
                    TS(hi, m3, -1.0, None, ALU.mult).then_inc(vector_done, vector.one("neg_hi", *key))
                    own("neg_hi", *key)
                    ve.tensor_copy(negmax[:, 0:heads, 0, ts], f(hi)).then_inc(vector_done, vector.one("neg_copy", *key))
                    STT(negmax[:, 0:heads, 1, ts], m3, -1.0, f(hi), ALU.mult, ALU.subtract
                        ).then_inc(vector_done, vector.one("neg_lo", *key))

                def spread(dst, src, ts):
                    n = ts.stop - ts.start
                    return TT(dst.rearrange("p (t n) -> p t n", t=n),
                              src.rearrange("p (a n) -> p a n", a=1).broadcast_to((NMAX, n, P)),
                              mask8[:, ts].rearrange("p (t a) -> p t a", a=1).broadcast_to((NMAX, n, P)), ALU.mult)

                def add0(u, jt, pair):
                    scalar_wait("exp0", *u, jt, pair)
                    if u[0] == 1 and jt == 1:
                        dve.wait_ge(tensor_done, tensor.at(b, "den0", 0, u[1]))
                    if jt > 1:
                        if adder(*u, jt - 1, pair) == "vector":
                            own("add0", *u, jt - 1, pair)
                        else:
                            dve.wait_ge(pool_done, gps.at(b, "add0", *u, jt - 1, pair))
                    total = acc0[:, u[1], pair, :]
                    first = p0[:, 0, pair, :] if jt == 1 else total
                    TT(total, first, p0[:, jt % DEPTH, pair, :], ALU.add
                       ).then_inc(vector_done, vector.one("add0", *u, jt, pair))

                def max_rows(g, half):
                    ts = slice(half * HT, (half + 1) * HT)
                    negate((g, half), G, ts, ("max0", *rows_of((g, half), G * HT - 1)))
                    t = tile_wait("m0", g, half)
                    for h in range(G):
                        spread(stack[IMAX:K0, 0, g, h, half * HALF:(half + 1) * HALF], t[0:NMAX, h * P:(h + 1) * P], ts
                               ).then_inc(vector_done, vector.one("max_rows", g, half, h))

                def inverse0(u):
                    den = tile_wait("den0", *u)
                    ve.reciprocal(rec0[:], den[:, 0:P]).then_inc(vector_done, vector.one("rec0", *u))
                    own("rec0", *u)
                    TT(rows0[:], rec0[:].rearrange("p (a n) -> p a n", a=1).broadcast_to((P, HT, P)),
                       seg_own[:].rearrange("p (t a) -> p t a", a=1).broadcast_to((P, HT, P)), ALU.mult
                       ).then_inc(vector_done, vector.one("rows0", *u))

                def normalise0(u):
                    scalar_wait("pv0_out", *u)
                    ex = tile_wait("ex0", *u)
                    s = slice(u[1] * HALF, (u[1] + 1) * HALF)
                    TT(raw[:, s], raw[:, s], ex[:, 0:HALF], ALU.mult).then_inc(vector_done, vector.one("res", *u))

                def res_lo(g, half):
                    scalar_wait("res_hi", g, half)
                    s = slice(half * HALF, (half + 1) * HALF)
                    STT(side[:, 1, g, s], raw[:, s], col("bv0", g), f(side[:, 0, g, s]), ALU.add, ALU.subtract
                        ).then_inc(vector_done, vector.one("res_lo", g, half))

                def x1(k):
                    if k == 0:
                        dve.wait_ge(act_loaded, 16 * b + 16)
                    t = tile_wait("out0", k)
                    for ct in range(CT):
                        a = act[:, ct, k * HALF:(k + 1) * HALF]
                        STT(a, t[:, ct * HALF:(ct + 1) * HALF], col("bo0", ct), a, ALU.add, ALU.add
                            ).then_inc(vector_done, vector.one("x1", k, ct))

                def statistics(layer, k):
                    for ct in range(CT):
                        ve.bn_stats(stats[:, ct, k, :], act[:, ct, k * HALF:(k + 1) * HALF]
                                    ).then_inc(vector_done, vector.one("stat", layer, k, ct))

                def aggregate(layer):
                    own("stat", layer, 1, CT - 1)
                    ve.memset(pairs[:, 45:46], 0.0)
                    for ct in range(CT):
                        ve.bn_aggr(mv[:, ct, :], stats[:, ct]).then_inc(vector_done, vector.one("mv", layer, ct))

                for g in range(NG):
                    for t in range(2):
                        if g == 0 and t == 1:
                            dve.wait_ge(z_stored, 16 * b)
                            dve.wait_ge(x3_stored, 16 * b)
                            dve.wait_ge(pool_done, gps.before(b, "pool", 9, CT - 1))
                        qk0_lo(t, g)
                for k in range(G * HT):
                    max0(*rows_of(UNITS[0], k))
                max_rows(*UNITS[0])
                for u in UNITS:
                    last, following = last_unit(*u), next_unit(*u)
                    for jt in range(NT):
                        if last and jt == 0:
                            inverse0(last)
                        elif last and jt == 2:
                            normalise0(last)
                        for pair in range(2):
                            if following:
                                max0(*rows_of(following, 2 * jt + pair))
                            if jt and adder(*u, jt - 1, pair) == "vector":
                                add0(u, jt - 1, pair)
                        if last and jt == 3:
                            res_lo(*last)
                        if not following and jt == 5:
                            x1(0)
                    if following:
                        max_rows(*following)
                own("x1", 0, CT - 1)
                statistics(1, 0)
                inverse0(UNITS[-1])
                normalise0(UNITS[-1])
                res_lo(*UNITS[-1])
                x1(1)
                own("x1", 1, CT - 1)
                statistics(1, 1)

                for layer in (1, 2):
                    aggregate(layer)

                    def v_lo(l, k):
                        scalar_wait("v_hi", l, k)
                        v = lambda w: w[:, 4 * k:4 * k + 4, :].rearrange("p t n -> p (t n)")
                        TT(v(vl), tile[slot("v", l, k)][:], f(v(vh)), ALU.subtract
                           ).then_inc(vector_done, vector.one("v_lo", l, k))

                    def feat_lo(l, k):
                        hi, lo = (side[:, 0], side[:, 1]) if l == 2 else (xh, xl)
                        for ct in range(CT):
                            scalar_wait("feat_hi", l, k, ct)
                            s = slice(k * HALF, (k + 1) * HALF)
                            TT(lo[:, ct, s], act[:, ct, s], f(hi[:, ct, s]), ALU.subtract
                               ).then_inc(vector_done, vector.one("feat_lo", l, k, ct))

                    own("mv", layer, 1)
                    if layer == 1:
                        t = tile_wait("gn")
                        ve.tensor_copy(gdev, t[:, 2:4]).then_inc(vector_done, vector.one("gn_dev"))
                        own("gn_dev")
                        TT(gsq, gdev, gdev, ALU.mult).then_inc(vector_done, vector.one("gn"))
                        dve.wait_ge(tensor_done, tensor.at(b, "pv_groups"))
                        TS(veps, t[:, 4:6], 1e-6, None, ALU.add).then_inc(vector_done, vector.one("var", 1))
                        mean = t[:, 0:2]
                    else:
                        TS(veps, mv[:, :, 1], 1e-5, None, ALU.add).then_inc(vector_done, vector.one("var", 2))
                        mean = mv[:, :, 0]
                    scalar_wait("std", layer)
                    ve.reciprocal(y0, y2).then_inc(vector_done, vector.one("inv_std", layer))
                    own("inv_std", layer)
                    TT(y1, y0, y0, ALU.mult).then_inc(vector_done, vector.one("newton", layer, 0))
                    own("newton", layer, 0)
                    STT(y2, y1, -0.5, veps, ALU.mult, ALU.mult).then_inc(vector_done, vector.one("newton", layer, 1))
                    own("newton", layer, 1)
                    if layer == 1:
                        STT(inv_std, y2, 1.5, y0, ALU.add, ALU.mult).then_inc(vector_done, vector.one("newton", 1, 2))
                        own("newton", 1, 2)
                        TT(col("scale"), inv_std, col("gnw"), ALU.mult).then_inc(vector_done, vector.one("scale", 1))
                        own("scale", 1)
                        TT(mscale, mean, col("scale"), ALU.mult).then_inc(vector_done, vector.one("offset", 1))
                        own("offset", 1)
                        TT(col("shift"), col("gnb"), mscale, ALU.subtract).then_inc(vector_done, vector.one("shift", 1))
                    else:
                        STT(col("scale"), y2, 1.5, y0, ALU.add, ALU.mult).then_inc(vector_done, vector.one("newton", 2, 2))
                        own("newton", 2, 2)
                        STT(col("shift"), mean, -1.0, col("scale"), ALU.mult, ALU.mult
                            ).then_inc(vector_done, vector.one("shift", 2))
                    own("shift", layer)
                    for k in range(2):
                        s = slice(k * HALF, (k + 1) * HALF)
                        for ct in range(CT):
                            if k:
                                own("norm_lo", layer, 0, ct)
                            TS(tmp[:, ct * HALF:(ct + 1) * HALF], act[:, ct, s], col("scale", ct), col("shift", ct),
                               ALU.mult, ALU.add).then_inc(vector_done, vector.one("norm", layer, k, ct))
                        for ct in range(CT):
                            own("norm", layer, k, ct)
                            scalar_wait("norm_hi", layer, k, ct)
                            TT(xl[:, ct, s], tmp[:, ct * HALF:(ct + 1) * HALF], f(xh[:, ct, s]), ALU.subtract
                               ).then_inc(vector_done, vector.one("norm_lo", layer, k, ct))
                    if layer == 2:
                        v_lo(2, 0)
                        feat_lo(2, 1)
                    for t in range(2):
                        for ct in range(CT):
                            scalar_wait("qk_hi", layer, t, ct)
                            STT(qk_r[:, t, 1, ct, :], tile[slot("qk", layer, t, ct)][:], col(f"b{'qk'[t]}{layer}", ct),
                                f(qk_r[:, t, 0, ct, :]), ALU.add, ALU.subtract
                                ).then_inc(vector_done, vector.one("qk_lo", layer, t, ct))
                    if layer == 1:
                        v_lo(1, 0)
                    for it in range(NT):
                        t = tile_wait("s", layer, it)
                        ve.tensor_reduce(maxima[:, it:it + 1], t[:], X, ALU.max
                                         ).then_inc(vector_done, vector.one("max", layer, it))
                    negate((layer,), 1, slice(0, NT), ("max", layer, NT - 1))
                    t = tile_wait("m", layer)
                    spread(max_in[0:NMAX, :], t[0:NMAX, 0:P], slice(0, NT)).then_inc(vector_done, vector.one("max_in", layer))
                    v_lo(layer, 1)

                    def reciprocal(half):
                        den = tile_wait("den", layer, half)
                        ve.reciprocal(den[:, 0:HALF], den[:, 0:HALF]).then_inc(vector_done, vector.one("rec", layer, half))

                    def finish(half):
                        own("rec", layer, half)
                        scalar_wait("pv_out", layer, half)
                        r3 = raw[:].rearrange("p (t n) -> p t n", t=CT)
                        TT(r3, r3, tile[slot("den", layer, half)][:, 0:HALF].rearrange("p (a n) -> p a n", a=1).broadcast_to((P, CT, HALF)),
                           ALU.mult).then_inc(vector_done, vector.one("out", layer, half))
                        own("out", layer, half)
                        for ct in range(CT):
                            a = act[:, ct, half * HALF:(half + 1) * HALF]
                            STT(a, r3[:, ct, :], col(f"bvo{layer}", ct), a, ALU.add, ALU.add
                                ).then_inc(vector_done, vector.one("x", layer, half, ct))

                    def exp_lo(n):
                        scalar_wait("exp" if n < NT - 1 else "exp_hi", layer, n)
                        TT(pl[:, n % 2, :], p12[:, n % 2, :], f(ph[:, n % 2, :]), ALU.subtract
                           ).then_inc(vector_done, vector.one("exp_lo", layer, n))

                    def add(n):
                        if n % 4 > 1:
                            own("add", layer, n - 1)
                        elif n == 5:
                            dve.wait_ge(tensor_done, tensor.at(b, "den", layer, 0))
                        first = p12[:, 0, :] if n % 4 == 1 else acc[:]
                        scalar_wait("exp", layer, n)
                        TT(acc[:], first, p12[:, n % 2, :], ALU.add).then_inc(vector_done, vector.one("add", layer, n))

                    for n in range(NT - 1):
                        if n == 5:
                            reciprocal(0)
                        if n == 6:
                            finish(0)
                        exp_lo(n)
                        if n % 4:
                            add(n)
                        if n == 3:
                            own("add", layer, 3)
                            TT(acc[:, 0:HALF], acc[:, 0:HALF], acc[:, HALF:], ALU.add
                               ).then_inc(vector_done, vector.one("fold", layer))
                    own("x", layer, 0, 1)
                    statistics(layer + 1, 0)
                    feat_lo(layer + 1, 0)
                    add(NT - 1)
                    exp_lo(NT - 1)
                    reciprocal(1)
                    finish(1)
                    own("x", layer, 1, 1)
                    if layer == 1:
                        statistics(2, 1)

                feat_lo(3, 1)
                kw = kt[:].rearrange("p t (w e) -> p (t w) e", e=WIN)
                W4 = NT * C // WIN // 2

                def wide(ap):
                    return ap.rearrange("p (w a) -> p w a", a=1).broadcast_to((P, W4, WIN))

                for k in range(2):
                    t = tile_wait("kt", k)
                    w, wm = kw[:, k * W4:(k + 1) * W4, :], win[:, k * W4:(k + 1) * W4]
                    w_in = t[:].rearrange("p (w e) -> p w e", e=WIN)
                    ve.tensor_reduce(wm, w_in, X, ALU.max).then_inc(vector_done, vector.one("win_max", k))
                    own("win_max", k)
                    TT(w, w_in, wide(wm), ALU.subtract).then_inc(vector_done, vector.one("kt_sub", k))
                    if k == 0:
                        statistics(3, 1)
                        aggregate(3)
                for ct in range(CT):
                    scalar_wait("x_hi", ct)
                    TT(xl[:, ct, :], x_in[:, ct, :], f(xh[:, ct, :]), ALU.subtract
                       ).then_inc(vector_done, vector.one("x_lo", ct))
                t = tile_wait("qv")
                TT(qv[:], t[:].rearrange("p (t n) -> p t n", t=2),
                   b3row[:].rearrange("p (a n) -> p a n", a=1).broadcast_to((P, 2, 2 * C)), ALU.add
                   ).then_inc(vector_done, vector.one("qv_in"))

                def windows(k):
                    w, ws = kw[:, k * W4:(k + 1) * W4, :], win[:, k * W4:(k + 1) * W4]
                    wr = win_r[:, k * W4:(k + 1) * W4]
                    scalar_wait("kt_exp", k)
                    ve.tensor_reduce(ws, w, X, ALU.add).then_inc(vector_done, vector.one("win_sum", k))
                    own("win_sum", k)
                    ve.reciprocal(wr, ws).then_inc(vector_done, vector.one("win_rec", k))
                    if k == 1:
                        own("win_rec", k)
                        TT(w, w, wide(wr), ALU.mult).then_inc(vector_done, vector.one("sm", k))

                windows(0)
                t = tile_wait("mt")
                TT(mtm[:], t[:, 0:CT * P].rearrange("p (t n) -> p t n", t=CT),
                   heads_mask[:].rearrange("p (a n) -> p a n", a=1).broadcast_to((P, CT, P)), ALU.mult
                   ).then_inc(vector_done, vector.one("mt_in"))
                TT(kbar, t[:, HALF:HALF + CT], col("b3"), ALU.add).then_inc(vector_done, vector.one("kbar"))
                windows(1)
                t = tile_wait("g")
                ve.tensor_copy(logits_in, t[:, HALF:HALF + 4]).then_inc(vector_done, vector.one("mix", 0))
                own("mix", 0)
                TT(larger, logits_in[:, 0:2], logits_in[:, 2:4], ALU.max).then_inc(vector_done, vector.one("mix", 1))
                own("mix", 1)
                TT(logits[:, 0:2], logits_in[:, 0:2], larger, ALU.subtract).then_inc(vector_done, vector.one("mix", 2))
                TT(logits[:, 2:4], logits_in[:, 2:4], larger, ALU.subtract).then_inc(vector_done, vector.one("mix", 3))
                scalar_wait("mix_exp")
                TT(mix_sum, mix_e[:, 0:2], mix_e[:, 2:4], ALU.add).then_inc(vector_done, vector.one("mix_sum"))
                own("mix_sum")
                ve.reciprocal(mix_rec, mix_sum).then_inc(vector_done, vector.one("mix_rec"))
                own("mix_rec")
                STT(mix_pi, mix_e[:, 0:2], float(D) ** -0.5, mix_rec, ALU.mult, ALU.mult
                    ).then_inc(vector_done, vector.one("mix_pi"))
                own("mix_pi")

                def smt_lo(ct):
                    scalar_wait("smt_hi", ct)
                    TT(qk_r[:, 0, 1, ct, :], tile[slot("smt", ct)][:], f(qk_r[:, 0, 0, ct, :]), ALU.subtract
                       ).then_inc(vector_done, vector.one("smt_lo", ct))

                smt_lo(0)
                for ct in range(CT):
                    scalar_wait("g_hi", CT - 1)
                    STT(gl[:, ct, :], t[:, ct * C:(ct + 1) * C], mix_pi[:, ct:ct + 1], f(gh[:, ct, :]),
                        ALU.mult, ALU.subtract).then_inc(vector_done, vector.one("g_lo", ct))
                smt_lo(1)
                for ct in range(CT):
                    scalar_wait("z_kept", ct)
                    for k in range(2):
                        ve.bn_stats(bn_rows[:, ct, bass.ds(2 * b + k, 1), :], zbuf[:, ct, k * HALF:(k + 1) * HALF]
                                    ).then_inc(vector_done, vector.one("z_stat", ct, k))
                assert not vector.todo

            chain = 0

            def link(ins):
                nonlocal chain
                chain += 1
                ins.then_inc(bn_steps, 1)
                dve.wait_ge(bn_steps, chain)

            dve.wait_ge(vector_done, vector.at(B - 1, "z_stat", CT - 1, 1))
            for ct in range(CT):
                link(ve.bn_aggr(mv[:, ct, :], bn_rows[:, ct]))
            link(TS(veps, mv[:, :, 1], 1e-5, None, ALU.add))
            chain += 1
            dve.wait_ge(bn_steps, chain)
            link(ve.reciprocal(y0, y2))
            link(TT(y1, y0, y0, ALU.mult))
            link(STT(y2, y1, -0.5, veps, ALU.mult, ALU.mult))
            link(STT(inv_std, y2, 1.5, y0, ALU.add, ALU.mult))
            link(TT(col("bnscale"), inv_std, col("bnw"), ALU.mult))
            link(TT(mscale, mv[:, :, 0], col("bnscale"), ALU.mult))
            link(TT(col("bnshift"), col("bnb"), mscale, ALU.subtract))
            for k, b in enumerate(FIN_ORDER):
                z, x3 = fin[b]
                for ct in range(CT):
                    dve.wait_ge(bn_scaled, CT * k + ct + 1)
                    TT(z[:, ct, :], z[:, ct, :], x3[:, ct, :], ALU.add).then_inc(bn_added, 1)

        @block.tensor
        def _(pe):
            mm = nc.tensor.matmul
            halves = [slice(0, HALF), slice(HALF, N)]

            def three(out, lhs, rhs, first=True, last=True, low=None):
                n = len(lhs[0])
                for m, (a, c) in enumerate(((0, 0), (1, 0), (0, 1))):
                    if c and low:
                        low()
                    for kt_ in range(n):
                        ins = mm(out, lhs[a][kt_], rhs[c][kt_], start=first and kt_ == 0 and m == 0,
                                 stop=last and kt_ == n - 1 and m == 2)
                return ins

            pe.wait_ge(consts_made, 16)
            for k in range(9):
                if k >= SLOTS:
                    pe.wait_ge(setup_scalar, 10 + k - SLOTS)
                    pe.wait_ge(setup_vector, (8, 9, 9, 10, 11, 11)[k - SLOTS])
                pe.wait_ge(weights_in[2 + k], 16)
                w = stage[:, (4 + k) * U:(5 + k) * U].rearrange("p (t n) -> p t n", t=CT)
                for ct in range(CT):
                    for ot in range(CT):
                        ins = nc.tensor.transpose(tile[k % SLOTS][:, ct * C + ot * P:ct * C + (ot + 1) * P],
                                                  w[:, ot, ct * P:(ct + 1) * P], ident[:])
                ins.then_inc(setup_tensor, 1)
            pe.wait_ge(setup_scalar, 19)
            pe.wait_ge(setup_vector, 12)
            pe.wait_ge(vectors_in, 16 * NVEC)
            for k in range(2):
                pe.wait_ge(weights_in[11 + k], 16)
                wv = stage[:, (13 + k) * U:(14 + k) * U].rearrange("p (t n) -> p t n", t=CT)
                wo = acc0[:, 0, k, 0:U].rearrange("p (t n) -> p t n", t=CT)
                for ct in range(CT):
                    for et in range(CT):
                        ins = mm(tile[k][:, ct * C:(ct + 1) * C], wv[:, et, ct * P:(ct + 1) * P], wo[:, et, :],
                                 start=et == 0, stop=et == CT - 1)
                ins.then_inc(setup_tensor, 1)
            for k in range(2):
                wo = acc0[:, 0, k, 0:U].rearrange("p (t n) -> p t n", t=CT)
                for ot in range(CT):
                    for et in range(CT):
                        ins = mm(pv[:, 2 * k + ot:2 * k + ot + 1], wo[:, et, ot * P:(ot + 1) * P],
                                 col(f"bv{k + 1}", et), start=et == 0, stop=et == CT - 1)
            ins.then_inc(setup_tensor, 1)
            pe.wait_ge(scalar_done, scalar.count)
            pe.wait_ge(vector_done, vector.count)
            mm(tile[0][:, 0:P], ones[:], ident[:], start=True, stop=True).then_inc(tensor_done, tensor.count)

            with pe.Fori(0, B) as b:
                tensor.start()

                def scalar_wait(*step):
                    pe.wait_ge(scalar_done, scalar.at(b, *step))

                def vector_wait(*step):
                    pe.wait_ge(vector_done, vector.at(b, *step))

                def free(*name):
                    engine, count = leaver(b, *name)
                    pe.wait_ge(scalar_done if engine == "scalar" else vector_done, count)
                    return tile[slot(*name)]

                kts = range(CT)

                def qk0(t, g):
                    o = free("qk0", t, g)
                    for s in halves:
                        ins = three(o[:, s], [[w[:, kt_, t, g * P:(g + 1) * P] for kt_ in kts] for w in (w0h, w0l)],
                                    [[v[:, kt_, s] for kt_ in kts] for v in (xh, xl)])
                    ins.then_inc(tensor_done, tensor.one("qk0", t, g))

                def s0(g, h, it):
                    if it == 0 or it == HT:
                        pe.wait_ge(stacked[g][h], 48 * b + 48)
                    o = free("s0", g, h, it)
                    for s in halves:
                        ins = mm(o[:, s], stack[0:IMAX, 0, g, h, it * P:(it + 1) * P], stack[0:IMAX, 1, g, h, s],
                                 start=True, stop=True)
                    ins.then_inc(tensor_done, tensor.one("s0", g, h, it))

                def m0(g, half):
                    vector_wait("neg_lo", g, half)
                    o = free("m0", g, half)
                    for h in range(G):
                        ins = nc.tensor.transpose(o[0:NMAX, h * P:(h + 1) * P],
                                                  negmax[:, h].rearrange("p s t -> p (s t)"), ident[:])
                    ins.then_inc(tensor_done, tensor.one("m0", g, half))

                def st0(g, half, jt, pair):
                    if g == 0 and half == 0 and jt == 0 and pair == 0:
                        pe.wait_ge(key_ones_in, 16 * b + 16)
                    o = free("st0", g, half, jt, pair)
                    for k in range(2):
                        h = 2 * pair + k
                        if jt == 0:
                            vector_wait("max_rows", g, half, h)
                        ins = mm(o[:, halves[k]], stack[0:K0, 1, g, h, jt * P:(jt + 1) * P],
                                 stack[0:K0, 0, g, h, halves[half]], start=True, stop=True)
                    ins.then_inc(tensor_done, tensor.one("st0", g, half, jt, pair))

                def pv0(g, half, jt, part):
                    if part == 0:
                        scalar_wait("exp0", g, half, jt, 1)
                        if jt == 0 and g == 1:
                            scalar_wait("pv0_out", 0, half)
                    whole = jt in (0, NT - 1)
                    first, n = (0, HALF) if whole else (part * HALF // 2, HALF // 2)
                    for h in range(G) if part == 0 or not whole else ():
                        i, o = (k * HALF + first for k in (h % 2, half))
                        ins = mm(pv[D * h:D * h + D, o:o + n], v0[:, jt, g * P + D * h:g * P + D * h + D],
                                 p0[:, jt % DEPTH, h // 2, i:i + n], start=jt == 0, stop=jt == NT - 1)
                    if part == (0 if whole else 1):
                        ins.then_inc(tensor_done, tensor.one("pv0", g, half, jt))

                def den0(g, half):
                    for pair in range(2):
                        if adder(g, half, SUMMED - 1, pair) == "pool":
                            pe.wait_ge(pool_done, gps.at(b, "add0", g, half, SUMMED - 1, pair))
                        else:
                            vector_wait("add0", g, half, SUMMED - 1, pair)
                    o = free("den0", g, half)
                    for jt in range(SUMMED - 1, NT):
                        if jt >= SUMMED:
                            scalar_wait("exp0", g, half, jt, 1)
                        src = acc0[:, half] if jt < SUMMED else p0[:, jt % DEPTH]
                        for t in range(HT):
                            seg = segment[:, D - SEG - SEG * t:2 * D - SEG - SEG * t]
                            for h in range(G):
                                i = (h % 2) * HALF + t * P
                                ins = mm(o[D * h:D * h + D, 0:P], seg, src[:, h // 2, i:i + P],
                                         start=t == 0 and jt == SUMMED - 1, stop=t == HT - 1 and jt == NT - 1)
                    ins.then_inc(tensor_done, tensor.one("den0", g, half))

                def ex0(g, half):
                    o = free("ex0", g, half)
                    vector_wait("rows0", g, half)
                    mm(o[:, 0:HALF], heads_mask[:], rows0[:], start=True, stop=True
                       ).then_inc(tensor_done, tensor.one("ex0", g, half))

                def out0(k):
                    o = free("out0", k)
                    for g, part_w, part in ((0, 0, 0), (0, 1, 0), (0, 0, 1), (1, 0, 0), (1, 1, 0), (1, 0, 1)):
                        if (g, part_w) == (1, 0):
                            if part == 0:
                                scalar_wait("res_hi", 1, k)
                            else:
                                vector_wait("res_lo", 1, k)
                        for ct in range(CT):
                            ins = mm(o[:, halves[ct]], (wo0h, wo0l)[part_w][:, g, ct * P:(ct + 1) * P],
                                     side[:, part, g, halves[k]], start=(g, part_w, part) == (0, 0, 0),
                                     stop=(g, part) == (1, 1))
                    ins.then_inc(tensor_done, tensor.one("out0", k))

                pe.wait_ge(scalar_done, scalar.before(b, "x_hi", CT - 1))
                pe.wait_ge(vector_done, vector.before(b, "x_lo", CT - 1))
                for g in range(NG):
                    for t in range(2):
                        qk0(t, g)

                def v0_tile(k):
                    o = free("v0", k)
                    for q in range(2):
                        i = slice((2 * k + q) * P, (2 * k + q + 1) * P)
                        ins = three(o[:, q * C:(q + 1) * C], [[v[:, kt_, i] for kt_ in kts] for v in (xh, xl)],
                                    [[w[:, kt_, 2, :] for kt_ in kts] for w in (w0h, w0l)])
                    ins.then_inc(tensor_done, tensor.one("v0", k))

                for k in range(G * HT):
                    if k in (3, 6, 9, 12):
                        v0_tile(k // 3 - 1)
                    s0(*rows_of(UNITS[0], k))
                m0(*UNITS[0])
                for u in UNITS:
                    last, following = last_unit(*u), next_unit(*u)
                    for jt in range(NT):
                        for pair in range(2):
                            st0(*u, jt, pair)
                            if following:
                                s0(*rows_of(following, 2 * jt + pair))
                            if jt:
                                pv0(*u, jt - 1, pair)
                        if last and jt == 1:
                            ex0(*last)
                        if not following and jt == 4:
                            out0(0)
                    if following:
                        pv0(*u, NT - 1, 0)
                        pv0(*u, NT - 1, 1)
                        m0(*following)
                        den0(*u)
                    else:
                        den0(*u)
                        pv0(*u, NT - 1, 0)
                        pv0(*u, NT - 1, 1)
                ex0(*UNITS[-1])
                out0(1)

                for layer in (1, 2):
                    if layer == 1:
                        vector_wait("mv", 1, 1)
                        o = free("gn")
                        mm(o[:, 0:2], gn_avg[:], mv[:, :, 0], start=True, stop=True)
                        mm(o[:, 2:4], gn_rest[:], mv[:, :, 0], start=True, stop=True)
                        mm(o[:, 4:6], gn_avg[:], mv[:, :, 1], start=True, stop=False
                           ).then_inc(tensor_done, tensor.one("gn"))
                        vector_wait("gn")
                        mm(o[:, 4:6], gn_avg[:], gsq, start=False, stop=True
                           ).then_inc(tensor_done, tensor.one("pv_groups"))

                    def v_tile(k):
                        if layer == 2 and k == 1:
                            vector_wait("feat_lo", 2, 1, CT - 1)
                        feat = (xh, xl) if layer == 1 else (side[:, 0], side[:, 1])
                        wh, wl = wqk[layer, "v", "h"], wqk[layer, "v", "l"]
                        o = free("v", layer, k)
                        for q in range(4):
                            j = slice((4 * k + q) * P, (4 * k + q + 1) * P)
                            ins = three(o[:, q * C:(q + 1) * C], [[v[:, kt_, j] for kt_ in kts] for v in feat],
                                        [[w[:, kt_, :] for kt_ in kts] for w in (wh, wl)])
                        ins.then_inc(tensor_done, tensor.one("v", layer, k))

                    if layer == 2:
                        vector_wait("feat_lo", 2, 0, CT - 1)
                        v_tile(0)
                    for t in range(2):
                        wh, wl = wqk[layer, "qk"[t], "h"], wqk[layer, "qk"[t], "l"]
                        for ct in range(CT):
                            o = free("qk", layer, t, ct)
                            for k, s in enumerate(halves):
                                low = None
                                if t == 0 and ct == 0:
                                    scalar_wait("norm_hi", layer, k, CT - 1)
                                    low = lambda: vector_wait("norm_lo", layer, k, CT - 1)
                                ins = three(o[:, s], [[w[:, kt_, ct * P:(ct + 1) * P] for kt_ in kts] for w in (wh, wl)],
                                            [[v[:, kt_, s] for kt_ in kts] for v in (xh, xl)], low=low)
                            ins.then_inc(tensor_done, tensor.one("qk", layer, t, ct))
                    if layer == 1:
                        v_tile(0)
                    scalar_wait("qk_hi", layer, 1, 1)
                    for it in range(NT):
                        o = free("s", layer, it)
                        for s in halves:
                            for kt_ in kts:
                                ins = mm(o[:, s], qk_r[:, 0, 0, kt_, it * P:(it + 1) * P], qk_r[:, 1, 0, kt_, s],
                                         start=kt_ == 0, stop=kt_ == CT - 1)
                        ins.then_inc(tensor_done, tensor.one("s", layer, it))

                    def negated():
                        vector_wait("neg_lo", layer)
                        nc.tensor.transpose(free("m", layer)[0:NMAX, 0:P], negmax[:, 0].rearrange("p s t -> p (s t)"),
                                            ident[:]).then_inc(tensor_done, tensor.one("m", layer))

                    def scores(n):
                        half, jp = divmod(n, 4)
                        o = free("st", layer, n)
                        for q in range(2):
                            j = slice((2 * jp + q) * P, (2 * jp + q + 1) * P)
                            three(o[:, halves[q]], [[qk_r[:, 1, part, kt_, j] for kt_ in kts] for part in range(2)],
                                  [[qk_r[:, 0, part, kt_, halves[half]] for kt_ in kts] for part in range(2)], last=False)

                    def less_maxima(n):
                        for q in range(2):
                            ins = mm(tile[slot("st", layer, n)][:, halves[q]], ones_r[:], max_in[:, halves[n // 4]],
                                     start=False, stop=True)
                        ins.then_inc(tensor_done, tensor.one("st", layer, n))

                    def values(n):
                        half, jp = divmod(n, 4)
                        scalar_wait("exp_hi", layer, n)
                        vector_wait("exp_lo", layer, n)
                        if n == 4:
                            scalar_wait("pv_out", layer, 0)
                        if n == 0:
                            vector_wait("v_lo", layer, 1)
                        for q in range(2):
                            j = 2 * jp + q
                            for ct in range(CT):
                                ins = three(pv[:, halves[ct]], [[v[:, j, ct * P:(ct + 1) * P]] for v in (vh, vl)],
                                            [[p[:, n % 2, halves[q]]] for p in (ph, pl)],
                                            first=jp == 0 and q == 0, last=jp == 3 and q == 1)
                        ins.then_inc(tensor_done, tensor.one("pv", layer, n))

                    def sums(half):
                        if half == 0:
                            vector_wait("fold", layer)
                        else:
                            vector_wait("add", layer, NT - 1)
                        o = free("den", layer, half)
                        for q in range(half + 1):
                            ins = mm(o[:, 0:HALF], ones[:], acc[:, halves[q]], start=q == 0, stop=q == half)
                        ins.then_inc(tensor_done, tensor.one("den", layer, half))

                    v_tile(1)
                    negated()
                    vector_wait("qk_lo", layer, 1, 1)
                    for n in range(2):
                        scores(n)
                        if n == 0:
                            vector_wait("max_in", layer)
                        less_maxima(n)
                    for n in range(2, NT):
                        scores(n)
                        less_maxima(n)
                        values(n - 2)
                        if n == 5:
                            sums(0)
                    values(NT - 2)
                    sums(1)
                    values(NT - 1)

                for k in range(2):
                    vector_wait("feat_lo", 3, k, CT - 1)
                    o = free("kt", k)
                    for q in range(4):
                        i = slice((4 * k + q) * P, (4 * k + q + 1) * P)
                        ins = three(o[:, q * C:(q + 1) * C], [[v[:, kt_, i] for kt_ in kts] for v in (xh, xl)],
                                    [[w[:, kt_, :] for kt_ in kts] for w in (w3h, w3l)], last=False)
                        ins = mm(o[:, q * C:(q + 1) * C], ones_r[:], b3_parts[:], start=False, stop=True)
                    ins.then_inc(tensor_done, tensor.one("kt", k))
                pe.wait_ge(pool_done, gps.at(b, "pool", 9, CT - 1))
                pe.wait_ge(w3_back, 32 * b + 32)
                o = free("qv")
                for k in range(2):
                    for kt_ in kts:
                        ins = mm(o[:, halves[k]], xp[:, kt_, k * P:(k + 1) * P], w3f[:, kt_, :],
                                 start=kt_ == 0, stop=kt_ == CT - 1)
                ins.then_inc(tensor_done, tensor.one("qv"))
                vector_wait("qv_in")
                o = free("mt")
                for ct in range(CT):
                    for k in range(2):
                        mm(o[:, ct * P:(ct + 1) * P], qv[:, k, ct * P:(ct + 1) * P],
                           qv[:, k, C + ct * P:C + (ct + 1) * P], start=k == 0, stop=k == 1)
                for ct in range(CT):
                    for kt_ in kts:
                        ins = mm(o[:, HALF + ct:HALF + ct + 1], w3f[:, kt_, ct * P:(ct + 1) * P], mv[:, kt_, 0:1],
                                 start=kt_ == 0, stop=kt_ == CT - 1)
                ins.then_inc(tensor_done, tensor.one("mt"))
                vector_wait("kbar")
                o = free("g")
                for ct in range(CT):
                    mm(o[:, ct * C:(ct + 1) * C], mtm[:, ct, :], wo3[:, ct, :], start=True, stop=True)
                mm(o[:, HALF:HALF + 2], mix_own[:], kbar, start=True, stop=True)
                mm(o[:, HALF + 2:HALF + 4], mix_other[:], kbar, start=True, stop=True
                   ).then_inc(tensor_done, tensor.one("g"))
                pe.wait_ge(pool_done, gps.at(b, "sm", 0))
                vector_wait("sm", 1)
                for ct in range(CT):
                    o = free("smt", ct)
                    for nt in range(NT):
                        ins = nc.tensor.transpose(o[:, nt * P:(nt + 1) * P], kt[:, nt, ct * P:(ct + 1) * P], ident[:])
                    ins.then_inc(tensor_done, tensor.one("smt", ct))
                for ct in range(CT):
                    o = free("z", ct)
                    for kt_, part_g, part in ((0, 0, 0), (0, 1, 0), (0, 0, 1), (1, 0, 0), (1, 1, 0), (1, 0, 1)):
                        if ct == 0 and (part_g, part) == (1, 0) and kt_ == 0:
                            vector_wait("g_lo", 1)
                        elif ct == 0 and (kt_, part_g, part) == (1, 0, 0):
                            scalar_wait("smt_hi", 1)
                        elif ct == 0 and (kt_, part) == (1, 1):
                            vector_wait("smt_lo", 1)
                        elif ct == 0 and (kt_, part_g, part) == (0, 0, 0):
                            scalar_wait("g_hi", 1)
                        for s in halves:
                            ins = mm(o[:, s], (gh, gl)[part_g][:, kt_, ct * P:(ct + 1) * P], qk_r[:, 0, part, kt_, s],
                                     start=(kt_, part_g, part) == (0, 0, 0), stop=(kt_, part) == (1, 1))
                    ins.then_inc(tensor_done, tensor.one("z", ct))
                assert not tensor.todo


_INS = ["x", "L0_conv_w_proj", "L0_conv_b_proj", "L0_conv_w_out", "L0_conv_b_out", "L1_conv_gn_w", "L1_conv_gn_b",
        "L1_conv_wq", "L1_conv_bq", "L1_conv_wk", "L1_conv_bk", "L1_conv_wv", "L1_conv_bv", "L1_conv_wo", "L1_conv_bo",
        "L2_conv_f_w", "L2_conv_f_b", "L2_conv_g_w", "L2_conv_g_b", "L2_conv_h_w", "L2_conv_h_b", "L2_conv_o_w",
        "L2_conv_o_b", "L3_conv_w_qk", "L3_conv_b_qk", "L3_conv_w_v", "L3_conv_b_v", "L3_conv_mix_weight",
        "L3_conv_w_out", "L3_conv_bn_weight", "L3_conv_bn_bias"]


def kernel(**inputs):
    import numpy as _np
    import concourse.bacc as _bacc
    from concourse import mybir as _mybir
    from concourse.bass_utils import run_bass_kernel_spmd as _run

    nc = _bacc.Bacc("TRN2", target_bir_lowering=False, num_devices=1)
    arrays, args = {}, []
    for name in _INS:
        a = _np.ascontiguousarray(inputs[name])
        arrays[f"in_{name}_dram"] = a
        args.append(nc.dram_tensor(f"in_{name}_dram", a.shape, _mybir.dt.from_np(a.dtype), kind="ExternalInput").ap())
    args.append(nc.dram_tensor("out_dram", (B, C, 32, 32), F32, kind="ExternalOutput").ap())
    conv_seq_kernel(nc, *args)
    r = _run(nc, [arrays], core_ids=[0])
    return r.results[0]["out_dram"]
```
